# Optimizing a Trainium2 kernel written in Bass

```python
import numpy as np
import jax
import jax.numpy as jnp

def _softmax(x, axis=-1):
    return jax.nn.softmax(x, axis=axis)

def _gelu(x):
    return jax.nn.gelu(x, approximate=True)

def _silu(x):
    return jax.nn.silu(x)

def _sigmoid(x):
    return jax.nn.sigmoid(x)

def _layernorm(x, axis=-1, eps=1e-05):
    m = jnp.mean(x, axis=axis, keepdims=True)
    v = jnp.var(x, axis=axis, keepdims=True)
    return (x - m) / jnp.sqrt(v + eps)

def _scatter_add(tgt, idx, src, axis=0):
    return tgt.at[idx].add(src)

def _segment_sum(src, seg, n):
    return jax.ops.segment_sum(src, seg, n)
kernel_name = 'mk_gnn_preln_d2_gnn_r8_b733ca'

def setup_inputs(seed: int=0):
    np.random.seed(seed)
    _w = jnp.asarray

    def _rec_inputs():
        import jax
        import jax.numpy as jnp
        _gk = jax.random.key(seed)
        x = -0.0007083 + 1.001 * jax.random.normal(jax.random.fold_in(_gk, 1), (6250, 48), jnp.float32)
        src = jax.random.randint(jax.random.fold_in(_gk, 2), (200000,), 0, 6250, jnp.int32)
        dst = jax.random.randint(jax.random.fold_in(_gk, 3), (200000,), 0, 6250, jnp.int32)
        _o = jnp.argsort(dst, stable=True)
        src = src[_o]
        dst = dst[_o]
        edge_attr_40 = jax.random.uniform(jax.random.fold_in(_gk, 12), (200000, 40), jnp.float32, 0.0, 1)
        edge_weight = jax.random.uniform(jax.random.fold_in(_gk, 14), (200000,), jnp.float32, 0.0, 7.99999)
        node_type_119 = jax.random.randint(jax.random.fold_in(_gk, 15), (6250,), 0, 119, jnp.int32)
        node_vec = jax.random.uniform(jax.random.fold_in(_gk, 16), (6250,), jnp.float32, 0.0, 3.99996)
        return (x, src, dst, edge_attr_40, edge_weight, node_type_119, node_vec)
    x, src, dst, edge_attr_40, edge_weight, node_type_119, node_vec = _rec_inputs()

    def _L0_gnn_setup():
        import jax, jax.numpy as jnp
        import numpy as np
        N = 6250
        E = 150000
        H = 48
        RBF = 40
        L = 4
        NELEM = 119
        G = 32
        CUT = 6.0

        def _ln(x, g, b):
            m = x.mean(-1, keepdims=True)
            v = ((x - m) ** 2).mean(-1, keepdims=True)
            return (x - m) * jax.lax.rsqrt(v + 1e-05) * g + b
        key = jax.random.key(seed)
        k = jax.random.split(key, 16)
        s = 0.1
        return {'h': jax.random.normal(k[0], (N, H), jnp.float32), 'edge_index': jax.random.randint(k[1], (2, E), 0, N), 'edge_attr': jax.random.uniform(k[2], (E, RBF), dtype=jnp.float32), 'distances': jax.random.uniform(k[3], (E,), dtype=jnp.float32) * 8.0, 'atom_z': jax.random.randint(k[4], (N,), 0, NELEM), 'node_mult': jax.random.uniform(k[5], (N,), dtype=jnp.float32) * 3.0 + 1.0, 'batch': jnp.sort(jax.random.randint(k[6], (N,), 0, 64)), 'Wq': jax.random.normal(k[7], (L, H, H), jnp.float32) * s, 'gq': jnp.ones((L, H), jnp.float32), 'bq': jnp.zeros((L, H), jnp.float32), 'Wk': jax.random.normal(k[8], (L, H, H), jnp.float32) * s, 'gk': jnp.ones((L, H), jnp.float32), 'bk': jnp.zeros((L, H), jnp.float32), 'Wm': jax.random.normal(k[9], (L, H, H), jnp.float32) * s, 'Wu': jax.random.normal(k[10], (L, 2 * H, H), jnp.float32) * s, 'go': jnp.ones((L, H), jnp.float32), 'bo': jnp.zeros((L, H), jnp.float32), 'F1W': jax.random.normal(k[11], (RBF, H), jnp.float32) * s, 'F1b': jnp.zeros((H,), jnp.float32), 'F2W': jax.random.normal(k[12], (H, H), jnp.float32) * s, 'F2b': jnp.zeros((H,), jnp.float32), 'gn': jnp.ones((H,), jnp.float32), 'bn': jnp.zeros((H,), jnp.float32), 'emb': jax.random.normal(k[13], (NELEM, G), jnp.float32) * 0.01, 'adapt': jax.random.normal(k[14], (G, G), jnp.float32) * 0.01}
    _L0_gnn_all = _L0_gnn_setup()
    _L0_gnn_in = {k: v for k, v in _L0_gnn_all.items() if k in ('Wq', 'gq', 'bq', 'Wk', 'gk', 'bk', 'Wm', 'Wu', 'go', 'bo', 'F1W', 'F1b', 'F2W', 'F2b', 'gn', 'bn', 'emb', 'adapt')}
    del _L0_gnn_all

    def _L1_gnn_setup():
        import jax, jax.numpy as jnp
        import numpy as np
        N_NODES = 12500
        N_EDGES = 200000
        C_IN = 48
        C_OUT = 48
        key = jax.random.key(seed)
        k_x, k_e, k_w = jax.random.split(key, 3)
        x = jax.random.normal(k_x, (N_NODES, C_IN), dtype=jnp.float32)
        edge_index = jax.random.randint(k_e, (2, N_EDGES), 0, N_NODES, dtype=jnp.int64)
        W = jax.random.normal(k_w, (C_IN, C_OUT), dtype=jnp.float32) * (1.0 / np.sqrt(C_IN))
        b = jnp.zeros((C_OUT,), dtype=jnp.float32)
        return {'x': x, 'edge_index': edge_index, 'W': W, 'b': b}
    _L1_gnn_all = _L1_gnn_setup()
    _L1_gnn_in = {k: v for k, v in _L1_gnn_all.items() if k in ('W', 'b')}
    del _L1_gnn_all
    return {'x': x, 'src': src, 'dst': dst, 'edge_attr_40': edge_attr_40, 'edge_weight': edge_weight, 'node_type_119': node_type_119, 'node_vec': node_vec, 'L0_gnn_Wq': _L0_gnn_in['Wq'], 'L0_gnn_gq': _L0_gnn_in['gq'], 'L0_gnn_bq': _L0_gnn_in['bq'], 'L0_gnn_Wk': _L0_gnn_in['Wk'], 'L0_gnn_gk': _L0_gnn_in['gk'], 'L0_gnn_bk': _L0_gnn_in['bk'], 'L0_gnn_Wm': _L0_gnn_in['Wm'], 'L0_gnn_Wu': _L0_gnn_in['Wu'], 'L0_gnn_go': _L0_gnn_in['go'], 'L0_gnn_bo': _L0_gnn_in['bo'], 'L0_gnn_F1W': _L0_gnn_in['F1W'], 'L0_gnn_F1b': _L0_gnn_in['F1b'], 'L0_gnn_F2W': _L0_gnn_in['F2W'], 'L0_gnn_F2b': _L0_gnn_in['F2b'], 'L0_gnn_gn': _L0_gnn_in['gn'], 'L0_gnn_bn': _L0_gnn_in['bn'], 'L0_gnn_emb': _L0_gnn_in['emb'], 'L0_gnn_adapt': _L0_gnn_in['adapt'], 'L1_gnn_W': _L1_gnn_in['W'], 'L1_gnn_b': _L1_gnn_in['b']}

def reference(x, src, dst, edge_attr_40, edge_weight, node_type_119, node_vec, L0_gnn_Wq, L0_gnn_gq, L0_gnn_bq, L0_gnn_Wk, L0_gnn_gk, L0_gnn_bk, L0_gnn_Wm, L0_gnn_Wu, L0_gnn_go, L0_gnn_bo, L0_gnn_F1W, L0_gnn_F1b, L0_gnn_F2W, L0_gnn_F2b, L0_gnn_gn, L0_gnn_bn, L0_gnn_emb, L0_gnn_adapt, L1_gnn_W, L1_gnn_b):
    import jax
    import jax.numpy as jnp

    def _L0_gnn_ref(h, edge_index, edge_attr, distances, atom_z, node_mult, batch, Wq, gq, bq, Wk, gk, bk, Wm, Wu, go, bo, F1W, F1b, F2W, F2b, gn, bn, emb, adapt):
        import jax, jax.numpy as jnp
        import numpy as np
        N = 6250
        E = 150000
        H = 48
        RBF = 40
        L = 4
        NELEM = 119
        G = 32
        CUT = 6.0

        def _ln(x, g, b):
            m = x.mean(-1, keepdims=True)
            v = ((x - m) ** 2).mean(-1, keepdims=True)
            return (x - m) * jax.lax.rsqrt(v + 1e-05) * g + b
        src, dst = (edge_index[0], edge_index[1])
        gate = jax.nn.silu(edge_attr @ F1W + F1b) @ F2W + F2b
        ei = emb[atom_z[src]]
        ej = emb[atom_z[dst]]
        gate = gate + (ei * (ej @ adapt)).sum(-1, keepdims=True)
        cw = jnp.where(distances < CUT, 0.5 * (jnp.cos(jnp.pi * distances / CUT) + 1.0), 0.0)
        mj = node_mult[dst]
        msg = gate * h[dst] * (cw * mj)[:, None]
        agg = jax.ops.segment_sum(msg, src, num_segments=N)
        tot = jnp.clip(jax.ops.segment_sum(mj, src, num_segments=N), 1e-08, None)
        h = _ln(h + agg / tot[:, None], gn, bn)
        logm = jnp.log(jnp.clip(node_mult, 1.0, None))
        for i in range(L):
            Q = _ln(h @ Wq[i], gq[i], bq[i])
            K = _ln(h @ Wk[i], gk[i], bk[i])
            qi = Q[src]
            kj = K[dst]
            score = (qi * kj).sum(-1) + 0.1 * (edge_attr * qi[:, :RBF]).sum(-1) + logm[dst]
            smax = jax.ops.segment_max(score, src, num_segments=N)
            es = jnp.exp(jnp.minimum(score - smax[src], 20.0))
            denom = jax.ops.segment_sum(es, src, num_segments=N)
            alpha = es / (denom[src] + 1e-10)
            m = h[dst] @ Wm[i]
            aggi = jax.ops.segment_sum(alpha[:, None] * m, src, num_segments=N)
            z = jnp.concatenate([h, aggi], axis=-1) @ Wu[i]
            z = jnp.where(z > 0, z, 0.01 * z)
            h = _ln(h + z, go[i], bo[i])
        return h

    def _L1_gnn_ref(x, edge_index, W, b):
        import jax, jax.numpy as jnp
        import numpy as np
        N_NODES = 12500
        N_EDGES = 200000
        C_IN = 48
        C_OUT = 48
        N = x.shape[0]
        loops = jnp.arange(N, dtype=edge_index.dtype)
        src = jnp.concatenate([edge_index[0], loops])
        dst = jnp.concatenate([edge_index[1], loops])
        deg = jax.ops.segment_sum(jnp.ones(src.shape, dtype=x.dtype), dst, num_segments=N)
        dinv = jnp.where(deg > 0, jax.lax.rsqrt(deg), 0.0)
        norm = dinv[src] * dinv[dst]
        h = x @ W
        msg = h[src] * norm[:, None]
        out = jax.ops.segment_sum(msg, dst, num_segments=N)
        return out + b
    edge_index = jnp.stack([src, dst])
    batch0 = jnp.zeros((6250,), jnp.int32)
    h = jnp.maximum(_layernorm(x, axis=-1), 0.0)
    x = x + _L0_gnn_ref(h, edge_index, edge_attr_40, edge_weight, node_type_119, node_vec, batch0, L0_gnn_Wq, L0_gnn_gq, L0_gnn_bq, L0_gnn_Wk, L0_gnn_gk, L0_gnn_bk, L0_gnn_Wm, L0_gnn_Wu, L0_gnn_go, L0_gnn_bo, L0_gnn_F1W, L0_gnn_F1b, L0_gnn_F2W, L0_gnn_F2b, L0_gnn_gn, L0_gnn_bn, L0_gnn_emb, L0_gnn_adapt)
    h = jnp.maximum(_layernorm(x, axis=-1), 0.0)
    x = x + _L1_gnn_ref(h, edge_index, L1_gnn_W, L1_gnn_b)
    return x

_drawn_inputs = setup_inputs


def setup_inputs(seed=0):
    import zlib

    import numpy as np

    out = dict(_drawn_inputs(seed))
    spreads = {'L0_gnn_gq': (1.0, 0.2),
     'L0_gnn_bq': (0.0, 0.1),
     'L0_gnn_gk': (1.0, 0.2),
     'L0_gnn_bk': (0.0, 2.0),
     'L0_gnn_go': (1.0, 0.2),
     'L0_gnn_bo': (0.0, 0.1),
     'L0_gnn_F1b': (0.0, 0.709),
     'L0_gnn_F2b': (0.0, 0.1),
     'L0_gnn_gn': (1.0, 0.2),
     'L0_gnn_bn': (0.0, 0.1),
     'L1_gnn_b': (0.0, 0.1)}
    factors = {'L0_gnn_emb': 64.0, 'L0_gnn_adapt': 64.0}
    for name, (base, spread) in spreads.items():
        noise = np.random.default_rng([zlib.crc32(name.encode()), seed]).standard_normal(out[name].shape)
        drawn = base * np.exp(spread * noise) if base else spread * noise
        out[name] = jnp.asarray(drawn.astype(out[name].dtype))
    for name, factor in factors.items():
        out[name] = (out[name] * factor).astype(out[name].dtype)
    return out
```

```python
from contextlib import ExitStack

import concourse.bass as bass
from concourse import mybir

F32 = mybir.dt.float32
I32 = mybir.dt.int32
BF16 = mybir.dt.bfloat16
ALU = mybir.AluOpType
ACT = mybir.ActivationFunctionType
AX = mybir.AxisListType
ds = bass.ds

N, E, H, RBF, LAYERS, NELEM, EMB = 6250, 200000, 48, 40, 4, 119, 32
NB = 50
NP = N // NB
P = 128
J = 4
EG = P * J
NG = (E + NB * (EG - 1)) // EG
EC = E // NP
U = 4
RW = RBF + 5
C_SRC, C_CUT, C_DROW, C_DST, C_POS2 = RBF, RBF + 1, RBF + 2, RBF + 3, RBF + 4
MW = H + 1
VW = H + 1
QW = H + 1
KW = 2 * H + 2
GW = H + EMB + 1
CH = 5
NC_ = NB // CH
BIG = 1.0e30
ROUND = 12582912.0
assert NG % U == 0 and NB * NP == N and EC * NP == E and EC % U == 0 and NC_ * CH == NB


def run_steps(eng, body, total):
    for i in range(U):
        body(i, i)
    with eng.Fori(U, total - U, U) as t:
        for u in range(U):
            body(t + u, u)
    for i in range(total - U, total):
        body(i, i % U)


def at_least(i, k):
    return not isinstance(i, int) or i >= k


def before(i, total):
    return not isinstance(i, int) or i < total


def build(nc, x, src, dst, ea, weight, z, mult, Wq, gq, bq, Wk, gk, bk, Wm, Wu, go, bo,
          F1W, F1b, F2W, F2b, gn, bn, emb, adapt, W1, b1, out):
    ctx = ExitStack()
    with ctx:
        def sb(name, shape, dt=F32):
            return ctx.enter_context(nc.sbuf_tensor(name, shape, dt))

        def ps(name, shape, dt=F32):
            return ctx.enter_context(nc.psum_tensor(name, shape, dt))

        def sem(name):
            return ctx.enter_context(nc.semaphore(name))

        def dram(name, shape, dt=F32):
            return nc.dram_tensor(name, shape, dt).ap()

        ctx.enter_context(nc.allow_non_contiguous_dma(reason="short rows of records and index columns"))

        rec_d = dram("rec_d", [NG * EG, RW])
        msg_d = dram("msg_d", [NG * EG, MW])
        emb2_d = dram("emb2_d", [NELEM, 2 * EMB])
        gate_d = dram("gate_d", [N, GW])
        kh_d = dram("kh_d", [N, KW])
        own_d = dram("own_d", [NB, NP, QW])
        ei_d = dram("ei_d", [NB, NP, EMB])
        acc_d = dram("acc_d", [NG, NP, VW])
        blk_d = [dram(f"blk_d{k}", [NG]) for k in range(2)]
        rec_g = rec_d.rearrange("(g p j) c -> g p j c", p=P, j=J)
        msg_g = msg_d.rearrange("(g p j) c -> g p j c", p=P, j=J)

        ident = sb("ident", [P, P])
        ones = sb("ones", [P, P])
        upper = sb("upper", [P, P])
        row_iota = sb("row_iota", [P, NP])
        blk_iota = sb("blk_iota", [P, NB])
        grp_iota = sb("grp_iota", [NG // J, J])
        eps = sb("eps", [P, 1])
        half_pi = sb("half_pi", [P, 1])
        X = sb("X", [NP, NB, H])
        HA = sb("HA", [NP, NB, 2 * H])
        big_a = sb("big_a", [NP, NB, 2 * H])
        big_b = sb("big_b", [NP, NB, 2 * H])
        agg_in = sb("agg_in", [NP, NB, VW])
        row_out = sb("row_out", [NP, NB * KW])
        own_out = sb("own_out", [NP, NB, QW])
        stat = sb("stat", [NP, 3, 2 * NB])
        mult_sb = sb("mult_sb", [NP, NB])
        logm = sb("logm", [NP, NB])
        z_sb = sb("z_sb", [NP, NB], I32)
        dinv = sb("dinv", [NP, NB])
        emb_sb = sb("emb_sb", [NELEM, 2 * EMB])
        embT = sb("embT", [EMB, NELEM])
        adapt_sb = sb("adapt_sb", [EMB, EMB])
        F1W_sb = sb("F1W_sb", [RBF, H])
        F1b_sb = sb("F1b_sb", [H, 1])
        F2W_sb = sb("F2W_sb", [H, H])
        F2b_sb = sb("F2b_sb", [1, H])
        wqk = sb("wqk", [H, 2 * H])
        wm = sb("wm", [H, H])
        wmT = sb("wmT", [H, H])
        wub = sb("wub", [H, H])
        wmu = sb("wmu", [H, H])
        wu = sb("wu", [2 * H, H])
        gains = sb("gains", [NP, 6 * H])
        gains_n = sb("gains_n", [NP, 3 * H])
        xT = sb("xT", [2 * H, CH * P])
        row_fill = sb("row_fill", [P, 16 * RW])
        pos1 = sb("pos1", [NP, EC], I32)
        metaf = sb("metaf", [NP, EC, 3])
        metai = sb("metai", [NP, EC, 2], I32)
        cnt = sb("cnt", [NP, NB])
        first = sb("first", [NP, NB])
        groups = sb("groups", [NP, NB])
        gend = sb("gend", [NP, NB])
        cmp_g = sb("cmp_g", [NG // J, J, NB])
        blk_g = sb("blk_g", [NG // J, J])
        blk_row = sb("blk_row", [P, NG + 1])
        keep = [sb(f"keep{k}", [P, NG]) for k in range(2)]
        fresh = sb("fresh", [P, NG])
        blk_i = [sb(f"blk_i{k}", [1, NG], I32) for k in range(2)]
        last_i = [sb(f"last_i{k}", [1, NB], I32) for k in range(2)]

        rec = [sb(f"rec{s}", [P, J, RW]) for s in range(U)]
        row = [sb(f"row{s}", [P, J, KW]) for s in range(U)]
        own = [sb(f"own{s}", [NP, QW]) for s in range(U)]
        oh = [sb(f"oh{s}", [P, J, NP]) for s in range(U)]
        ohT = [sb(f"ohT{s}", [NP, J * P]) for s in range(2)]
        neg_t = [sb(f"neg{s}", [P, J * P]) for s in range(2)]
        neg = [neg_t[s][:, 0:J * NP].rearrange("p (j n) -> p j n", j=J) for s in range(2)]
        masked_t = [sb(f"masked{s}", [P, J * P]) for s in range(2)]
        masked = [masked_t[s][:, 0:J * NP].rearrange("p (j n) -> p j n", j=J) for s in range(2)]
        prod = [sb(f"prod{s}", [P, J, QW]) for s in range(2)]
        score = [sb(f"score{s}", [P, J]) for s in range(U)]
        smax = [sb(f"smax{s}", [NP, 1]) for s in range(U)]
        gmax = sb("gmax", [NP, 1])
        arg = [sb(f"arg{s}", [P, J + 1]) for s in range(U)]
        es = [sb(f"es{s}", [P, J + 1]) for s in range(U)]
        vals = [sb(f"vals{s}", [P, J, VW]) for s in range(2)]
        acc = [sb(f"acc{s}", [NP, VW]) for s in range(U)]
        idx = [sb(f"idx{s}", [NP, U], I32) for s in range(U)]

        flat_a = big_a[:, :, :].rearrange("p a b -> p (a b)")
        flat_b = big_b[:, :, :].rearrange("p a b -> p (a b)")
        key_i = [agg_in[:, :, :].rearrange("p a b -> p (a b)")[:, 0:EC].bitcast(I32),
                 row_out[:, 0:EC].bitcast(I32)]
        keyf, blk, mask = flat_a[:, 0:EC], flat_a[:, EC:2 * EC], flat_a[:, 2 * EC:3 * EC]
        cum, pos, zero_e = flat_b[:, 0:EC], flat_b[:, EC:2 * EC], flat_b[:, 2 * EC:3 * EC]
        wt = row_out[:, EC:2 * EC]
        cosw = row_out[:, 2 * EC:3 * EC]
        FILL = 16
        fill_r = row_fill[:, 0:FILL * RW].rearrange("p (f c) -> p f c", c=RW)
        fill_m = fill_r[:, :, :].rearrange("p a b -> p (a b)")

        p_ohT = [ps(f"p_ohT{s}", [P, J * P]) for s in range(2)]
        p_mT = [ps(f"p_mT{s}", [P, J * P]) for s in range(2)]
        p_own = ps("p_own", [P, 512])
        p_mg = ps("p_mg", [P, 512])
        p_agg = ps("p_agg", [P, 512])
        p_x = ps("p_x", [P, 512])
        own_bank = [p_own, p_x]
        agg_bank = [p_agg, p_mg]

        def bc(ap, shape):
            return ap.to_broadcast(shape)

        loaded = sem("loaded")
        consts = sem("consts")
        fills = sem("fills")
        filled = sem("filled")
        fill2 = sem("fill2")
        filled2 = sem("filled2")
        ready_emb = sem("ready_emb")
        counted = sem("counted")
        summed = sem("summed")
        taken = sem("taken")
        blk_made = sem("blk_made")
        blk_out = sem("blk_out")
        blk_in = sem("blk_in")
        cos_in = sem("cos_in")
        cos_out = sem("cos_out")
        small = sem("small")
        embT_p = sem("embT_p")
        embT_s = sem("embT_s")
        emb_p = sem("emb_p")
        emb_s = sem("emb_s")
        emb_out = sem("emb_out")
        var1 = sem("var1")
        std1 = sem("std1")

        def layer_norm(eng, dst_, src_, shape, var_sem, std_sem, v, tmp=None):
            n = shape[1]
            mean, var, rstd = stat[:, 0, 0:n], stat[:, 1, 0:n], stat[:, 2, 0:n]
            eng.tensor_reduce(mean, src_, AX.X, ALU.add)
            eng.drain()
            eng.tensor_scalar(mean, mean, 1.0 / H, None, ALU.mult)
            eng.drain()
            eng.tensor_tensor(dst_, src_, bc(mean.unsqueeze(2), shape), ALU.subtract)
            eng.drain()
            eng.tensor_tensor(tmp, dst_, dst_, ALU.mult)
            eng.drain()
            eng.tensor_reduce(var, tmp, AX.X, ALU.add).then_inc(var_sem, 1)
            eng.wait_ge(std_sem, v)
            eng.reciprocal(rstd, rstd)
            eng.drain()
            eng.tensor_tensor(dst_, dst_, bc(rstd.unsqueeze(2), shape), ALU.mult)
            eng.drain()

        def layer_norm_in_place(eng, y, tmp, shape, var_sem, std_sem, v):
            layer_norm(eng, y, y, shape, var_sem, std_sem, v, tmp=tmp)

        def deviation(eng, n, var_sem, std_sem, v):
            eng.wait_ge(var_sem, v)
            eng.activation(stat[:, 2, 0:n], stat[:, 1, 0:n], ACT.Sqrt, bias=eps[0:NP, 0:1],
                           scale=1.0 / H).then_inc(std_sem, 1)

        with nc.Block() as block:
            @block.sync
            def _(sp):
                sp.dma_start(key_i[0], src.rearrange("(p t) -> p t", p=NP)).then_inc(loaded, 16)
                sp.dma_start(key_i[1], dst.rearrange("(p t) -> p t", p=NP)).then_inc(loaded, 16)
                sp.dma_start(wt, weight.rearrange("(p t) -> p t", p=NP)).then_inc(loaded, 16)
                sp.dma_start(X[:, :, :], x.rearrange("(p b) c -> p b c", b=NB)).then_inc(loaded, 16)
                sp.dma_start(mult_sb[:, :], mult.rearrange("(p b) -> p b", b=NB)).then_inc(loaded, 16)
                sp.dma_start(z_sb[:, :], z.rearrange("(p b) -> p b", b=NB)).then_inc(loaded, 16)
                sp.dma_start(emb_sb[:, 0:EMB], emb).then_inc(loaded, 16)
                sp.dma_start(adapt_sb[:, :], adapt).then_inc(loaded, 16)
                sp.dma_start(F1W_sb[:, :], F1W).then_inc(loaded, 16)
                sp.dma_start(F1b_sb[:, :], F1b.rearrange("(p a) -> p a", a=1)).then_inc(loaded, 16)
                sp.dma_start(F2W_sb[:, :], F2W).then_inc(loaded, 16)
                sp.dma_start(F2b_sb[:, :], F2b.rearrange("(a p) -> a p", a=1)).then_inc(loaded, 16)
                for k, v in enumerate((gn, bn, b1)):
                    sp.dma_start(gains_n[:, k * H:(k + 1) * H],
                                 v.rearrange("(a p) -> a p", a=1).to_broadcast([NP, H])).then_inc(loaded, 16)
                sp.wait_ge(fills, 1)
                sp.dma_start(rec_d.rearrange("(q p f) c -> p q (f c)", p=P, f=FILL),
                             fill_r[:, :, :].rearrange("p f c -> p (f c)").unsqueeze(1)
                             .to_broadcast([P, NG * EG // P // FILL, FILL * RW])).then_inc(filled, 16)
                sp.wait_ge(emb_s, 1)
                sp.dma_start(emb2_d, emb_sb[:, :]).then_inc(emb_out, 16)
                sp.wait_ge(emb_out, 16)
                for k in range(2):
                    sp.wait_ge(blk_made, k + 1)
                    sp.dma_start(blk_d[k].rearrange("(p j) -> p j", j=J), blk_g[:, :]).then_inc(blk_out, 16)
                    sp.wait_ge(blk_out, 16 * (k + 1))
                    sp.dma_start(blk_row[:, 1:NG + 1], blk_d[k].rearrange("(a n) -> a n", a=1)
                                 .to_broadcast([P, NG])).then_inc(blk_in, 16)
                sp.wait_ge(filled, 16)

            @block.gpsimd
            def _(pool):
                pool.memset(ident[:, :], 0.0).then_inc(consts, 1)
                pool.memset(ones[:, :], 1.0).then_inc(consts, 1)
                pool.iota(row_iota[:, :], pattern=[[1, NP]], base=0, channel_multiplier=0,
                          allow_small_or_imprecise_dtypes=True).then_inc(consts, 1)
                pool.iota(blk_iota[:, :], pattern=[[1, NB]], base=0, channel_multiplier=0,
                          allow_small_or_imprecise_dtypes=True).then_inc(consts, 1)
                pool.iota(grp_iota[:, :], pattern=[[1, J]], base=0, channel_multiplier=J,
                          allow_small_or_imprecise_dtypes=True).then_inc(consts, 1)
                pool.wait_ge(consts, 5)
                pool.affine_select(out=ident[:, :], in_=ident[:, :], compare_op=ALU.not_equal, fill=1.0,
                                   base=0, pattern=[[-1, P]], channel_multiplier=1).then_inc(consts, 1)
                pool.affine_select(out=upper[:, :], in_=ones[:, :], compare_op=ALU.is_gt, fill=0.0,
                                   base=0, pattern=[[1, P]], channel_multiplier=-1).then_inc(consts, 1)
                pool.wait_ge(loaded, 16 * 15)
                pool.wait_ge(emb_out, 16)
                for b in range(NB):
                    pool.indirect_dma_start(
                        out=HA[:, b, 0:2 * EMB], out_offset=None, in_=emb2_d[:, :],
                        in_offset=bass.IndirectOffsetOnAxis(ap=z_sb[:, b:b + 1], axis=0)
                    ).then_inc(ready_emb, 16)
                pool.wait_ge(ready_emb, 16 * NB)

            @block.tensor
            def _(pe):
                pe.wait_ge(consts, 7)
                pe.wait_ge(loaded, 16 * 15)
                pe.transpose(p_x[0:EMB, 0:NELEM], emb_sb[:, 0:EMB], ident[0:NELEM, 0:NELEM]).then_inc(embT_p, 1)
                pe.wait_ge(embT_s, 1)
                pe.matmul(p_x[0:NELEM, 256:256 + EMB], embT[:, :], adapt_sb[:, :],
                          start=True, stop=True).then_inc(emb_p, 1)
                for k in range(2):
                    pe.wait_ge(counted, k + 1)
                    if k:
                        pe.wait_ge(taken, k)
                    pe.matmul(p_own[0:NP, 0:NB], upper[0:NP, 0:NP], cnt[:, :], start=True, stop=True)
                    pe.matmul(p_own[0:NP, 256:256 + NB], ones[0:NP, 0:NP], cnt[:, :], start=True,
                              stop=True).then_inc(summed, 1)

            @block.scalar
            def _(act):
                act.wait_ge(embT_p, 1)
                act.activation(embT[:, :], p_x[0:EMB, 0:NELEM], ACT.Copy).then_inc(embT_s, 1)
                act.wait_ge(emb_p, 1)
                act.activation(emb_sb[:, EMB:2 * EMB], p_x[0:NELEM, 256:256 + EMB], ACT.Copy).then_inc(emb_s, 1)
                act.wait_ge(cos_in, 1)
                act.activation(cosw, cosw, ACT.Sin, bias=half_pi[0:NP, 0:1],
                               scale=-3.141592653589793 / 6.0).then_inc(cos_out, 1)
                deviation(act, NB, var1, std1, 1)

            @block.vector
            def _(v):
                v.memset(fill_r[:, :, 0:C_SRC], 0.0)
                v.memset(fill_r[:, :, C_SRC:C_SRC + 1], -1.0)
                v.memset(fill_r[:, :, C_CUT:C_DST + 1], 0.0)
                v.memset(fill_r[:, :, C_POS2:RW].bitcast(I32), 2 * NG * EG).then_inc(fills, 1)
                v.memset(zero_e, 0.0)
                v.memset(eps[:, :], 1.0e-5)
                v.memset(half_pi[:, :], 3.141592653589793 / 2.0)
                for s in range(U):
                    v.memset(arg[s][:, :], 0.0)
                    v.memset(smax[s][:, :], -BIG)
                    v.memset(acc[s][:, :], 0.0)
                v.memset(blk_row[:, 0:1], -1.0)
                v.wait_ge(consts, 7)
                v.wait_ge(loaded, 16 * 15)
                v.scalar_tensor_tensor(out=cosw, in0=wt, scalar=-1.0, in1=wt, op0=ALU.mult, op1=ALU.max)
                v.drain()
                v.tensor_scalar(cosw, cosw, 6.0, None, ALU.min).then_inc(cos_in, 1)
                for k in range(2):
                    v.tensor_copy(keyf, key_i[k])
                    v.drain()
                    v.tensor_scalar(mask, keyf, 1.0 / NB, 0.5 / NB - 0.5, ALU.mult, ALU.add)
                    v.drain()
                    where = metaf[:, :, 0] if k == 0 else metaf[:, :, 2]
                    v.tensor_scalar(where, mask, ROUND, ROUND, ALU.add, ALU.subtract)
                    v.drain()
                    v.scalar_tensor_tensor(out=blk, in0=where, scalar=-float(NB), in1=keyf,
                                           op0=ALU.mult, op1=ALU.add)
                    v.drain()
                    for b in range(NB):
                        v.tensor_scalar(mask, blk, float(b), 0.0, ALU.is_equal, ALU.add,
                                        accum_out=cnt[:, b:b + 1])
                        v.drain()
                    v.drain().then_inc(counted, 1)
                    v.wait_ge(summed, k + 1)
                    v.tensor_scalar(groups[:, :], p_own[0:NP, 256:256 + NB], 1.0 / EG, 0.5 - 0.5 / EG,
                                    ALU.mult, ALU.add)
                    v.drain()
                    v.tensor_scalar(groups[:, :], groups[:, :], ROUND, ROUND, ALU.add, ALU.subtract)
                    v.drain()
                    v.tensor_scalar(groups[:, :], groups[:, :], 1.0, None, ALU.max)
                    v.drain()
                    v.tensor_tensor_scan(gend[:, :], groups[:, :], zero_e[:, 0:NB], 0.0, ALU.add, ALU.add)
                    v.drain()
                    v.tensor_tensor(first[:, :], gend[:, :], groups[:, :], ALU.subtract)
                    v.drain()
                    v.tensor_scalar(first[:, :], first[:, :], float(EG), -1.0, ALU.mult, ALU.add)
                    v.drain()
                    v.tensor_tensor(first[:, :], first[:, :], p_own[0:NP, 0:NB], ALU.add).then_inc(taken, 1)
                    v.tensor_scalar(last_i[k][:, :], gend[0:1, :], -1.0, None, ALU.add)
                    v.tensor_tensor(cmp_g[:, :, :], bc(gend[0:NG // J, :].unsqueeze(1), [NG // J, J, NB]),
                                    bc(grp_iota[:, :].unsqueeze(2), [NG // J, J, NB]), ALU.is_le)
                    v.drain()
                    if k:
                        v.wait_ge(blk_out, 16)
                    v.tensor_reduce(blk_g[:, :], cmp_g[:, :, :], AX.X, ALU.add)
                    v.drain()
                    v.tensor_scalar(blk_g[:, :], blk_g[:, :], float(NB - 1), None, ALU.min).then_inc(blk_made, 1)
                    for b in range(NB):
                        v.tensor_scalar(mask, blk, float(b), None, ALU.is_equal)
                        v.drain()
                        v.tensor_tensor_scan(cum, mask, zero_e, first[:, b:b + 1], ALU.add, ALU.add)
                        v.drain()
                        v.copy_predicated(pos, mask.bitcast(I32), cum)
                        v.drain()
                    if k == 0:
                        v.tensor_copy(pos1[:, :], pos)
                    else:
                        v.tensor_copy(metai[:, :, 1], pos)
                    v.wait_ge(blk_in, 16 * (k + 1))
                    v.tensor_copy(blk_i[k][:, :], blk_row[0:1, 1:NG + 1])
                    v.tensor_tensor(keep[k][:, :], blk_row[:, 1:NG + 1], blk_row[:, 0:NG], ALU.is_equal)
                    v.drain()
                v.tensor_scalar(fresh[:, :], keep[0][:, :], -1.0, 2.0 * BIG, ALU.add, ALU.mult)
                v.tensor_copy(metai[:, :, 0], key_i[1])
                v.wait_ge(cos_out, 1)
                v.tensor_scalar(metaf[:, :, 1], cosw, 1.0, 0.5, ALU.add, ALU.mult)
                v.drain()
                layer_norm(v, big_a[:, :, 0:H], X[:, :, :], [NP, NB, H], var1, std1, 1, tmp=big_b[:, :, 0:H])
                g_rows = row_out[:, 0:NB * GW].rearrange("p (b c) -> p b c", b=NB)
                v.tensor_scalar(g_rows[:, :, 0:H], big_a[:, :, 0:H], 0.0, None, ALU.max)
                v.wait_ge(ready_emb, 16 * NB)
                v.tensor_copy(g_rows[:, :, H:H + EMB], HA[:, :, EMB:2 * EMB])
                v.tensor_copy(g_rows[:, :, H + EMB:GW], mult_sb[:, :].unsqueeze(2))
                v.tensor_copy(own_out[:, :, 0:EMB], HA[:, :, 0:EMB])
                v.drain()
                v.tensor_copy(HA[:, :, 0:H], g_rows[:, :, 0:H])
                v.drain()

        tabs_out = sem("tabs_out")
        ea_in = [sem(f"ea_in{s}") for s in range(U)]
        meta_in = sem("meta_in")
        sent = [sem(f"sent{s}") for s in range(U)]
        hot = sem("hot")
        hist = sem("hist")
        held = sem("held")
        hist_n = sem("hist_n")
        hot_r = [oh[s][:, :, :].rearrange("p a b -> p (a b)")[:, 0:J * NP // 2].bitcast(BF16)
                 .rearrange("p (a b) -> p a b", a=J) for s in range(2)]
        hot_b = [masked_t[s][:, 0:J * NB // 2].bitcast(BF16)
                 .rearrange("p (a b) -> p a b", a=J) for s in range(2)]
        ea_p = ea.rearrange("(p t) c -> p t c", p=NP)
        STEPS = EC // U

        with nc.Block() as block:
            @block.sync
            def _(sp):
                sp.dma_start(gate_d.rearrange("(p b) c -> p (b c)", b=NB), row_out[:, 0:NB * GW]).then_inc(tabs_out, 16)
                sp.dma_start(ei_d.rearrange("b p c -> p b c"), own_out[:, :, 0:EMB]).then_inc(tabs_out, 16)
                sp.wait_ge(fill2, 1)
                sp.dma_start(msg_d.rearrange("(q p f) c -> p q (f c)", p=P, f=8),
                             fill_m[:, 0:8 * MW].unsqueeze(1)
                             .to_broadcast([P, NG * EG // P // 8, 8 * MW])).then_inc(filled2, 16)

                def body(i, u):
                    if at_least(i, U):
                        sp.wait_ge(sent[u], 16 * (i - u))
                    sp.dma_start(rec[u][0:NP, :, 0:RBF], ea_p[:, ds(i * J, J), :]).then_inc(ea_in[u], 16)
                run_steps(sp, body, STEPS)
                sp.wait_ge(filled2, 16)
                sp.wait_ge(tabs_out, 32)

            @block.vector
            def _(v):
                v.memset(fill_r[:, :, :], 0.0)
                v.drain()
                v.memset(fill_m[:, 0:8 * MW].rearrange("p (f c) -> p f c", c=MW)[:, :, H:MW], -1.0)
                v.drain().then_inc(fill2, 1)

                def body(i, u):
                    if at_least(i, U):
                        v.wait_ge(sent[u], 16 * (i - u))
                        v.sem_inc(held, 1)
                    v.tensor_copy(rec[u][0:NP, :, C_DST:RW].bitcast(I32), metai[:, ds(i * J, J), :])
                    v.tensor_copy(rec[u][0:NP, :, C_SRC:C_DST], metaf[:, ds(i * J, J), :])
                    v.tensor_copy(idx[u][:, :], pos1[:, ds(i * J, J)]).then_inc(meta_in, 1)
                    if at_least(i, 2):
                        v.wait_ge(hist, i - 1)
                    v.tensor_tensor(hot_r[u % 2][0:NP], bc(row_iota[0:NP, :].unsqueeze(1), [NP, J, NP]),
                                    bc(metaf[:, ds(i * J, J), 2:3], [NP, J, NP]), ALU.is_equal)
                    v.scalar_tensor_tensor(out=score[u][0:NP, :].unsqueeze(2), in0=metaf[:, ds(i * J, J), 2:3],
                                           scalar=-float(NB), in1=metai[:, ds(i * J, J), 0:1],
                                           op0=ALU.mult, op1=ALU.add)
                    v.drain()
                    v.tensor_tensor(hot_b[u % 2][0:NP], bc(blk_iota[0:NP, :].unsqueeze(1), [NP, J, NB]),
                                    bc(score[u][0:NP, :].unsqueeze(2), [NP, J, NB]), ALU.is_equal).then_inc(hot, 1)
                run_steps(v, body, STEPS)
                v.wait_ge(hist, STEPS)
                v.tensor_scalar(dinv[:, :], p_x[0:NP, 0:NB], 1.0, None, ALU.add)
                v.drain().then_inc(hist_n, 1)
                v.wait_ge(hist_n, 2)
                v.reciprocal(dinv[:, :], dinv[:, :])
                v.drain()

            @block.scalar
            def _(act):
                act.wait_ge(hist_n, 1)
                act.activation(dinv[:, :], dinv[:, :], ACT.Sqrt)
                act.drain()
                act.activation(logm[:, :], mult_sb[:, :], ACT.Copy, bias=-1.0)
                act.drain()
                act.activation(logm[:, :], logm[:, :], ACT.Relu)
                act.drain()
                act.activation(logm[:, :], logm[:, :], ACT.Ln, bias=ones[0:NP, 0:1])
                act.drain().then_inc(hist_n, 1)

            @block.tensor
            def _(pe):
                def body(i, u):
                    pe.wait_ge(hot, i + 1)
                    for j in range(J):
                        mm = pe.matmul(p_x[0:NP, 0:NB], hot_r[u % 2][0:NP, j, :], hot_b[u % 2][0:NP, j, :],
                                       start=isinstance(i, int) and i == 0 and j == 0,
                                       stop=isinstance(i, int) and i == STEPS - 1 and j == J - 1,
                                       skip_group_check=True)
                    mm.then_inc(hist, 1)
                run_steps(pe, body, STEPS)

            @block.gpsimd
            def _(pool):
                def body(i, u):
                    pool.wait_ge(ea_in[u], 4 * (i - u) + 16)
                    pool.wait_ge(meta_in, i + 1)
                    pool.sem_inc(held, 1)
                    for j in range(J):
                        pool.indirect_dma_start(
                            out=rec_d[:, :], out_offset=bass.IndirectOffsetOnAxis(ap=idx[u][:, j:j + 1], axis=0),
                            in_=rec[u][0:NP, j, :], in_offset=None).then_inc(sent[u], 16)
                run_steps(pool, body, STEPS)
                for u in range(U):
                    pool.wait_ge(sent[u], 16 * STEPS)

        def sums_of_blocks(sp, k, base, sums_in, accs, total):
            for s in range(U):
                sp.wait_ge(accs[s], 4 * base + 4 * total)
            sp.sem_inc(held, 1)
            with sp.Fori(0, NB) as b:
                g = sp.value_load(last_i[k][0:1, ds(b, 1)], min_val=0, max_val=NG - 1)
                sp.dma_start(agg_in[:, ds(b, 1), :], acc_d[ds(g, 1), :, :].rearrange("a p c -> p a c")).then_inc(sums_in, 16)

        def one_hot(v, i, u, base, col, ready, arrived, tile):
            v.tensor_tensor(oh[u][:, :, :], bc(row_iota[:, :].unsqueeze(1), [P, J, NP]),
                            bc(tile[u][:, :, col:col + 1], [P, J, NP]), ALU.is_equal).then_inc(ready, 1)

        def gather_rows(pool, table, u, width, arrived):
            for j in range(J):
                pool.indirect_dma_start(
                    out=row[u][:, j, 0:width], out_offset=None, in_=table,
                    in_offset=bass.IndirectOffsetOnAxis(ap=rec[u][:, j, C_DST:C_DST + 1].bitcast(I32), axis=0)
                ).then_inc(arrived[u], 16)

        def flip_one_hot(pe, u, flipped_p):
            for j in range(J):
                mm = pe.transpose(p_ohT[u % 2][0:NP, j * P:(j + 1) * P], oh[u][:, j, :], ident[:, :])
            mm.then_inc(flipped_p, 1)

        def gather_own(pe, u, bank, width, done):
            for j in range(J):
                mm = pe.matmul(bank[:, j * width:(j + 1) * width], ohT[u % 2][:, j * P:(j + 1) * P],
                               own[u][:, 0:width], start=True, stop=True)
            mm.then_inc(done, 1)

        def sum_group(pe, u, bank, rhs, done):
            for j in range(J):
                mm = pe.matmul(bank[0:NP, 0:VW], oh[u][:, j, :], rhs[:, j, :],
                               start=(j == 0), stop=(j == J - 1))
            mm.then_inc(done, 1)

        def load_group(sp, i, u, base, own_tab, width, arrived, used):
            if at_least(i, U):
                sp.wait_ge(used, base + i - U + 1)
                sp.sem_inc(held, 1)
            b = sp.value_load(blk_i[0][0:1, ds(i, 1)], min_val=0, max_val=NB - 1)
            sp.dma_start(rec[u][:, :, :].rearrange("p j c -> p (j c)"),
                         rec_g[ds(i, 1), :, :, :].rearrange("a p j c -> p (a j c)")).then_inc(arrived[u], 16)
            sp.dma_start(own[u][:, 0:width], own_tab[ds(b, 1), :, :].rearrange("a p c -> p (a c)")).then_inc(arrived[u], 16)

        g_rec = [sem(f"g_rec{s}") for s in range(U)]
        g_row = [sem(f"g_row{s}") for s in range(U)]
        g_hot = sem("g_hot")
        g_flip_p = sem("g_flip_p")
        g_flip = sem("g_flip")
        g_eaT_p = sem("g_eaT_p")
        g_eaT = sem("g_eaT")
        g_own = sem("g_own")
        g_f1 = sem("g_f1")
        g_silu = sem("g_silu")
        g_gate = sem("g_gate")
        g_vals = sem("g_vals")
        g_agg = sem("g_agg")
        g_acc = sem("g_acc")
        g_store = [sem(f"g_store{s}") for s in range(U)]
        g_sums = sem("g_sums")
        g_var = sem("g_var")
        g_std = sem("g_std")
        eaT = [masked_t[s][0:RBF, :] for s in range(2)]
        silu = [neg_t[s][0:H, :] for s in range(2)]

        with nc.Block() as block:
            @block.sync
            def _(sp):
                run_steps(sp, lambda i, u: load_group(sp, i, u, 0, ei_d, EMB, g_rec, g_vals), NG)
                sums_of_blocks(sp, 0, 0, g_sums, g_store, NG)
                sp.wait_ge(g_sums, 16 * NB)

            @block.gpsimd
            def _(pool):
                def body(i, u):
                    pool.wait_ge(g_rec[u], 8 * (i - u) + 32)
                    if at_least(i, U):
                        pool.wait_ge(g_vals, i - U + 1)
                    pool.sem_inc(held, 1)
                    gather_rows(pool, gate_d[:, :], u, GW, g_row)
                run_steps(pool, body, NG)

            @block.vector
            def _(v):
                def hots(i, u):
                    v.wait_ge(g_rec[u], 8 * (i - u) + 32)
                    one_hot(v, i, u, 0, C_SRC, g_hot, None, rec)

                def weights(i, u):
                    s = u % 2
                    v.wait_ge(g_row[u], 16 * (i - u) + 64)
                    v.tensor_tensor(arg[u][:, 0:J].unsqueeze(2), rec[u][:, :, C_CUT:C_CUT + 1],
                                    row[u][:, :, H + EMB:GW], ALU.mult)
                    v.wait_ge(g_own, i + 1)
                    v.tensor_tensor(prod[s][:, :, 0:EMB], row[u][:, :, H:H + EMB],
                                    own_bank[s][:, 0:J * EMB].rearrange("p (j c) -> p j c", j=J), ALU.mult)
                    v.drain()
                    v.tensor_reduce(score[u][:, :], prod[s][:, :, 0:EMB], AX.X, ALU.add)
                    v.tensor_tensor(row[u][:, :, 0:H], row[u][:, :, 0:H],
                                    bc(arg[u][:, 0:J].unsqueeze(2), [P, J, H]), ALU.mult)
                    v.drain()
                    v.wait_ge(g_gate, i + 1)
                    v.tensor_tensor(prod[s][:, :, 0:H], p_mg[:, 0:J * H].rearrange("p (j c) -> p j c", j=J),
                                    bc(score[u][:, :].unsqueeze(2), [P, J, H]), ALU.add)
                    v.drain()
                    v.tensor_copy(vals[s][:, :, H:VW], row[u][:, :, H + EMB:GW])
                    v.tensor_tensor(vals[s][:, :, 0:H], prod[s][:, :, 0:H], row[u][:, :, 0:H],
                                    ALU.mult).then_inc(g_vals, 1)

                def sums(i, u):
                    v.wait_ge(g_agg, i + 1)
                    if at_least(i, U):
                        v.wait_ge(g_store[u], 4 * (i - u))
                    v.scalar_tensor_tensor(out=acc[u][:, :], in0=acc[(u - 1) % U][:, :],
                                           scalar=keep[0][0:NP, ds(i, 1)], in1=p_agg[0:NP, 0:VW],
                                           op0=ALU.mult, op1=ALU.add).then_inc(g_acc, 1)

                def body(i, u):
                    if before(i + 1, NG):
                        hots(i + 1, (u + 1) % U)
                    weights(i, u)
                    if at_least(i, 1):
                        sums(i - 1, (u - 1) % U)
                hots(0, 0)
                run_steps(v, body, NG)
                sums(NG - 1, (NG - 1) % U)
                v.wait_ge(g_sums, 16 * NB)
                v.tensor_scalar(stat[:, 0, 0:NB], agg_in[:, :, H], 1.0e-8, None, ALU.max)
                v.drain()
                v.reciprocal(stat[:, 0, 0:NB], stat[:, 0, 0:NB])
                v.drain()
                v.tensor_tensor(big_a[:, :, 0:H], agg_in[:, :, 0:H], bc(stat[:, 0, 0:NB].unsqueeze(2), [NP, NB, H]), ALU.mult)
                v.drain()
                v.tensor_tensor(big_a[:, :, 0:H], big_a[:, :, 0:H], HA[:, :, 0:H], ALU.add)
                v.drain()
                layer_norm(v, HA[:, :, 0:H], big_a[:, :, 0:H], [NP, NB, H], g_var, g_std, 1, tmp=big_b[:, :, 0:H])
                v.tensor_tensor(HA[:, :, 0:H], HA[:, :, 0:H], bc(gains_n[:, 0:H].unsqueeze(1), [NP, NB, H]), ALU.mult)
                v.drain()
                v.tensor_tensor(HA[:, :, 0:H], HA[:, :, 0:H], bc(gains_n[:, H:2 * H].unsqueeze(1), [NP, NB, H]), ALU.add)
                v.drain()

            @block.scalar
            def _(act):
                def turned(i, u):
                    s = u % 2
                    act.wait_ge(g_flip_p, i + 1)
                    if at_least(i, 2):
                        act.wait_ge(g_own, i - 1)
                    act.activation(ohT[s][:, :], p_ohT[s][0:NP, :], ACT.Copy).then_inc(g_flip, 1)
                    act.wait_ge(g_eaT_p, i + 1)
                    if at_least(i, 2):
                        act.wait_ge(g_f1, i - 1)
                    act.activation(eaT[s][:, :], p_mT[0][0:RBF, :], ACT.Copy).then_inc(g_eaT, 1)
                    act.wait_ge(g_f1, i + 1)
                    if at_least(i, 2):
                        act.wait_ge(g_gate, i - 1)
                    act.activation(silu[s][:, :], p_mT[1][0:H, :], ACT.Silu,
                                   bias=F1b_sb[:, 0:1]).then_inc(g_silu, 1)

                def store(i, u):
                    act.wait_ge(g_acc, i + 1)
                    act.dma_start(acc_d[ds(i, 1), :, :].rearrange("a p c -> p (a c)"), acc[u][:, :]).then_inc(g_store[u], 16)

                def body(i, u):
                    if before(i + 1, NG):
                        turned(i + 1, (u + 1) % U)
                    if at_least(i, 2):
                        store(i - 2, (u - 2) % U)
                turned(0, 0)
                run_steps(act, body, NG)
                for i in (NG - 2, NG - 1):
                    store(i, i % U)
                deviation(act, NB, g_var, g_std, 1)

            @block.tensor
            def _(pe):
                def front(i, u):
                    s = u % 2
                    pe.wait_ge(g_hot, i + 1)
                    if at_least(i, 2):
                        pe.wait_ge(g_flip, i - 1)
                    flip_one_hot(pe, u, g_flip_p)
                    if at_least(i, 1):
                        pe.wait_ge(g_eaT, i)
                        pe.sem_inc(held, 1)
                    for j in range(J):
                        mm = pe.transpose(p_mT[0][0:RBF, j * P:(j + 1) * P], rec[u][:, j, 0:RBF], ident[:, :])
                    mm.then_inc(g_eaT_p, 1)
                    if at_least(i, 2):
                        pe.wait_ge(g_vals, i - 1)
                    pe.wait_ge(g_flip, i + 1)
                    gather_own(pe, u, own_bank[u % 2], EMB, g_own)
                    pe.wait_ge(g_eaT, i + 1)
                    if at_least(i, 1):
                        pe.wait_ge(g_silu, i)
                        pe.sem_inc(held, 1)
                    pe.matmul(p_mT[1][0:H, :], F1W_sb[:, :], eaT[s][:, :], start=True, stop=True).then_inc(g_f1, 1)

                def gate(i, u):
                    s = u % 2
                    pe.wait_ge(g_silu, i + 1)
                    if at_least(i, 1):
                        pe.wait_ge(g_vals, i)
                    pe.sem_inc(held, 1)
                    for j in range(J):
                        cols = p_mg[:, j * H:(j + 1) * H]
                        pe.matmul(cols, silu[s][:, j * P:(j + 1) * P], F2W_sb[:, :], start=True, stop=False)
                        mm = pe.matmul(cols, ones[0:1, :], F2b_sb[:, :], start=False, stop=True)
                    mm.then_inc(g_gate, 1)

                def sums(i, u):
                    pe.wait_ge(g_vals, i + 1)
                    if at_least(i, 1):
                        pe.wait_ge(g_acc, i)
                    sum_group(pe, u, p_agg, vals[u % 2], g_agg)

                def body(i, u):
                    gate(i, u)
                    if at_least(i, 1):
                        sums(i - 1, (u - 1) % U)
                    if before(i + 1, NG):
                        front(i + 1, (u + 1) % U)
                front(0, 0)
                run_steps(pe, body, NG)
                sums(NG - 1, (NG - 1) % U)

        w_in = sem("w_in")
        wmT_p = sem("wmT_p")
        wmT_s = sem("wmT_s")
        wmu_p = sem("wmu_p")
        wmu_s = sem("wmu_s")
        wmu_in = sem("wmu_in")
        n_h = sem("n_h")
        t_p = sem("t_p")
        t_s = sem("t_s")
        y_p = sem("y_p")
        y_s = sem("y_s")
        n_var = sem("n_var")
        n_std = sem("n_std")
        n_tab = sem("n_tab")
        n_out = sem("n_out")
        a_agg = sem("a_agg")
        l_done = sem("l_done")
        l_rec = [sem(f"l_rec{s}") for s in range(U)]
        l_row = [sem(f"l_row{s}") for s in range(U)]
        l_hot = sem("l_hot")
        l_flip_p = sem("l_flip_p")
        l_flip = sem("l_flip")
        l_neg = sem("l_neg")
        l_own = sem("l_own")
        l_mask = sem("l_mask")
        l_mT = sem("l_mT")
        l_max = sem("l_max")
        l_mg = sem("l_mg")
        l_arg = sem("l_arg")
        l_es = sem("l_es")
        l_vals = sem("l_vals")
        l_agg = sem("l_agg")
        l_acc = sem("l_acc")
        l_store = [sem(f"l_store{s}") for s in range(U)]
        l_sums = sem("l_sums")

        def dense_pe(pe, c, n, src_, k, w, m, first_):
            if not first_:
                pe.wait_ge(t_s, n)
                pe.sem_inc(held, 1)
            for q in range(CH):
                bank = p_ohT[0] if q < 4 else p_ohT[1]
                mm = pe.transpose(bank[0:k, (q % 4) * P:(q % 4) * P + NP], src_(c * CH + q), ident[0:NP, 0:NP])
            mm.then_inc(t_p, 1)
            pe.wait_ge(t_s, n + 1)
            if not first_:
                pe.wait_ge(y_s, n)
            pe.sem_inc(held, 1)
            for q in range(CH):
                mm = pe.matmul(p_mT[0][0:NP, q * m:(q + 1) * m], xT[0:k, q * P:q * P + NP], w,
                               start=True, stop=True)
            mm.then_inc(y_p, 1)

        def dense_act(act, c, n, k, m, dst_):
            act.wait_ge(t_p, n + 1)
            act.activation(xT[0:k, 0:4 * P].rearrange("p (q e) -> p q e", q=4)[:, :, 0:NP],
                           p_ohT[0][0:k, :].rearrange("p (q e) -> p q e", q=4)[:, :, 0:NP], ACT.Copy)
            act.activation(xT[0:k, 4 * P:4 * P + NP], p_ohT[1][0:k, 0:NP], ACT.Copy).then_inc(t_s, 1)
            act.wait_ge(y_p, n + 1)
            act.activation(dst_(c), p_mT[0][0:NP, 0:CH * m].rearrange("p (q m) -> p q m", m=m),
                           ACT.Copy).then_inc(y_s, 1)

        kh = row_out[:, :].rearrange("p (b c) -> p b c", b=NB)

        with nc.Block() as block:
            @block.sync
            def _(sp):
                with sp.Fori(0, LAYERS) as l:
                    base = l * NG
                    sp.wait_ge(n_h, l + 1)
                    for k, a in enumerate((gq, gk, bq, bk, go, bo)):
                        sp.dma_start(gains[:, k * H:(k + 1) * H], a[ds(l, 1), :].to_broadcast([NP, H])).then_inc(w_in, 16)
                    sp.dma_start(wqk[:, 0:H], Wq[ds(l, 1), :, :].rearrange("a p c -> p (a c)")).then_inc(w_in, 16)
                    sp.dma_start(wqk[:, H:2 * H], Wk[ds(l, 1), :, :].rearrange("a p c -> p (a c)")).then_inc(w_in, 16)
                    sp.dma_start(wm[:, :], Wm[ds(l, 1), :, :].rearrange("a p c -> p (a c)")).then_inc(w_in, 16)
                    sp.dma_start(wub[:, :], Wu[ds(l, 1), H:2 * H, :].rearrange("a p c -> p (a c)")).then_inc(w_in, 16)
                    sp.dma_start(wu[0:H, :], Wu[ds(l, 1), 0:H, :].rearrange("a p c -> p (a c)")).then_inc(w_in, 16)
                    sp.wait_ge(wmu_s, l + 1)
                    sp.dma_start(wu[H:2 * H, :], wmu[:, :]).then_inc(wmu_in, 16)
                    sp.wait_ge(n_tab, l + 1)
                    sp.dma_start(kh_d.rearrange("(p b) c -> p (b c)", b=NB), row_out[:, :]).then_inc(n_out, 16)
                    sp.dma_start(own_d.rearrange("b p c -> p b c"), own_out[:, :, :]).then_inc(n_out, 16)
                    sp.wait_ge(n_out, l * 32 + 32)
                    sp.sem_inc(held, 1)
                    run_steps(sp, lambda i, u: load_group(sp, i, u, base, own_d, QW, l_rec, l_mask), NG)
                    sums_of_blocks(sp, 0, base, l_sums, l_store, NG)
                sp.wait_ge(l_sums, 16 * NB * LAYERS)

            @block.gpsimd
            def _(pool):
                with pool.Fori(0, LAYERS) as l:
                    base = l * NG
                    pool.wait_ge(n_out, l * 32 + 32)

                    def body(i, u):
                        pool.wait_ge(l_rec[u], 8 * (base + i - u) + 32)
                        if at_least(i, U):
                            pool.wait_ge(l_vals, base + i - U + 1)
                        pool.sem_inc(held, 1)
                        gather_rows(pool, kh_d[:, :], u, KW, l_row)
                    run_steps(pool, body, NG)

            @block.vector
            def _(v):
                v.memset(own_out[:, :, H:QW], 1.0)
                v.memset(kh[:, :, 2 * H + 1:KW], 1.0)
                v.tensor_copy(kh[:, :, H:H + 1], logm[:, :].unsqueeze(2))
                v.drain().then_inc(n_h, 1)
                with v.Fori(0, LAYERS) as l:
                    base = l * NG
                    v.wait_ge(y_s, l * 2 * NC_ + NC_)
                    v.wait_ge(w_in, l * 176 + 176)
                    qk_in = big_a[:, :, :].rearrange("p b (a c) -> p (b a) c", a=2)
                    qk_out = big_b[:, :, :].rearrange("p b (a c) -> p (b a) c", a=2)
                    shape = [NP, 2 * NB, H]
                    layer_norm_in_place(v, qk_in, qk_out, shape, n_var, n_std, 2 * l + 1)
                    v.tensor_tensor(big_a[:, :, :], big_a[:, :, :], bc(gains[:, 0:2 * H].unsqueeze(1), [NP, NB, 2 * H]), ALU.mult)
                    v.drain()
                    v.tensor_tensor(own_out[:, :, 0:H], big_a[:, :, 0:H], bc(gains[:, 2 * H:3 * H].unsqueeze(1), [NP, NB, H]), ALU.add)
                    v.tensor_tensor(kh[:, :, 0:H], big_a[:, :, H:2 * H], bc(gains[:, 3 * H:4 * H].unsqueeze(1), [NP, NB, H]), ALU.add)
                    v.tensor_copy(kh[:, :, H + 1:2 * H + 1], HA[:, :, 0:H])
                    v.drain().then_inc(n_tab, 1)

                    def hots(i, u):
                        v.wait_ge(l_rec[u], 8 * (base + i - u) + 32)
                        one_hot(v, i, u, base, C_SRC, l_hot, None, rec)

                    def scores(i, u):
                        s = u % 2
                        v.wait_ge(l_row[u], 16 * (base + i - u) + 64)
                        v.scalar_tensor_tensor(out=row[u][:, :, 0:RBF], in0=rec[u][:, :, 0:RBF], scalar=0.1,
                                               in1=row[u][:, :, 0:RBF], op0=ALU.mult, op1=ALU.add)
                        v.drain()
                        v.wait_ge(l_own, base + i + 1)
                        v.tensor_tensor(prod[s][:, :, :], row[u][:, :, 0:QW],
                                        p_own[:, 0:J * QW].rearrange("p (j c) -> p j c", j=J), ALU.mult)
                        v.drain()
                        v.tensor_reduce(score[u][:, :], prod[s][:, :, :], AX.X, ALU.add)
                        v.drain()
                        v.wait_ge(l_neg, base + i + 1)
                        v.tensor_tensor(masked[s][:, :, :], neg[s][:, :, :],
                                        bc(score[u][:, :].unsqueeze(2), [P, J, NP]), ALU.add).then_inc(l_mask, 1)

                    def maxima(i, u):
                        v.wait_ge(l_mT, base + i + 1)
                        v.tensor_reduce(gmax[:, :], p_mT[u % 2][0:NP, :], AX.X, ALU.max)
                        v.drain()
                        old, pen = smax[(u - 1) % U], fresh[0:NP, ds(i, 1)]
                        v.scalar_tensor_tensor(out=smax[u][:, :], in0=old[:, :], scalar=pen, in1=gmax[:, :],
                                               op0=ALU.add, op1=ALU.max)
                        v.drain()
                        v.scalar_tensor_tensor(out=arg[u][0:NP, J:J + 1], in0=old[:, :], scalar=pen,
                                               in1=smax[u][:, :], op0=ALU.add, op1=ALU.subtract).then_inc(l_max, 1)

                    def shifted(i, u):
                        v.wait_ge(l_mg, base + i + 1)
                        v.tensor_tensor(arg[u][:, 0:J], score[u][:, :], p_mg[:, 0:J], ALU.subtract)
                        v.drain()
                        v.tensor_scalar(arg[u][:, 0:J], arg[u][:, 0:J], 20.0, None, ALU.min).then_inc(l_arg, 1)

                    def weigh(i, u):
                        v.wait_ge(l_es, base + i + 1)
                        v.tensor_tensor(vals[u % 2][:, :, :], row[u][:, :, H + 1:KW],
                                        bc(es[u][:, 0:J].unsqueeze(2), [P, J, VW]), ALU.mult).then_inc(l_vals, 1)

                    def sums(i, u):
                        v.wait_ge(l_agg, base + i + 1)
                        if at_least(i, U):
                            v.wait_ge(l_store[u], 4 * (base + i - u))
                        v.scalar_tensor_tensor(out=acc[u][:, :], in0=acc[(u - 1) % U][:, :],
                                               scalar=es[u][0:NP, J:J + 1], in1=p_agg[0:NP, 0:VW],
                                               op0=ALU.mult, op1=ALU.add).then_inc(l_acc, 1)

                    def body(i, u):
                        w = (u - 1) % U
                        if at_least(i, 1):
                            shifted(i - 1, w)
                        scores(i, u)
                        if at_least(i, 1):
                            weigh(i - 1, w)
                        if before(i + 1, NG):
                            hots(i + 1, (u + 1) % U)
                        maxima(i, u)
                        if at_least(i, 1):
                            sums(i - 1, w)
                    hots(0, 0)
                    run_steps(v, body, NG)
                    w = (NG - 1) % U
                    shifted(NG - 1, w)
                    weigh(NG - 1, w)
                    sums(NG - 1, w)
                    v.wait_ge(l_sums, l * 16 * NB + 16 * NB)
                    v.tensor_scalar(stat[:, 0, 0:NB], agg_in[:, :, H], 1.0e-10, None, ALU.add)
                    v.drain()
                    v.reciprocal(stat[:, 0, 0:NB], stat[:, 0, 0:NB])
                    v.drain()
                    v.tensor_tensor(HA[:, :, H:2 * H], agg_in[:, :, 0:H],
                                    bc(stat[:, 0, 0:NB].unsqueeze(2), [NP, NB, H]), ALU.mult).then_inc(a_agg, 1)
                    v.wait_ge(y_s, l * 2 * NC_ + 2 * NC_)
                    zz, t1 = big_a[:, :, 0:H], big_b[:, :, 0:H]
                    v.scalar_tensor_tensor(out=t1, in0=zz, scalar=0.01, in1=zz, op0=ALU.mult, op1=ALU.max)
                    v.drain()
                    v.tensor_tensor(zz, t1, HA[:, :, 0:H], ALU.add)
                    v.drain()
                    layer_norm_in_place(v, zz, t1, [NP, NB, H], n_var, n_std, 2 * l + 2)
                    v.tensor_tensor(zz, zz, bc(gains[:, 4 * H:5 * H].unsqueeze(1), [NP, NB, H]), ALU.mult)
                    v.drain()
                    v.tensor_tensor(HA[:, :, 0:H], zz, bc(gains[:, 5 * H:6 * H].unsqueeze(1), [NP, NB, H]), ALU.add)
                    v.drain().then_inc(n_h, 1)

            @block.scalar
            def _(act):
                with act.Fori(0, LAYERS) as l:
                    base = l * NG
                    act.wait_ge(wmT_p, l + 1)
                    act.activation(wmT[:, :], p_x[0:H, 0:H], ACT.Copy).then_inc(wmT_s, 1)
                    act.wait_ge(wmu_p, l + 1)
                    act.activation(wmu[:, :], p_x[0:H, 128:128 + H], ACT.Copy).then_inc(wmu_s, 1)
                    for c in range(NC_):
                        dense_act(act, c, l * 2 * NC_ + c, H, 2 * H, lambda c: big_a[:, c * CH:(c + 1) * CH, :])
                    deviation(act, 2 * NB, n_var, n_std, 2 * l + 1)

                    def turned(i, u):
                        s = u % 2
                        act.wait_ge(l_hot, base + i + 1)
                        if at_least(i, 2):
                            act.wait_ge(l_mask, base + i - 1)
                        act.activation(neg[s][:, :, :], oh[u][:, :, :], ACT.Copy, scale=BIG,
                                       bias=-BIG).then_inc(l_neg, 1)
                        act.wait_ge(l_flip_p, base + i + 1)
                        if at_least(i, 2):
                            act.wait_ge(l_mg, base + i - 1)
                        act.activation(ohT[s][:, :], p_ohT[s][0:NP, :], ACT.Copy).then_inc(l_flip, 1)

                    def exps(i, u):
                        act.wait_ge(l_arg, base + i + 1)
                        act.activation(es[u][:, :], arg[u][:, :], ACT.Exp).then_inc(l_es, 1)

                    def store(i, u):
                        act.wait_ge(l_acc, base + i + 1)
                        act.dma_start(acc_d[ds(i, 1), :, :].rearrange("a p c -> p (a c)"), acc[u][:, :]).then_inc(l_store[u], 16)

                    def body(i, u):
                        if at_least(i, 1):
                            exps(i - 1, (u - 1) % U)
                        if before(i + 1, NG):
                            turned(i + 1, (u + 1) % U)
                        if at_least(i, 2):
                            store(i - 2, (u - 2) % U)
                    turned(0, 0)
                    run_steps(act, body, NG)
                    exps(NG - 1, (NG - 1) % U)
                    for i in (NG - 2, NG - 1):
                        store(i, i % U)
                    for c in range(NC_):
                        dense_act(act, c, l * 2 * NC_ + NC_ + c, 2 * H, H, lambda c: big_a[:, c * CH:(c + 1) * CH, 0:H])
                    deviation(act, NB, n_var, n_std, 2 * l + 2)

            @block.tensor
            def _(pe):
                with pe.Fori(0, LAYERS) as l:
                    base = l * NG
                    pe.wait_ge(w_in, l * 176 + 176)
                    pe.sem_inc(held, 1)
                    pe.transpose(p_x[0:H, 0:H], wm[:, :], ident[0:H, 0:H]).then_inc(wmT_p, 1)
                    pe.wait_ge(wmT_s, l + 1)
                    pe.sem_inc(held, 1)
                    pe.matmul(p_x[0:H, 128:128 + H], wmT[:, :], wub[:, :], start=True, stop=True).then_inc(wmu_p, 1)
                    pe.wait_ge(n_h, l + 1)
                    pe.sem_inc(held, 1)
                    for c in range(NC_):
                        dense_pe(pe, c, l * 2 * NC_ + c, lambda b: HA[:, b, 0:H], H, wqk[:, :], 2 * H, c == 0)

                    def front(i, u):
                        pe.wait_ge(l_hot, base + i + 1)
                        if at_least(i, 2):
                            pe.wait_ge(l_flip, base + i - 1)
                        flip_one_hot(pe, u, l_flip_p)

                    def queries(i, u):
                        pe.wait_ge(l_rec[u], 8 * (base + i - u) + 32)
                        pe.wait_ge(l_flip, base + i + 1)
                        if at_least(i, 1):
                            pe.wait_ge(l_mask, base + i)
                        gather_own(pe, u, p_own, QW, l_own)

                    def flip_masked(i, u):
                        pe.wait_ge(l_mask, base + i + 1)
                        if at_least(i, 2):
                            pe.wait_ge(l_max, base + i - 1)
                        for j in range(J):
                            mm = pe.transpose(p_mT[u % 2][0:NP, j * P:(j + 1) * P], masked[u % 2][:, j, :], ident[:, :])
                        mm.then_inc(l_mT, 1)

                    def gather_max(i, u):
                        pe.wait_ge(l_max, base + i + 1)
                        if at_least(i, 1):
                            pe.wait_ge(l_arg, base + i)
                        for j in range(J):
                            mm = pe.matmul(p_mg[:, j:j + 1], ohT[u % 2][:, j * P:(j + 1) * P], smax[u][:, :],
                                           start=True, stop=True)
                        mm.then_inc(l_mg, 1)

                    def sums(i, u):
                        pe.wait_ge(l_vals, base + i + 1)
                        if at_least(i, 1):
                            pe.wait_ge(l_acc, base + i)
                        sum_group(pe, u, p_agg, vals[u % 2], l_agg)

                    def body(i, u):
                        flip_masked(i, u)
                        if at_least(i, 1):
                            sums(i - 1, (u - 1) % U)
                        if before(i + 1, NG):
                            front(i + 1, (u + 1) % U)
                        gather_max(i, u)
                        if before(i + 1, NG):
                            queries(i + 1, (u + 1) % U)
                    pe.wait_ge(n_std, 2 * l + 1)
                    front(0, 0)
                    queries(0, 0)
                    run_steps(pe, body, NG)
                    sums(NG - 1, (NG - 1) % U)
                    pe.wait_ge(wmu_in, l * 16 + 16)
                    pe.wait_ge(a_agg, l + 1)
                    pe.sem_inc(held, 1)
                    for c in range(NC_):
                        dense_pe(pe, c, l * 2 * NC_ + NC_ + c, lambda b: HA[:, b, :], 2 * H, wu[:, :], H, c == 0)
                    pe.wait_ge(n_std, 2 * l + 2)

        c_h = sem("c_h")
        c_w = sem("c_w")
        c_var = sem("c_var")
        c_std = sem("c_std")
        c_tab = sem("c_tab")
        c_out = sem("c_out")
        DN = 2 * NC_ * LAYERS
        with nc.Block() as block:
            @block.vector
            def _(v):
                v.tensor_tensor(X[:, :, :], X[:, :, :], HA[:, :, 0:H], ALU.add)
                v.drain()
                layer_norm(v, big_a[:, :, 0:H], X[:, :, :], [NP, NB, H], c_var, c_std, 1, tmp=big_b[:, :, 0:H])
                v.tensor_scalar(HA[:, :, 0:H], big_a[:, :, 0:H], 0.0, None, ALU.max).then_inc(c_h, 1)
                v.wait_ge(y_s, DN + NC_)
                v.tensor_tensor(HA[:, :, H:2 * H], big_a[:, :, 0:H], bc(dinv[:, :].unsqueeze(2), [NP, NB, H]), ALU.mult)
                v.drain().then_inc(c_tab, 1)

            @block.scalar
            def _(act):
                deviation(act, NB, c_var, c_std, 1)
                for c in range(NC_):
                    dense_act(act, c, DN + c, H, H, lambda c: big_a[:, c * CH:(c + 1) * CH, 0:H])

            @block.tensor
            def _(pe):
                pe.wait_ge(c_w, 16)
                pe.wait_ge(c_h, 1)
                for c in range(NC_):
                    dense_pe(pe, c, DN + c, lambda b: HA[:, b, 0:H], H, wm[:, :], H, c == 0)

            @block.sync
            def _(sp):
                sp.dma_start(wm[:, :], W1).then_inc(c_w, 16)
                sp.wait_ge(c_tab, 1)
                sp.dma_start(own_d[:, :, 0:H].rearrange("b p c -> p b c"), HA[:, :, H:2 * H]).then_inc(c_out, 16)
                sp.wait_ge(c_out, 16)

        m_rec = [sem(f"m_rec{s}") for s in range(U)]
        m_hot = sem("m_hot")
        m_flip_p = sem("m_flip_p")
        m_flip = sem("m_flip")
        m_own = sem("m_own")
        m_msg = sem("m_msg")
        m_sent = [sem(f"m_sent{s}") for s in range(U)]
        with nc.Block() as block:
            @block.sync
            def _(sp):
                def body(i, u):
                    if at_least(i, U):
                        sp.wait_ge(m_sent[u], 16 * (i - u))
                        sp.sem_inc(held, 1)
                    b = sp.value_load(blk_i[0][0:1, ds(i, 1)], min_val=0, max_val=NB - 1)
                    sp.dma_start(rec[u][:, :, :].rearrange("p j c -> p (j c)"),
                                 rec_g[ds(i, 1), :, :, :].rearrange("a p j c -> p (a j c)")).then_inc(m_rec[u], 16)
                    sp.dma_start(own[u][:, 0:H], own_d[ds(b, 1), :, 0:H].rearrange("a p c -> p (a c)")).then_inc(m_rec[u], 16)
                run_steps(sp, body, NG)

            @block.vector
            def _(v):
                def hots(i, u):
                    v.wait_ge(m_rec[u], 8 * (i - u) + 32)
                    one_hot(v, i, u, 0, C_SRC, m_hot, None, rec)

                def body(i, u):
                    if before(i + 1, NG):
                        hots(i + 1, (u + 1) % U)
                    if at_least(i, U):
                        v.wait_ge(m_sent[u], 16 * (i - u))
                    v.tensor_copy(row[u][:, :, H:MW], rec[u][:, :, C_DROW:C_DROW + 1])
                    v.wait_ge(m_own, i + 1)
                    v.sem_inc(held, 1)
                    v.tensor_copy(row[u][:, :, 0:H],
                                  own_bank[u % 2][:, 0:J * H].rearrange("p (j c) -> p j c", j=J)).then_inc(m_msg, 1)
                hots(0, 0)
                run_steps(v, body, NG)

            @block.scalar
            def _(act):
                def body(i, u):
                    act.wait_ge(m_flip_p, i + 1)
                    if at_least(i, 2):
                        act.wait_ge(m_own, i - 1)
                    act.activation(ohT[u % 2][:, :], p_ohT[u % 2][0:NP, :], ACT.Copy).then_inc(m_flip, 1)
                run_steps(act, body, NG)

            @block.tensor
            def _(pe):
                def front(i, u):
                    pe.wait_ge(m_hot, i + 1)
                    if at_least(i, 2):
                        pe.wait_ge(m_flip, i - 1)
                    flip_one_hot(pe, u, m_flip_p)

                def body(i, u):
                    if before(i + 1, NG):
                        front(i + 1, (u + 1) % U)
                    pe.wait_ge(m_flip, i + 1)
                    if at_least(i, 2):
                        pe.wait_ge(m_msg, i - 1)
                    gather_own(pe, u, own_bank[u % 2], H, m_own)
                front(0, 0)
                run_steps(pe, body, NG)

            @block.gpsimd
            def _(pool):
                def body(i, u):
                    pool.wait_ge(m_msg, i + 1)
                    pool.sem_inc(held, 1)
                    for j in range(J):
                        pool.indirect_dma_start(
                            out=msg_d[:, :], out_offset=bass.IndirectOffsetOnAxis(
                                ap=rec[u][:, j, C_POS2:RW].bitcast(I32), axis=0),
                            in_=row[u][:, j, 0:MW], in_offset=None, bounds_check=NG * EG - 1,
                            oob_is_err=False).then_inc(m_sent[u], 16)
                run_steps(pool, body, NG)
                for u in range(U):
                    pool.wait_ge(m_sent[u], 16 * NG)

        d_msg = [sem(f"d_msg{s}") for s in range(U)]
        d_hot = sem("d_hot")
        d_agg = sem("d_agg")
        d_acc = sem("d_acc")
        d_store = [sem(f"d_store{s}") for s in range(U)]
        d_sums = sem("d_sums")
        d_res = sem("d_res")
        d_out = sem("d_out")
        msgt = [row[s][:, :, :].rearrange("p j c -> p (j c)")[:, 0:J * MW].rearrange("p (j c) -> p j c", j=J)
                for s in range(U)]
        with nc.Block() as block:
            @block.sync
            def _(sp):
                def body(i, u):
                    if at_least(i, U):
                        sp.wait_ge(d_agg, i - U + 1)
                    sp.dma_start(msgt[u].rearrange("p j c -> p (j c)"),
                                 msg_g[ds(i, 1), :, :, :].rearrange("a p j c -> p (a j c)")).then_inc(d_msg[u], 16)
                run_steps(sp, body, NG)
                sums_of_blocks(sp, 1, 0, d_sums, d_store, NG)
                sp.wait_ge(d_res, 1)
                sp.dma_start(out.rearrange("(p b) c -> p b c", b=NB), X[:, :, :]).then_inc(d_out, 16)
                sp.wait_ge(d_out, 16)

            @block.vector
            def _(v):
                def hots(i, u):
                    v.wait_ge(d_msg[u], 4 * (i - u) + 16)
                    if at_least(i, U):
                        v.wait_ge(d_agg, i - U + 1)
                    one_hot(v, i, u, 0, H, d_hot, None, msgt)

                def body(i, u):
                    if before(i + 1, NG):
                        hots(i + 1, (u + 1) % U)
                    if at_least(i, 1):
                        v.wait_ge(d_acc, i)
                    v.wait_ge(d_agg, i + 1)
                    if at_least(i, U):
                        v.wait_ge(d_store[u], 4 * (i - u))
                    v.scalar_tensor_tensor(out=acc[u][:, :], in0=acc[(u - 1) % U][:, :],
                                           scalar=keep[1][0:NP, ds(i, 1)], in1=agg_bank[u % 2][0:NP, 0:VW],
                                           op0=ALU.mult, op1=ALU.add).then_inc(d_acc, 1)
                hots(0, 0)
                run_steps(v, body, NG)
                v.wait_ge(d_sums, 16 * NB)
                v.tensor_tensor(big_a[:, :, 0:H], agg_in[:, :, 0:H], HA[:, :, H:2 * H], ALU.add)
                v.drain()
                v.tensor_tensor(big_a[:, :, 0:H], big_a[:, :, 0:H], bc(dinv[:, :].unsqueeze(2), [NP, NB, H]), ALU.mult)
                v.drain()
                v.tensor_tensor(X[:, :, :], X[:, :, :], big_a[:, :, 0:H], ALU.add)
                v.drain()
                v.tensor_tensor(X[:, :, :], X[:, :, :], bc(gains_n[:, 2 * H:3 * H].unsqueeze(1), [NP, NB, H]), ALU.add)
                v.drain().then_inc(d_res, 1)

            @block.scalar
            def _(act):
                def body(i, u):
                    act.wait_ge(d_acc, i + 1)
                    act.dma_start(acc_d[ds(i, 1), :, :].rearrange("a p c -> p (a c)"), acc[u][:, :]).then_inc(d_store[u], 16)
                run_steps(act, body, NG)

            @block.tensor
            def _(pe):
                def body(i, u):
                    pe.wait_ge(d_hot, i + 1)
                    if at_least(i, 2):
                        pe.wait_ge(d_acc, i - 1)
                    sum_group(pe, u, agg_bank[u % 2], msgt[u], d_agg)
                run_steps(pe, body, NG)


_INS = ["x", "src", "dst", "edge_attr_40", "edge_weight", "node_type_119", "node_vec",
        "L0_gnn_Wq", "L0_gnn_gq", "L0_gnn_bq", "L0_gnn_Wk", "L0_gnn_gk", "L0_gnn_bk", "L0_gnn_Wm", "L0_gnn_Wu",
        "L0_gnn_go", "L0_gnn_bo", "L0_gnn_F1W", "L0_gnn_F1b", "L0_gnn_F2W", "L0_gnn_F2b", "L0_gnn_gn",
        "L0_gnn_bn", "L0_gnn_emb", "L0_gnn_adapt", "L1_gnn_W", "L1_gnn_b"]


def kernel(**inputs):
    import numpy as _np
    import concourse.bacc as _bacc
    from concourse import mybir as _mybir
    from concourse.bass_utils import run_bass_kernel_spmd as _run

    nc = _bacc.Bacc("TRN2", target_bir_lowering=False, num_devices=1)
    arrays, args = {}, []
    for name in _INS:
        a = _np.ascontiguousarray(inputs[name])
        arrays[f"in_{name}"] = a
        args.append(nc.dram_tensor(f"in_{name}", a.shape, _mybir.dt.from_np(a.dtype), kind="ExternalInput").ap())
    args.append(nc.dram_tensor("out_0", (N, H), F32, kind="ExternalOutput").ap())
    build(nc, *args)
    r = _run(nc, [arrays], core_ids=[0])
    return r.results[0]["out_0"]
```

```python
from contextlib import ExitStack

import concourse.bass as bass
from concourse import mybir

F32 = mybir.dt.float32
I32 = mybir.dt.int32
BF16 = mybir.dt.bfloat16
ALU = mybir.AluOpType
ACT = mybir.ActivationFunctionType
AX = mybir.AxisListType
ds = bass.ds

N, E, H, RBF, LAYERS, NELEM, EMB = 6250, 200000, 48, 40, 4, 119, 32
NB = 50
NP = N // NB
P = 128
J = 4
EG = P * J
NG = (E + NB * (EG - 1)) // EG
FREE_G = -(-E // EG)
EC = E // NP
U = 8
S = 4
RW = RBF + 5
RG = RW + H
C_SRC, C_CUT, C_DROW, C_DST, C_POS2 = RBF, RBF + 1, RBF + 2, RBF + 3, RBF + 4
PARTS = 3
MW = PARTS * H + 2
VW = H + 1
QW = H + 1
KW = 2 * H + 2
GW = H + EMB + 1
CH = 5
NC_ = NB // CH
BIG = 1.0e30
ROUND = 12582912.0
assert NG % U == 0 and NB * NP == N and EC * NP == E and EC % (U * J) == 0 and NC_ * CH == NB


def after_step(per_step, i, u):
    return per_step // U * (i - u) + per_step


def before_step(per_step, i, u):
    return per_step // U * (i - u)


def run_steps(eng, body, total):
    for i in range(U):
        body(i, i)
    with eng.Fori(U, total - U, U) as t:
        for u in range(U):
            body(t + u, u)
    for i in range(total - U, total):
        body(i, i % U)


def at_least(i, k):
    return not isinstance(i, int) or i >= k


def before(i, total):
    return not isinstance(i, int) or i < total


def build(nc, x, src, dst, ea, weight, z, mult, Wq, gq, bq, Wk, gk, bk, Wm, Wu, go, bo,
          F1W, F1b, F2W, F2b, gn, bn, emb, adapt, W1, b1, out):
    ctx = ExitStack()
    with ctx:
        def sb(name, shape, dt=F32):
            return ctx.enter_context(nc.sbuf_tensor(name, shape, dt))

        def ps(name, shape, dt=F32):
            return ctx.enter_context(nc.psum_tensor(name, shape, dt))

        def sem(name):
            return ctx.enter_context(nc.semaphore(name))

        def dram(name, shape, dt=F32):
            return nc.dram_tensor(name, shape, dt).ap()

        ctx.enter_context(nc.allow_non_contiguous_dma(reason="short rows of records and index columns"))

        rec_d = dram("rec_d", [NG * EG, RG])
        lean_d = dram("lean_d", [NG, P, J * RW])
        msg_d = dram("msg_d", [NG * EG, MW], BF16)
        emb2_d = dram("emb2_d", [NELEM, 2 * EMB])
        gate_d = dram("gate_d", [N, GW])
        kh_d = dram("kh_d", [N, KW])
        own_d = dram("own_d", [NB, NP, PARTS * QW], BF16)
        ei_d = dram("ei_d", [NB, NP, PARTS * EMB], BF16)
        acc_d = dram("acc_d", [NG, NP, VW])
        blk_d = [dram(f"blk_d{k}", [NG]) for k in range(2)]
        rec_g = rec_d.rearrange("(g p j) c -> g p (j c)", p=P, j=J)
        msg_g = msg_d.rearrange("(g p j) c -> g p (j c)", p=P, j=J)

        ident = sb("ident", [P, P])
        ones = sb("ones", [P, P])
        upper = sb("upper", [P, P])
        identb = sb("identb", [P, P], BF16)
        row_iota = sb("row_iota", [P, P], BF16)
        blk_iota = sb("blk_iota", [P, NB])
        grp_iota = sb("grp_iota", [NG // J, J])
        eps = sb("eps", [P, 1])
        half_pi = sb("half_pi", [P, 1])
        X = sb("X", [NP, NB, H])
        HA = sb("HA", [NP, NB, 2 * H])
        big_a = sb("big_a", [NP, NB, 2 * H])
        big_b = sb("big_b", [NP, NB, 2 * H])
        agg_in = sb("agg_in", [NP, NB, VW])
        row_out = sb("row_out", [NP, NB * KW])
        own_out = sb("own_out", [NP, NB, QW])
        stat = sb("stat", [NP, 3, 2 * NB])
        mult_sb = sb("mult_sb", [NP, NB])
        logm = sb("logm", [NP, NB])
        z_sb = sb("z_sb", [NP, NB], I32)
        dinv = sb("dinv", [NP, NB])
        emb_sb = sb("emb_sb", [NELEM, 2 * EMB])
        embT = sb("embT", [EMB, NELEM])
        adapt_sb = sb("adapt_sb", [EMB, EMB])
        F1W_sb = sb("F1W_sb", [RBF, H])
        F1b_sb = sb("F1b_sb", [H, 1])
        F2W_sb = sb("F2W_sb", [H + 1, H])
        wqk = sb("wqk", [H, 2 * H])
        wm = sb("wm", [H, H])
        wmT = sb("wmT", [H, H])
        wub = sb("wub", [H, H])
        wmu = sb("wmu", [H, H])
        wu = sb("wu", [2 * H, H])
        gains = sb("gains", [NP, 6 * H])
        gains_n = sb("gains_n", [NP, 3 * H])
        fill_r = sb("fill_r", [P, J, RG])
        fill_m = sb("fill_m", [P, J, MW], BF16)
        pos1 = sb("pos1", [NP, EC], I32)
        meta_t = sb("meta_t", [P, EC * 3])
        metaf = meta_t[0:NP, :].rearrange("p (t c) -> p t c", c=3)
        metai_t = sb("metai_t", [P, EC * 2], I32)
        metai = metai_t[0:NP, :].rearrange("p (t c) -> p t c", c=2)
        cnt = sb("cnt", [NP, NB])
        first = sb("first", [NP, NB])
        groups = sb("groups", [NP, NB])
        gend = sb("gend", [NP, NB])
        cmp_g = sb("cmp_g", [NG // J, J, NB])
        blk_g = sb("blk_g", [NG // J, J])
        blk_row = sb("blk_row", [P, NG + 1])
        keep = [sb(f"keep{k}", [P, NG]) for k in range(2)]
        fresh = sb("fresh", [P, NG])
        blk_i = [sb(f"blk_i{k}", [1, NG], I32) for k in range(2)]
        last_i = [sb(f"last_i{k}", [1, NB], I32) for k in range(2)]

        rec_t = [sb(f"rec{s}", [P, J * RG]) for s in range(U)]
        rec_w = [t[:, :].rearrange("p (j c) -> p j c", j=J) for t in rec_t]
        rec = [t[:, 0:J * RW].rearrange("p (j c) -> p j c", j=J) for t in rec_t]
        row = [metai_t[:, s * J * KW:(s + 1) * J * KW].bitcast(F32).rearrange("p (j c) -> p j c", j=J)
               for s in range(U)]
        own = [sb(f"own{s}", [NP, PARTS * QW], BF16) for s in range(U)]
        oh = [sb(f"oh{s}", [P, J, P], BF16) for s in range(S)]
        ohf = [meta_t[:, s * J * P:(s + 1) * J * P].rearrange("p (j n) -> p j n", j=J) for s in range(S)]
        xT = [meta_t[0:2 * H, S * J * P + s * CH * P:S * J * P + (s + 1) * CH * P] for s in range(2)]
        ohT = [sb(f"ohT{s}", [P, J * P], BF16) for s in range(S)]
        neg_t = [sb(f"neg{s}", [P, J * P]) for s in range(2)]
        masked_t = [sb(f"masked{s}", [P, J * P]) for s in range(2)]
        prod = [sb(f"prod{s}", [P, J, QW]) for s in range(2)]
        score = [sb(f"score{s}", [P, J]) for s in range(U)]
        smax = [sb(f"smax{s}", [NP, 1]) for s in range(U)]
        gmax = [sb(f"gmax{s}", [NP, 1]) for s in range(2)]
        parts = [sb(f"parts{s}", [NP, PARTS], BF16) for s in range(2)]
        msum = [sb(f"msum{s}", [P, J]) for s in range(2)]
        arg = [sb(f"arg{s}", [P, J + 1]) for s in range(U)]
        es = [sb(f"es{s}", [P, J + 1]) for s in range(U)]
        vals = [sb(f"vals{s}", [P, J, VW]) for s in range(2)]
        acc = [sb(f"acc{s}", [NP, VW]) for s in range(U)]
        idx = [sb(f"idx{s}", [NP, J], I32) for s in range(U)]

        flat_a = big_a[:, :, :].rearrange("p a b -> p (a b)")
        flat_b = big_b[:, :, :].rearrange("p a b -> p (a b)")
        key_i = [agg_in[:, :, :].rearrange("p a b -> p (a b)")[:, 0:EC].bitcast(I32),
                 row_out[:, 0:EC].bitcast(I32)]
        keyf, blk, mask = flat_a[:, 0:EC], flat_a[:, EC:2 * EC], flat_a[:, 2 * EC:3 * EC]
        cum, pos, zero_e = flat_b[:, 0:EC], flat_b[:, EC:2 * EC], flat_b[:, 2 * EC:3 * EC]
        wt = row_out[:, EC:2 * EC]
        cosw = row_out[:, 2 * EC:3 * EC]

        p_t = [ps(f"p_t{s}", [P, J * P]) for s in range(2)]
        p_ohT = [t[:, :].bitcast(BF16)[:, 0:J * P] for t in p_t]
        p_mT = [ps(f"p_mT{s}", [P, J * P]) for s in range(2)]
        p_own = ps("p_own", [P, 512])
        p_mg = ps("p_mg", [P, 512])
        p_agg = ps("p_agg", [P, 512])
        p_x = ps("p_x", [P, 512])
        own_bank = [p_own, p_x]
        agg_bank = [p_agg, p_mg]

        def bc(ap, shape):
            return ap.to_broadcast(shape)

        loaded = sem("loaded")
        consts = sem("consts")
        fills = sem("fills")
        filled = sem("filled")
        filled_last = sem("filled_last")
        held = sem("held")
        fill_of = [(rec_g, fill_r), (msg_g, fill_m)]
        ready_emb = sem("ready_emb")
        counted = sem("counted")
        summed = sem("summed")
        taken = sem("taken")
        blk_made = sem("blk_made")
        blk_out = sem("blk_out")
        blk_in = sem("blk_in")
        cos_in = sem("cos_in")
        cos_out = sem("cos_out")
        small = sem("small")
        embT_p = sem("embT_p")
        embT_s = sem("embT_s")
        emb_p = sem("emb_p")
        emb_s = sem("emb_s")
        emb_out = sem("emb_out")
        var1 = sem("var1")
        std1 = sem("std1")

        def layer_norm(eng, dst_, src_, shape, var_sem, std_sem, v, tmp=None):
            n = shape[1]
            mean, var, rstd = stat[:, 0, 0:n], stat[:, 1, 0:n], stat[:, 2, 0:n]
            eng.tensor_reduce(mean, src_, AX.X, ALU.add)
            eng.drain()
            eng.tensor_scalar(mean, mean, 1.0 / H, None, ALU.mult)
            eng.drain()
            eng.tensor_tensor(dst_, src_, bc(mean.unsqueeze(2), shape), ALU.subtract)
            eng.drain()
            eng.tensor_tensor(tmp, dst_, dst_, ALU.mult)
            eng.drain()
            eng.tensor_reduce(var, tmp, AX.X, ALU.add).then_inc(var_sem, 1)
            eng.wait_ge(std_sem, v)
            eng.reciprocal(rstd, rstd)
            eng.drain()
            eng.tensor_tensor(dst_, dst_, bc(rstd.unsqueeze(2), shape), ALU.mult)
            eng.drain()

        def layer_norm_in_place(eng, y, tmp, shape, var_sem, std_sem, v):
            layer_norm(eng, y, y, shape, var_sem, std_sem, v, tmp=tmp)

        def deviation(eng, n, var_sem, std_sem, v):
            eng.wait_ge(var_sem, v)
            eng.activation(stat[:, 2, 0:n], stat[:, 1, 0:n], ACT.Sqrt, bias=eps[0:NP, 0:1],
                           scale=1.0 / H).then_inc(std_sem, 1)

        def own3(w):
            return big_b[:, :, :].rearrange("p a b -> p (a b)").bitcast(BF16)[:, 0:NB * PARTS * w]\
                .rearrange("p (b k c) -> p b k c", b=NB, k=PARTS)

        def split3(v, src_, out3, rest):
            v.tensor_copy(out3[:, :, 0, :], src_)
            v.drain()
            v.tensor_tensor(rest, src_, out3[:, :, 0, :], ALU.subtract)
            v.drain()
            v.tensor_copy(out3[:, :, 1, :], rest)
            v.drain()
            v.tensor_tensor(out3[:, :, 2, :], rest, out3[:, :, 1, :], ALU.subtract)
            v.drain()

        with nc.Block() as block:
            @block.sync
            def _(sp):
                sp.dma_start(key_i[0], src.rearrange("(p t) -> p t", p=NP)).then_inc(loaded, 16)
                sp.dma_start(key_i[1], dst.rearrange("(p t) -> p t", p=NP)).then_inc(loaded, 16)
                sp.dma_start(wt, weight.rearrange("(p t) -> p t", p=NP)).then_inc(loaded, 16)
                sp.dma_start(X[:, :, :], x.rearrange("(p b) c -> p b c", b=NB)).then_inc(loaded, 16)
                sp.dma_start(mult_sb[:, :], mult.rearrange("(p b) -> p b", b=NB)).then_inc(loaded, 16)
                sp.dma_start(z_sb[:, :], z.rearrange("(p b) -> p b", b=NB)).then_inc(loaded, 16)
                sp.dma_start(emb_sb[:, 0:EMB], emb).then_inc(loaded, 16)
                sp.dma_start(adapt_sb[:, :], adapt).then_inc(loaded, 16)
                sp.dma_start(F1W_sb[:, :], F1W).then_inc(loaded, 16)
                sp.dma_start(F1b_sb[:, :], F1b.rearrange("(p a) -> p a", a=1)).then_inc(loaded, 16)
                sp.dma_start(F2W_sb[0:H, :], F2W).then_inc(loaded, 16)
                sp.dma_start(F2W_sb[H:H + 1, :], F2b.rearrange("(a p) -> a p", a=1)).then_inc(loaded, 16)
                for k, v in enumerate((gn, bn, b1)):
                    sp.dma_start(gains_n[:, k * H:(k + 1) * H],
                                 v.rearrange("(a p) -> a p", a=1).to_broadcast([NP, H])).then_inc(loaded, 16)
                sp.wait_ge(fills, 1)
                for table, fill in fill_of:
                    sp.dma_start(table[FREE_G:NG, :, :].rearrange("g p c -> p g c"),
                                 fill[:, :, :].rearrange("p j c -> p (j c)").unsqueeze(1)
                                 .to_broadcast([P, NG - FREE_G, J * fill.shape[2]])).then_inc(filled, 16)
                sp.wait_ge(emb_s, 1)
                sp.dma_start(emb2_d, emb_sb[:, :]).then_inc(emb_out, 16)
                sp.wait_ge(emb_out, 16)
                for k in range(2):
                    sp.wait_ge(blk_made, k + 1)
                    sp.dma_start(blk_d[k].rearrange("(p j) -> p j", j=J), blk_g[:, :]).then_inc(blk_out, 16)
                    sp.wait_ge(blk_out, 16 * (k + 1))
                    sp.dma_start(blk_row[:, 1:NG + 1], blk_d[k].rearrange("(a n) -> a n", a=1)
                                 .to_broadcast([P, NG])).then_inc(blk_in, 16)
                    table, fill = fill_of[k]
                    sp.wait_ge(filled, 32)
                    sp.sem_inc(held, 1)
                    with sp.Fori(0, NB) as b:
                        g = sp.value_load(last_i[k][0:1, ds(b, 1)], min_val=0, max_val=NG - 1)
                        sp.dma_start(table[ds(g, 1), :, :].rearrange("a p c -> p (a c)"),
                                     fill[:, :, :].rearrange("p j c -> p (j c)")).then_inc(filled_last, 16)
                sp.wait_ge(filled_last, 2 * NB * 16)

            @block.gpsimd
            def _(pool):
                pool.memset(ident[:, :], 0.0).then_inc(consts, 1)
                pool.memset(ones[:, :], 1.0).then_inc(consts, 1)
                pool.iota(row_iota[:, :], pattern=[[1, P]], base=0, channel_multiplier=0,
                          allow_small_or_imprecise_dtypes=True).then_inc(consts, 1)
                pool.iota(blk_iota[:, :], pattern=[[1, NB]], base=0, channel_multiplier=0,
                          allow_small_or_imprecise_dtypes=True).then_inc(consts, 1)
                pool.iota(grp_iota[:, :], pattern=[[1, J]], base=0, channel_multiplier=J,
                          allow_small_or_imprecise_dtypes=True).then_inc(consts, 1)
                pool.wait_ge(consts, 5)
                pool.affine_select(out=ident[:, :], in_=ident[:, :], compare_op=ALU.not_equal, fill=1.0,
                                   base=0, pattern=[[-1, P]], channel_multiplier=1).then_inc(consts, 1)
                pool.affine_select(out=upper[:, :], in_=ones[:, :], compare_op=ALU.is_gt, fill=0.0,
                                   base=0, pattern=[[1, P]], channel_multiplier=-1).then_inc(consts, 1)
                pool.wait_ge(loaded, 16 * 15)
                pool.wait_ge(emb_out, 16)
                for b in range(NB):
                    pool.indirect_dma_start(
                        out=HA[:, b, 0:2 * EMB], out_offset=None, in_=emb2_d[:, :],
                        in_offset=bass.IndirectOffsetOnAxis(ap=z_sb[:, b:b + 1], axis=0)
                    ).then_inc(ready_emb, 16)
                pool.wait_ge(ready_emb, 16 * NB)

            @block.tensor
            def _(pe):
                pe.wait_ge(consts, 7)
                pe.wait_ge(loaded, 16 * 15)
                pe.transpose(p_x[0:EMB, 0:NELEM], emb_sb[:, 0:EMB], ident[0:NELEM, 0:NELEM]).then_inc(embT_p, 1)
                pe.wait_ge(embT_s, 1)
                pe.matmul(p_x[0:NELEM, 256:256 + EMB], embT[:, :], adapt_sb[:, :],
                          start=True, stop=True).then_inc(emb_p, 1)
                for k in range(2):
                    pe.wait_ge(counted, k + 1)
                    if k:
                        pe.wait_ge(taken, k)
                    pe.matmul(p_own[0:NP, 0:NB], upper[0:NP, 0:NP], cnt[:, :], start=True, stop=True)
                    pe.matmul(p_own[0:NP, 256:256 + NB], ones[0:NP, 0:NP], cnt[:, :], start=True,
                              stop=True).then_inc(summed, 1)

            @block.scalar
            def _(act):
                act.wait_ge(embT_p, 1)
                act.activation(embT[:, :], p_x[0:EMB, 0:NELEM], ACT.Copy).then_inc(embT_s, 1)
                act.wait_ge(emb_p, 1)
                act.activation(emb_sb[:, EMB:2 * EMB], p_x[0:NELEM, 256:256 + EMB], ACT.Copy).then_inc(emb_s, 1)
                act.wait_ge(cos_in, 1)
                act.activation(cosw, cosw, ACT.Sin, bias=half_pi[0:NP, 0:1],
                               scale=-3.141592653589793 / 6.0).then_inc(cos_out, 1)
                deviation(act, NB, var1, std1, 1)

            @block.vector
            def _(v):
                v.memset(fill_r[:, :, 0:C_SRC], 0.0)
                v.memset(fill_r[:, :, C_SRC:C_SRC + 1], -1.0)
                v.memset(fill_r[:, :, C_CUT:C_DST + 1], 0.0)
                v.memset(fill_r[:, :, RW:RG], 0.0)
                v.memset(fill_r[:, :, C_POS2:RW].bitcast(I32), 2 * NG * EG)
                v.memset(fill_m[:, :, 0:PARTS * H], 0.0)
                v.memset(fill_m[:, :, PARTS * H:MW], -1.0).then_inc(fills, 1)
                v.memset(zero_e, 0.0)
                v.memset(eps[:, :], 1.0e-5)
                for s in range(2):
                    v.memset(neg_t[s][:, :], 1.0)
                v.memset(half_pi[:, :], 3.141592653589793 / 2.0)
                for s in range(U):
                    v.memset(arg[s][:, :], 0.0)
                    v.memset(smax[s][:, :], -BIG)
                    v.memset(acc[s][:, :], 0.0)
                v.memset(blk_row[:, 0:1], -1.0)
                v.wait_ge(consts, 7)
                v.wait_ge(loaded, 16 * 15)
                v.scalar_tensor_tensor(out=cosw, in0=wt, scalar=-1.0, in1=wt, op0=ALU.mult, op1=ALU.max)
                v.drain()
                v.tensor_scalar(cosw, cosw, 6.0, None, ALU.min).then_inc(cos_in, 1)
                for k in range(2):
                    v.tensor_copy(keyf, key_i[k])
                    v.drain()
                    v.tensor_scalar(mask, keyf, 1.0 / NB, 0.5 / NB - 0.5, ALU.mult, ALU.add)
                    v.drain()
                    where = metaf[:, :, 0] if k == 0 else metaf[:, :, 2]
                    v.tensor_scalar(where, mask, ROUND, ROUND, ALU.add, ALU.subtract)
                    v.drain()
                    v.scalar_tensor_tensor(out=blk, in0=where, scalar=-float(NB), in1=keyf,
                                           op0=ALU.mult, op1=ALU.add)
                    v.drain()
                    for b in range(NB):
                        v.tensor_scalar(mask, blk, float(b), 0.0, ALU.is_equal, ALU.add,
                                        accum_out=cnt[:, b:b + 1])
                        v.drain()
                    v.drain().then_inc(counted, 1)
                    v.wait_ge(summed, k + 1)
                    v.tensor_scalar(groups[:, :], p_own[0:NP, 256:256 + NB], 1.0 / EG, 0.5 - 0.5 / EG,
                                    ALU.mult, ALU.add)
                    v.drain()
                    v.tensor_scalar(groups[:, :], groups[:, :], ROUND, ROUND, ALU.add, ALU.subtract)
                    v.drain()
                    v.tensor_scalar(groups[:, :], groups[:, :], 1.0, None, ALU.max)
                    v.drain()
                    v.tensor_tensor_scan(gend[:, :], groups[:, :], zero_e[:, 0:NB], 0.0, ALU.add, ALU.add)
                    v.drain()
                    v.tensor_tensor(first[:, :], gend[:, :], groups[:, :], ALU.subtract)
                    v.drain()
                    v.tensor_scalar(first[:, :], first[:, :], float(EG), -1.0, ALU.mult, ALU.add)
                    v.drain()
                    v.tensor_tensor(first[:, :], first[:, :], p_own[0:NP, 0:NB], ALU.add).then_inc(taken, 1)
                    v.tensor_scalar(last_i[k][:, :], gend[0:1, :], -1.0, None, ALU.add)
                    v.tensor_tensor(cmp_g[:, :, :], bc(gend[0:NG // J, :].unsqueeze(1), [NG // J, J, NB]),
                                    bc(grp_iota[:, :].unsqueeze(2), [NG // J, J, NB]), ALU.is_le)
                    v.drain()
                    if k:
                        v.wait_ge(blk_out, 16)
                    v.tensor_reduce(blk_g[:, :], cmp_g[:, :, :], AX.X, ALU.add)
                    v.drain()
                    v.tensor_scalar(blk_g[:, :], blk_g[:, :], float(NB - 1), None, ALU.min).then_inc(blk_made, 1)
                    for b in range(NB):
                        v.tensor_scalar(mask, blk, float(b), None, ALU.is_equal)
                        v.drain()
                        v.tensor_tensor_scan(cum, mask, zero_e, first[:, b:b + 1], ALU.add, ALU.add)
                        v.drain()
                        v.copy_predicated(pos, mask.bitcast(I32), cum)
                        v.drain()
                    if k == 0:
                        v.tensor_copy(pos1[:, :], pos)
                    else:
                        v.tensor_copy(metai[:, :, 1], pos)
                    v.wait_ge(blk_in, 16 * (k + 1))
                    v.tensor_copy(blk_i[k][:, :], blk_row[0:1, 1:NG + 1])
                    v.tensor_tensor(keep[k][:, :], blk_row[:, 1:NG + 1], blk_row[:, 0:NG], ALU.is_equal)
                    v.drain()
                v.tensor_scalar(fresh[:, :], keep[0][:, :], -1.0, 2.0 * BIG, ALU.add, ALU.mult)
                v.tensor_copy(metai[:, :, 0], key_i[1])
                v.wait_ge(cos_out, 1)
                v.tensor_scalar(metaf[:, :, 1], cosw, 1.0, 0.5, ALU.add, ALU.mult)
                v.drain()
                layer_norm(v, big_a[:, :, 0:H], X[:, :, :], [NP, NB, H], var1, std1, 1, tmp=big_b[:, :, 0:H])
                g_rows = row_out[:, 0:NB * GW].rearrange("p (b c) -> p b c", b=NB)
                v.tensor_scalar(g_rows[:, :, 0:H], big_a[:, :, 0:H], 0.0, None, ALU.max)
                v.wait_ge(ready_emb, 16 * NB)
                v.tensor_copy(g_rows[:, :, H:H + EMB], HA[:, :, EMB:2 * EMB])
                v.tensor_copy(g_rows[:, :, H + EMB:GW], mult_sb[:, :].unsqueeze(2))
                v.tensor_copy(identb[:, :], ident[:, :])
                split3(v, HA[:, :, 0:EMB], own3(EMB), big_a[:, :, 0:EMB])
                v.tensor_copy(HA[:, :, 0:H], g_rows[:, :, 0:H])
                v.drain()

        tabs_out = sem("tabs_out")
        slot_in = [sem(f"slot_in{s}") for s in range(U)]
        meta_in = sem("meta_in")
        sent = [sem(f"sent{s}") for s in range(U)]
        hot = sem("hot")
        hist = sem("hist")
        hist_n = sem("hist_n")
        hot_r = [oh[s][:, :, :] for s in range(2)]
        hot_b = [ohT[s][:, 0:J * NB].rearrange("p (a b) -> p a b", a=J) for s in range(2)]
        s_eaT_p = sem("s_eaT_p")
        s_eaT = sem("s_eaT")
        s_f1 = sem("s_f1")
        s_silu = sem("s_silu")
        s_gate_p = sem("s_gate_p")
        s_gate = sem("s_gate")
        ea_p = ea.rearrange("(p t) c -> p t c", p=NP)
        eaT = [masked_t[s][0:RBF, 0:J * NP] for s in range(2)]
        silu = [neg_t[s][:, 0:J * NP] for s in range(2)]
        gate_bank = [p_own, p_mg]
        STEPS = EC // J

        with nc.Block() as block:
            @block.sync
            def _(sp):
                sp.dma_start(gate_d.rearrange("(p b) c -> p (b c)", b=NB), row_out[:, 0:NB * GW]).then_inc(tabs_out, 16)
                sp.dma_start(ei_d.rearrange("b p c -> p b c"),
                             own3(EMB).rearrange("p b k c -> p b (k c)")).then_inc(tabs_out, 16)

                def body(i, u):
                    if at_least(i, U):
                        sp.wait_ge(sent[u], before_step(64, i, u))
                    sp.dma_start(rec_w[u][0:NP, :, 0:RBF], ea_p[:, ds(i * J, J), :]).then_inc(slot_in[u], 16)
                run_steps(sp, body, STEPS)
                sp.wait_ge(tabs_out, 32)

            @block.vector
            def _(v):
                def body(i, u):
                    if at_least(i, U):
                        v.wait_ge(sent[u], before_step(64, i, u))
                        v.sem_inc(held, 1)
                    v.tensor_copy(rec_w[u][0:NP, :, C_DST:RW].bitcast(I32), metai[:, ds(i * J, J), :])
                    v.tensor_copy(rec_w[u][0:NP, :, C_SRC:C_DST], metaf[:, ds(i * J, J), :])
                    v.tensor_copy(idx[u][:, :], pos1[:, ds(i * J, J)]).then_inc(meta_in, 1)
                    if at_least(i, 2):
                        v.wait_ge(hist, i - 1)
                    v.tensor_tensor(hot_r[u % 2][0:NP], bc(row_iota[0:NP, :].unsqueeze(1), [NP, J, P]),
                                    bc(metaf[:, ds(i * J, J), 2:3], [NP, J, P]), ALU.is_equal)
                    v.scalar_tensor_tensor(out=score[u][0:NP, :].unsqueeze(2), in0=metaf[:, ds(i * J, J), 2:3],
                                           scalar=-float(NB), in1=metai[:, ds(i * J, J), 0:1],
                                           op0=ALU.mult, op1=ALU.add)
                    v.drain()
                    v.tensor_tensor(hot_b[u % 2][0:NP], bc(blk_iota[0:NP, :].unsqueeze(1), [NP, J, NB]),
                                    bc(score[u][0:NP, :].unsqueeze(2), [NP, J, NB]), ALU.is_equal).then_inc(hot, 1)
                    v.wait_ge(s_gate_p, i + 1)
                    v.tensor_copy(rec_w[u][0:NP, :, RW:RG], gate_bank[u % 2][0:NP, 0:J * H]
                                  .rearrange("p (j c) -> p j c", j=J)).then_inc(s_gate, 1)
                run_steps(v, body, STEPS)
                v.wait_ge(hist, STEPS)
                v.tensor_scalar(dinv[:, :], p_x[0:NP, 0:NB], 1.0, None, ALU.add)
                v.drain().then_inc(hist_n, 1)
                v.wait_ge(hist_n, 2)
                v.reciprocal(dinv[:, :], dinv[:, :])
                v.drain()

            @block.scalar
            def _(act):
                def body(i, u):
                    s = u % 2
                    act.wait_ge(s_eaT_p, i + 1)
                    if at_least(i, 2):
                        act.wait_ge(s_f1, i - 1)
                    act.activation(eaT[s].rearrange("p (j e) -> p j e", j=J),
                                   p_mT[0][0:RBF, :].rearrange("p (j e) -> p j e", j=J)[:, :, 0:NP],
                                   ACT.Copy).then_inc(s_eaT, 1)
                    act.wait_ge(s_f1, i + 1)
                    if at_least(i, 2):
                        act.wait_ge(s_gate_p, i - 1)
                    act.activation(silu[s][0:H, :], p_mT[1][0:H, 0:J * NP], ACT.Silu,
                                   bias=F1b_sb[:, 0:1]).then_inc(s_silu, 1)
                run_steps(act, body, STEPS)
                act.wait_ge(hist_n, 1)
                act.activation(dinv[:, :], dinv[:, :], ACT.Sqrt)
                act.drain()
                act.activation(logm[:, :], mult_sb[:, :], ACT.Copy, bias=-1.0)
                act.drain()
                act.activation(logm[:, :], logm[:, :], ACT.Relu)
                act.drain()
                act.activation(logm[:, :], logm[:, :], ACT.Ln, bias=ones[0:NP, 0:1])
                act.drain().then_inc(hist_n, 1)

            @block.tensor
            def _(pe):
                def front(i, u):
                    s = u % 2
                    pe.wait_ge(slot_in[u], after_step(16, i, u))
                    if at_least(i, 1):
                        pe.wait_ge(s_eaT, i)
                    pe.sem_inc(held, 1)
                    for j in range(J):
                        mm = pe.transpose(p_mT[0][0:RBF, j * P:j * P + NP], rec_w[u][0:NP, j, 0:RBF],
                                          ident[0:NP, 0:NP])
                    mm.then_inc(s_eaT_p, 1)

                def hidden(i, u):
                    pe.wait_ge(s_eaT, i + 1)
                    if at_least(i, 1):
                        pe.wait_ge(s_silu, i)
                    pe.sem_inc(held, 1)
                    pe.matmul(p_mT[1][0:H, 0:J * NP], F1W_sb[:, :], eaT[u % 2], start=True,
                              stop=True).then_inc(s_f1, 1)

                def gates(i, u):
                    s = u % 2
                    pe.wait_ge(s_silu, i + 1)
                    if at_least(i, 2):
                        pe.wait_ge(s_gate, i - 1)
                    pe.sem_inc(held, 1)
                    for j in range(J):
                        mm = pe.matmul(gate_bank[s][0:NP, j * H:(j + 1) * H], silu[s][0:H + 1, j * NP:(j + 1) * NP],
                                       F2W_sb[:, :], start=True, stop=True)
                    mm.then_inc(s_gate_p, 1)

                def count(i, u):
                    pe.wait_ge(hot, i + 1)
                    for j in range(J):
                        mm = pe.matmul(p_x[:, 0:NB], hot_r[u % 2][0:NP, j, :], hot_b[u % 2][0:NP, j, :],
                                       start=isinstance(i, int) and i == 0 and j == 0,
                                       stop=isinstance(i, int) and i == STEPS - 1 and j == J - 1,
                                       skip_group_check=True)
                    mm.then_inc(hist, 1)

                def body(i, u):
                    if before(i + 1, STEPS):
                        front(i + 1, (u + 1) % U)
                    gates(i, u)
                    if before(i + 1, STEPS):
                        hidden(i + 1, (u + 1) % U)
                    count(i, u)
                front(0, 0)
                hidden(0, 0)
                run_steps(pe, body, STEPS)

            @block.gpsimd
            def _(pool):
                def body(i, u):
                    pool.wait_ge(slot_in[u], after_step(16, i, u))
                    pool.wait_ge(meta_in, i + 1)
                    pool.wait_ge(s_gate, i + 1)
                    pool.sem_inc(held, 1)
                    for j in range(J):
                        pool.indirect_dma_start(
                            out=rec_d[:, :], out_offset=bass.IndirectOffsetOnAxis(ap=idx[u][:, j:j + 1], axis=0),
                            in_=rec_w[u][0:NP, j, :], in_offset=None).then_inc(sent[u], 16)
                run_steps(pool, body, STEPS)
                for u in range(U):
                    pool.wait_ge(sent[u], before_step(64, STEPS, 0))

        def sums_of_blocks(eng, k, first_b, last_b, base, sums_in, accs, total):
            for s in range(U):
                eng.wait_ge(accs[s], before_step(16, base + total, 0))
            eng.sem_inc(held, 1)
            with eng.Fori(first_b, last_b) as b:
                g = eng.value_load(last_i[k][0:1, ds(b, 1)], min_val=0, max_val=NG - 1)
                eng.dma_start(agg_in[:, ds(b, 1), :], acc_d[ds(g, 1), :, :]
                              .rearrange("a p c -> p a c")).then_inc(sums_in, 16)

        def one_hot(v, u, tile, col, ready):
            for j in range(J):
                ins = v.tensor_scalar(oh[u % S][:, j, :], row_iota[:, :], tile[:, j, col:col + 1], None,
                                      ALU.is_equal)
            ins.then_inc(ready, 1)

        def gather_rows(pool, table, u, width, tile, arrived):
            for j in range(J):
                pool.indirect_dma_start(
                    out=row[u][:, j, 0:width], out_offset=None, in_=table,
                    in_offset=bass.IndirectOffsetOnAxis(ap=tile[:, j, C_DST:C_DST + 1].bitcast(I32), axis=0)
                ).then_inc(arrived[u], 16)

        def flip_one_hot(pe, u, flipped_p):
            for j in range(J):
                mm = pe.transpose(p_ohT[u % 2][:, j * P:(j + 1) * P], oh[u % S][:, j, :], identb[:, :])
            mm.then_inc(flipped_p, 1)

        def gather_own(pe, u, bank, width, done):
            for j in range(J):
                for k in range(PARTS):
                    mm = pe.matmul(bank[:, j * width:(j + 1) * width], ohT[u % S][0:NP, j * P:(j + 1) * P],
                                   own[u][:, k * width:(k + 1) * width], start=(k == 0), stop=(k == PARTS - 1))
            mm.then_inc(done, 1)

        def sum_group(pe, u, rhs, done):
            for j in range(J):
                mm = pe.matmul(p_agg[:, 0:VW], ohf[u % S][:, j, :], rhs[:, j, :], start=(j == 0), stop=(j == J - 1))
            mm.then_inc(done, 1)

        def load_group(sp, i, u, base, tile, group_rows, own_tab, width, arrived, used):
            if at_least(i, U):
                sp.wait_ge(used, base + i - U + 1)
                sp.sem_inc(held, 1)
            b = sp.value_load(blk_i[0][0:1, ds(i, 1)], min_val=0, max_val=NB - 1)
            sp.dma_start(tile, group_rows).then_inc(arrived[u], 16)
            sp.dma_start(own[u][:, 0:width], own_tab[ds(b, 1), :, 0:width]
                         .rearrange("a p c -> p (a c)")).then_inc(arrived[u], 16)

        rec_in = [sem(f"rec_in{s}") for s in range(U)]
        row_in = [sem(f"row_in{s}") for s in range(U)]
        stored = [sem(f"stored{s}") for s in range(U)]
        PAST = (1 + LAYERS) * NG

        g_hot = sem("g_hot")
        g_ohf = sem("g_ohf")
        g_flip_p = sem("g_flip_p")
        g_flip = sem("g_flip")
        g_own = sem("g_own")
        g_vals = sem("g_vals")
        g_agg = sem("g_agg")
        g_acc = sem("g_acc")
        g_lean = [sem(f"g_lean{s}") for s in range(U)]
        g_sums = sem("g_sums")
        g_var = sem("g_var")
        g_std = sem("g_std")

        with nc.Block() as block:
            @block.sync
            def _(sp):
                def body(i, u):
                    if at_least(i, U):
                        sp.wait_ge(g_lean[u], before_step(16, i, u))
                        sp.sem_inc(held, 1)
                    load_group(sp, i, u, 0, rec_t[u][:, :], rec_g[ds(i, 1), :, :].rearrange("a p c -> p (a c)"),
                               ei_d, PARTS * EMB, rec_in, g_vals)
                run_steps(sp, body, NG)
                sums_of_blocks(sp, 0, 0, NB // 2, 0, g_sums, stored, NG)
                sp.wait_ge(g_sums, 16 * NB)

            @block.gpsimd
            def _(pool):
                def body(i, u):
                    pool.wait_ge(rec_in[u], after_step(32, i, u))
                    if at_least(i, U):
                        pool.wait_ge(g_vals, i - U + 1)
                    pool.sem_inc(held, 1)
                    gather_rows(pool, gate_d[:, :], u, GW, rec_w[u], row_in)
                run_steps(pool, body, NG)

            @block.vector
            def _(v):
                def hots(i, u):
                    v.wait_ge(rec_in[u], after_step(32, i, u))
                    one_hot(v, u, rec_w[u], C_SRC, g_hot)

                def weights(i, u):
                    s = u % 2
                    v.wait_ge(row_in[u], after_step(64, i, u))
                    v.tensor_tensor(arg[u][:, 0:J].unsqueeze(2), rec_w[u][:, :, C_CUT:C_CUT + 1],
                                    row[u][:, :, H + EMB:GW], ALU.mult)
                    v.wait_ge(g_own, i + 1)
                    v.tensor_tensor(prod[s][:, :, 0:EMB], row[u][:, :, H:H + EMB],
                                    own_bank[s][:, 0:J * EMB].rearrange("p (j c) -> p j c", j=J), ALU.mult)
                    v.drain()
                    v.tensor_reduce(score[u][:, :], prod[s][:, :, 0:EMB], AX.X, ALU.add)
                    v.tensor_tensor(row[u][:, :, 0:H], row[u][:, :, 0:H],
                                    bc(arg[u][:, 0:J].unsqueeze(2), [P, J, H]), ALU.mult)
                    v.drain()
                    v.tensor_tensor(prod[s][:, :, 0:H], rec_w[u][:, :, RW:RG],
                                    bc(score[u][:, :].unsqueeze(2), [P, J, H]), ALU.add)
                    v.drain()
                    v.tensor_copy(vals[s][:, :, H:VW], row[u][:, :, H + EMB:GW])
                    v.tensor_tensor(vals[s][:, :, 0:H], prod[s][:, :, 0:H], row[u][:, :, 0:H],
                                    ALU.mult).then_inc(g_vals, 1)

                def sums(i, u):
                    v.wait_ge(g_agg, i + 1)
                    if at_least(i, U):
                        v.wait_ge(stored[u], before_step(16, i, u))
                    v.scalar_tensor_tensor(out=acc[u][:, :], in0=acc[(u - 1) % U][:, :],
                                           scalar=keep[0][0:NP, ds(i, 1)], in1=p_agg[0:NP, 0:VW],
                                           op0=ALU.mult, op1=ALU.add).then_inc(g_acc, 1)

                def body(i, u):
                    if before(i + 1, NG):
                        hots(i + 1, (u + 1) % U)
                    weights(i, u)
                    if at_least(i, 1):
                        sums(i - 1, (u - 1) % U)
                hots(0, 0)
                run_steps(v, body, NG)
                sums(NG - 1, (NG - 1) % U)
                v.wait_ge(g_sums, 16 * NB)
                v.tensor_scalar(stat[:, 0, 0:NB], agg_in[:, :, H], 1.0e-8, None, ALU.max)
                v.drain()
                v.reciprocal(stat[:, 0, 0:NB], stat[:, 0, 0:NB])
                v.drain()
                v.tensor_tensor(big_a[:, :, 0:H], agg_in[:, :, 0:H], bc(stat[:, 0, 0:NB].unsqueeze(2), [NP, NB, H]), ALU.mult)
                v.drain()
                v.tensor_tensor(big_a[:, :, 0:H], big_a[:, :, 0:H], HA[:, :, 0:H], ALU.add)
                v.drain()
                layer_norm(v, HA[:, :, 0:H], big_a[:, :, 0:H], [NP, NB, H], g_var, g_std, 1, tmp=big_b[:, :, 0:H])
                v.tensor_tensor(HA[:, :, 0:H], HA[:, :, 0:H], bc(gains_n[:, 0:H].unsqueeze(1), [NP, NB, H]), ALU.mult)
                v.drain()
                v.tensor_tensor(HA[:, :, 0:H], HA[:, :, 0:H], bc(gains_n[:, H:2 * H].unsqueeze(1), [NP, NB, H]), ALU.add)
                v.drain()

            @block.scalar
            def _(act):
                def turned(i, u):
                    s = u % 2
                    act.wait_ge(g_hot, i + 1)
                    if at_least(i, S):
                        act.wait_ge(g_agg, i - S + 1)
                    act.activation(ohf[u % S][:, :, :], oh[u % S][:, :, :], ACT.Copy).then_inc(g_ohf, 1)
                    act.wait_ge(g_flip_p, i + 1)
                    if at_least(i, S):
                        act.wait_ge(g_own, i - S + 1)
                    act.activation(ohT[u % S][:, :], p_ohT[u % 2], ACT.Copy).then_inc(g_flip, 1)

                def store(i, u):
                    act.wait_ge(g_acc, i + 1)
                    act.dma_start(acc_d[ds(i, 1), :, :].rearrange("a p c -> p (a c)"), acc[u][:, :]).then_inc(stored[u], 16)

                def body(i, u):
                    act.wait_ge(rec_in[u], after_step(32, i, u))
                    act.dma_start(lean_d[ds(i, 1), :, :].rearrange("a p (j c) -> p (a j) c", j=J),
                                  rec_w[u][:, :, 0:RW]).then_inc(g_lean[u], 16)
                    if before(i + 1, NG):
                        turned(i + 1, (u + 1) % U)
                    if at_least(i, 2):
                        store(i - 2, (u - 2) % U)
                turned(0, 0)
                run_steps(act, body, NG)
                for i in (NG - 2, NG - 1):
                    store(i, i % U)
                sums_of_blocks(act, 0, NB // 2, NB, 0, g_sums, stored, NG)
                for s in range(U):
                    act.wait_ge(g_lean[s], before_step(16, NG, 0))
                deviation(act, NB, g_var, g_std, 1)

            @block.tensor
            def _(pe):
                def front(i, u):
                    pe.wait_ge(g_hot, i + 1)
                    if at_least(i, 2):
                        pe.wait_ge(g_flip, i - 1)
                    flip_one_hot(pe, u, g_flip_p)
                    if at_least(i, 2):
                        pe.wait_ge(g_vals, i - 1)
                    pe.wait_ge(g_flip, i + 1)
                    gather_own(pe, u, own_bank[u % 2], EMB, g_own)

                def sums(i, u):
                    pe.wait_ge(g_vals, i + 1)
                    pe.wait_ge(g_ohf, i + 1)
                    if at_least(i, 1):
                        pe.wait_ge(g_acc, i)
                    sum_group(pe, u, vals[u % 2], g_agg)

                def body(i, u):
                    if before(i + 1, NG):
                        front(i + 1, (u + 1) % U)
                    sums(i, u)
                front(0, 0)
                run_steps(pe, body, NG)

        w_in = sem("w_in")
        wmT_p = sem("wmT_p")
        wmT_s = sem("wmT_s")
        wmu_p = sem("wmu_p")
        wmu_s = sem("wmu_s")
        wmu_in = sem("wmu_in")
        n_h = sem("n_h")
        t_p = sem("t_p")
        t_s = sem("t_s")
        y_p = sem("y_p")
        y_s = sem("y_s")
        n_var = sem("n_var")
        n_std = sem("n_std")
        n_tab = sem("n_tab")
        n_out = sem("n_out")
        a_agg = sem("a_agg")
        l_done = sem("l_done")
        l_hot = sem("l_hot")
        l_flip_p = sem("l_flip_p")
        l_flip = sem("l_flip")
        l_neg = sem("l_neg")
        l_ohf = sem("l_ohf")
        l_own = sem("l_own")
        l_key = sem("l_key")
        l_prod = sem("l_prod")
        l_score = sem("l_score")
        l_mask = sem("l_mask")
        l_gmax = sem("l_gmax")
        l_smax = sem("l_smax")
        l_hi = sem("l_hi")
        l_mid = sem("l_mid")
        l_parts = sem("l_parts")
        l_msum = sem("l_msum")
        l_shift = sem("l_shift")
        l_mT = sem("l_mT")
        l_mg = sem("l_mg")
        l_arg = sem("l_arg")
        l_es = sem("l_es")
        l_vals = sem("l_vals")
        l_agg = sem("l_agg")
        l_acc = sem("l_acc")
        l_sums = sem("l_sums")

        t_banks = [(p_t[0], p_t[1]), (p_own, p_mg)]

        def dense_pe(pe, n, src_, k, w, m):
            def flip(c):
                if c >= 2:
                    pe.wait_ge(t_s, n + c - 1)
                    pe.sem_inc(held, 1)
                for q in range(CH):
                    bank = t_banks[c % 2][q // 4]
                    mm = pe.transpose(bank[0:k, (q % 4) * P:(q % 4) * P + NP], src_(c * CH + q), ident[0:NP, 0:NP])
                mm.then_inc(t_p, 1)
            flip(0)
            for c in range(NC_):
                if c + 1 < NC_:
                    flip(c + 1)
                pe.wait_ge(t_s, n + c + 1)
                if c >= 2:
                    pe.wait_ge(y_s, n + c - 1)
                pe.sem_inc(held, 1)
                for q in range(CH):
                    mm = pe.matmul(p_mT[c % 2][0:NP, q * m:(q + 1) * m], xT[c % 2][0:k, q * P:q * P + NP], w,
                                   start=True, stop=True)
                mm.then_inc(y_p, 1)

        def dense_act(act, n, k, m, dst_):
            def turned(c):
                act.wait_ge(t_p, n + c + 1)
                if c >= 2:
                    act.wait_ge(y_p, n + c - 1)
                act.activation(xT[c % 2][0:k, 0:4 * P].rearrange("p (q e) -> p q e", q=4)[:, :, 0:NP],
                               t_banks[c % 2][0][0:k, :].rearrange("p (q e) -> p q e", q=4)[:, :, 0:NP], ACT.Copy)
                act.activation(xT[c % 2][0:k, 4 * P:4 * P + NP], t_banks[c % 2][1][0:k, 0:NP],
                               ACT.Copy).then_inc(t_s, 1)
            turned(0)
            for c in range(NC_):
                if c + 1 < NC_:
                    turned(c + 1)
                act.wait_ge(y_p, n + c + 1)
                act.activation(dst_(c), p_mT[c % 2][0:NP, 0:CH * m].rearrange("p (q m) -> p q m", m=m),
                               ACT.Copy).then_inc(y_s, 1)

        kh = row_out[:, :].rearrange("p (b c) -> p b c", b=NB)

        with nc.Block() as block:
            @block.sync
            def _(sp):
                with sp.Fori(0, LAYERS) as l:
                    base = l * NG
                    past = base + NG
                    sp.wait_ge(n_h, l + 1)
                    for k, a in enumerate((gq, gk, bq, bk, go, bo)):
                        sp.dma_start(gains[:, k * H:(k + 1) * H], a[ds(l, 1), :].to_broadcast([NP, H])).then_inc(w_in, 16)
                    sp.dma_start(wqk[:, 0:H], Wq[ds(l, 1), :, :].rearrange("a p c -> p (a c)")).then_inc(w_in, 16)
                    sp.dma_start(wqk[:, H:2 * H], Wk[ds(l, 1), :, :].rearrange("a p c -> p (a c)")).then_inc(w_in, 16)
                    sp.dma_start(wm[:, :], Wm[ds(l, 1), :, :].rearrange("a p c -> p (a c)")).then_inc(w_in, 16)
                    sp.dma_start(wub[:, :], Wu[ds(l, 1), H:2 * H, :].rearrange("a p c -> p (a c)")).then_inc(w_in, 16)
                    sp.dma_start(wu[0:H, :], Wu[ds(l, 1), 0:H, :].rearrange("a p c -> p (a c)")).then_inc(w_in, 16)
                    sp.wait_ge(wmu_s, l + 1)
                    sp.dma_start(wu[H:2 * H, :], wmu[:, :]).then_inc(wmu_in, 16)
                    sp.wait_ge(n_tab, l + 1)
                    sp.dma_start(kh_d.rearrange("(p b) c -> p (b c)", b=NB), row_out[:, :]).then_inc(n_out, 16)
                    sp.dma_start(own_d.rearrange("b p c -> p b c"),
                                 own3(QW).rearrange("p b k c -> p b (k c)")).then_inc(n_out, 16)
                    sp.wait_ge(n_out, l * 32 + 32)
                    sp.sem_inc(held, 1)
                    run_steps(sp, lambda i, u: load_group(
                        sp, i, u, base, rec_t[u][:, 0:J * RW], lean_d[ds(i, 1), :, :].rearrange("a p c -> p (a c)"),
                        own_d, PARTS * QW, rec_in, l_prod), NG)
                    sums_of_blocks(sp, 0, 0, NB // 2, past, l_sums, stored, NG)
                sp.wait_ge(l_sums, 16 * NB * LAYERS)

            @block.gpsimd
            def _(pool):
                with pool.Fori(0, LAYERS) as l:
                    base = l * NG
                    past = base + NG
                    pool.wait_ge(n_out, l * 32 + 32)

                    def body(i, u):
                        pool.wait_ge(rec_in[u], after_step(32, past + i, u))
                        if at_least(i, U):
                            pool.wait_ge(l_vals, base + i - U + 1)
                        pool.sem_inc(held, 1)
                        gather_rows(pool, kh_d[:, :], u, KW, rec[u], row_in)
                    run_steps(pool, body, NG)

            @block.vector
            def _(v):
                v.memset(own_out[:, :, H:QW], 1.0)
                v.memset(kh[:, :, 2 * H + 1:KW], 1.0)
                v.tensor_copy(kh[:, :, H:H + 1], logm[:, :].unsqueeze(2))
                v.drain().then_inc(n_h, 1)
                with v.Fori(0, LAYERS) as l:
                    base = l * NG
                    past = base + NG
                    v.wait_ge(y_s, l * 2 * NC_ + NC_)
                    v.wait_ge(w_in, l * 176 + 176)
                    qk_in = big_a[:, :, :].rearrange("p b (a c) -> p (b a) c", a=2)
                    qk_out = big_b[:, :, :].rearrange("p b (a c) -> p (b a) c", a=2)
                    shape = [NP, 2 * NB, H]
                    layer_norm_in_place(v, qk_in, qk_out, shape, n_var, n_std, 2 * l + 1)
                    v.tensor_tensor(big_a[:, :, :], big_a[:, :, :], bc(gains[:, 0:2 * H].unsqueeze(1), [NP, NB, 2 * H]), ALU.mult)
                    v.drain()
                    v.tensor_tensor(own_out[:, :, 0:H], big_a[:, :, 0:H], bc(gains[:, 2 * H:3 * H].unsqueeze(1), [NP, NB, H]), ALU.add)
                    v.tensor_tensor(kh[:, :, 0:H], big_a[:, :, H:2 * H], bc(gains[:, 3 * H:4 * H].unsqueeze(1), [NP, NB, H]), ALU.add)
                    v.tensor_copy(kh[:, :, H + 1:2 * H + 1], HA[:, :, 0:H])
                    v.drain()
                    split3(v, own_out[:, :, :], own3(QW), big_a[:, :, 0:QW])
                    v.drain().then_inc(n_tab, 1)

                    def hots(i, u):
                        v.wait_ge(rec_in[u], after_step(32, past + i, u))
                        one_hot(v, u, rec[u], C_SRC, l_hot)

                    def keys(i, u):
                        v.wait_ge(row_in[u], after_step(64, past + i, u))
                        v.scalar_tensor_tensor(out=row[u][:, :, 0:RBF], in0=rec[u][:, :, 0:RBF], scalar=0.1,
                                               in1=row[u][:, :, 0:RBF], op0=ALU.mult, op1=ALU.add).then_inc(l_key, 1)

                    def products(i, u):
                        v.wait_ge(l_key, base + i + 1)
                        v.wait_ge(l_own, base + i + 1)
                        v.tensor_tensor(prod[u % 2][:, :, :], row[u][:, :, 0:QW],
                                        p_own[:, 0:J * QW].rearrange("p (j c) -> p j c", j=J),
                                        ALU.mult).then_inc(l_prod, 1)

                    def scores(i, u):
                        v.wait_ge(l_prod, base + i + 1)
                        v.tensor_reduce(score[u][:, :], prod[u % 2][:, :, :], AX.X, ALU.add).then_inc(l_score, 1)

                    def group_max(i, u):
                        v.wait_ge(l_mT, base + i + 1)
                        v.tensor_reduce(gmax[u % 2][:, :], p_mT[u % 2][0:NP, :], AX.X, ALU.max).then_inc(l_gmax, 1)

                    def run_max(i, u):
                        v.wait_ge(l_gmax, base + i + 1)
                        v.scalar_tensor_tensor(out=smax[u][:, :], in0=smax[(u - 1) % U][:, :],
                                               scalar=fresh[0:NP, ds(i, 1)], in1=gmax[u % 2][:, :],
                                               op0=ALU.add, op1=ALU.max).then_inc(l_smax, 1)

                    def high(i, u):
                        v.wait_ge(l_smax, base + i + 1)
                        v.tensor_copy(parts[u % 2][:, 0:1], smax[u][:, :]).then_inc(l_hi, 1)

                    def decay(i, u):
                        v.scalar_tensor_tensor(out=arg[u][0:NP, J:J + 1], in0=smax[(u - 1) % U][:, :],
                                               scalar=fresh[0:NP, ds(i, 1)], in1=smax[u][:, :],
                                               op0=ALU.add, op1=ALU.subtract)

                    def middle(i, u):
                        v.wait_ge(l_hi, base + i + 1)
                        v.tensor_tensor(parts[u % 2][:, 1:2], smax[u][:, :], parts[u % 2][:, 0:1],
                                        ALU.subtract).then_inc(l_mid, 1)

                    def low(i, u):
                        v.wait_ge(l_mid, base + i + 1)
                        v.scalar_tensor_tensor(out=parts[u % 2][:, 2:3], in0=smax[u][:, :],
                                               scalar=parts[u % 2][:, 0:1], in1=parts[u % 2][:, 1:2],
                                               op0=ALU.subtract, op1=ALU.subtract).then_inc(l_parts, 1)

                    def maximum_sum(i, u):
                        v.wait_ge(l_mg, base + i + 1)
                        v.tensor_reduce(msum[u % 2][:, :], p_mg[:, 0:J * PARTS].rearrange("p (j k) -> p j k", j=J),
                                        AX.X, ALU.add).then_inc(l_msum, 1)

                    def shifted(i, u):
                        v.wait_ge(l_msum, base + i + 1)
                        v.tensor_tensor(arg[u][:, 0:J], score[u][:, :], msum[u % 2][:, :],
                                        ALU.subtract).then_inc(l_shift, 1)

                    def clipped(i, u):
                        v.wait_ge(l_shift, base + i + 1)
                        v.tensor_scalar(arg[u][:, 0:J], arg[u][:, 0:J], 20.0, None, ALU.min).then_inc(l_arg, 1)

                    def weigh(i, u):
                        v.wait_ge(l_es, base + i + 1)
                        v.tensor_tensor(vals[u % 2][:, :, :], row[u][:, :, H + 1:KW],
                                        bc(es[u][:, 0:J].unsqueeze(2), [P, J, VW]), ALU.mult).then_inc(l_vals, 1)

                    def sums(i, u):
                        v.wait_ge(l_agg, base + i + 1)
                        if at_least(i, U):
                            v.wait_ge(stored[u], before_step(16, past + i, u))
                        v.scalar_tensor_tensor(out=acc[u][:, :], in0=acc[(u - 1) % U][:, :],
                                               scalar=es[u][0:NP, J:J + 1], in1=p_agg[0:NP, 0:VW],
                                               op0=ALU.mult, op1=ALU.add).then_inc(l_acc, 1)

                    def step(i, u, now, one, two, three):
                        a, b, c = (u - 1) % U, (u - 2) % U, (u - 3) % U
                        if one:
                            group_max(i - 1, a)
                        if now:
                            keys(i, u)
                        if one:
                            run_max(i - 1, a)
                        if now:
                            products(i, u)
                        if one:
                            high(i - 1, a)
                            decay(i - 1, a)
                        if now:
                            scores(i, u)
                        if one:
                            middle(i - 1, a)
                        if now and before(i + 2, NG):
                            hots(i + 2, (u + 2) % U)
                        if one:
                            low(i - 1, a)
                        if three:
                            sums(i - 3, c)
                        if one:
                            maximum_sum(i - 1, a)
                        if two:
                            weigh(i - 2, b)
                        if one:
                            shifted(i - 1, a)
                            clipped(i - 1, a)
                    hots(0, 0)
                    hots(1, 1)
                    run_steps(v, lambda i, u: step(i, u, True, at_least(i, 1), at_least(i, 2), at_least(i, 3)), NG)
                    step(NG, NG % U, False, True, True, True)
                    step(NG + 1, (NG + 1) % U, False, False, True, True)
                    step(NG + 2, (NG + 2) % U, False, False, False, True)
                    v.wait_ge(l_sums, l * 16 * NB + 16 * NB)
                    v.tensor_scalar(stat[:, 0, 0:NB], agg_in[:, :, H], 1.0e-10, None, ALU.add)
                    v.drain()
                    v.reciprocal(stat[:, 0, 0:NB], stat[:, 0, 0:NB])
                    v.drain()
                    v.tensor_tensor(HA[:, :, H:2 * H], agg_in[:, :, 0:H],
                                    bc(stat[:, 0, 0:NB].unsqueeze(2), [NP, NB, H]), ALU.mult).then_inc(a_agg, 1)
                    v.wait_ge(y_s, l * 2 * NC_ + 2 * NC_)
                    zz, t1 = big_a[:, :, 0:H], big_b[:, :, 0:H]
                    v.scalar_tensor_tensor(out=t1, in0=zz, scalar=0.01, in1=zz, op0=ALU.mult, op1=ALU.max)
                    v.drain()
                    v.tensor_tensor(zz, t1, HA[:, :, 0:H], ALU.add)
                    v.drain()
                    layer_norm_in_place(v, zz, t1, [NP, NB, H], n_var, n_std, 2 * l + 2)
                    v.tensor_tensor(zz, zz, bc(gains[:, 4 * H:5 * H].unsqueeze(1), [NP, NB, H]), ALU.mult)
                    v.drain()
                    v.tensor_tensor(HA[:, :, 0:H], zz, bc(gains[:, 5 * H:6 * H].unsqueeze(1), [NP, NB, H]), ALU.add)
                    v.drain().then_inc(n_h, 1)

            @block.scalar
            def _(act):
                with act.Fori(0, LAYERS) as l:
                    base = l * NG
                    past = base + NG
                    act.wait_ge(wmT_p, l + 1)
                    act.activation(wmT[:, :], p_x[0:H, 0:H], ACT.Copy).then_inc(wmT_s, 1)
                    act.wait_ge(wmu_p, l + 1)
                    act.activation(wmu[:, :], p_x[0:H, 128:128 + H], ACT.Copy).then_inc(wmu_s, 1)
                    dense_act(act, l * 2 * NC_, H, 2 * H, lambda c: big_a[:, c * CH:(c + 1) * CH, :])
                    deviation(act, 2 * NB, n_var, n_std, 2 * l + 1)

                    def turned(i, u):
                        act.wait_ge(l_hot, base + i + 1)
                        if at_least(i, 2):
                            act.wait_ge(l_mask, J * (base + i - 1))
                        act.activation(neg_t[u % 2][:, :], oh[u % S][:, :, :].rearrange("p j n -> p (j n)"), ACT.Copy,
                                       scale=BIG, bias=-BIG).then_inc(l_neg, 1)
                        act.wait_ge(l_flip_p, base + i + 1)
                        if at_least(i, S):
                            act.wait_ge(l_mg, base + i - S + 1)
                        act.activation(ohT[u % S][:, :], p_ohT[u % 2], ACT.Copy).then_inc(l_flip, 1)

                    def full(i, u):
                        if at_least(i, S):
                            act.wait_ge(l_agg, base + i - S + 1)
                        act.activation(ohf[u % S][:, :, :], oh[u % S][:, :, :], ACT.Copy).then_inc(l_ohf, 1)

                    def mask(i, u):
                        s = u % 2
                        act.wait_ge(l_score, base + i + 1)
                        act.wait_ge(l_neg, base + i + 1)
                        if at_least(i, 2):
                            act.wait_ge(l_mT, base + i - 1)
                        for j in range(J):
                            act.activation(masked_t[s][:, j * P:(j + 1) * P], neg_t[s][:, j * P:(j + 1) * P],
                                           ACT.Identity, bias=score[u][:, j:j + 1]).then_inc(l_mask, 1)

                    def exps(i, u):
                        act.wait_ge(l_arg, base + i + 1)
                        act.activation(es[u][:, :], arg[u][:, :], ACT.Exp).then_inc(l_es, 1)

                    def store(i, u):
                        act.wait_ge(l_acc, base + i + 1)
                        act.dma_start(acc_d[ds(i, 1), :, :].rearrange("a p c -> p (a c)"), acc[u][:, :]).then_inc(stored[u], 16)

                    def body(i, u):
                        mask(i, u)
                        if before(i + 2, NG):
                            turned(i + 2, (u + 2) % U)
                        full(i, u)
                        if at_least(i, 1):
                            exps(i - 1, (u - 1) % U)
                        if at_least(i, 4):
                            store(i - 4, (u - 4) % U)
                    turned(0, 0)
                    turned(1, 1)
                    run_steps(act, body, NG)
                    exps(NG - 1, (NG - 1) % U)
                    for i in range(NG - 4, NG):
                        store(i, i % U)
                    sums_of_blocks(act, 0, NB // 2, NB, past, l_sums, stored, NG)
                    dense_act(act, l * 2 * NC_ + NC_, 2 * H, H, lambda c: big_a[:, c * CH:(c + 1) * CH, 0:H])
                    deviation(act, NB, n_var, n_std, 2 * l + 2)

            @block.tensor
            def _(pe):
                with pe.Fori(0, LAYERS) as l:
                    base = l * NG
                    past = base + NG
                    pe.wait_ge(w_in, l * 176 + 176)
                    pe.sem_inc(held, 1)
                    pe.transpose(p_x[0:H, 0:H], wm[:, :], ident[0:H, 0:H]).then_inc(wmT_p, 1)
                    pe.wait_ge(wmT_s, l + 1)
                    pe.sem_inc(held, 1)
                    pe.matmul(p_x[0:H, 128:128 + H], wmT[:, :], wub[:, :], start=True, stop=True).then_inc(wmu_p, 1)
                    pe.wait_ge(n_h, l + 1)
                    pe.sem_inc(held, 1)
                    dense_pe(pe, l * 2 * NC_, lambda b: HA[:, b, 0:H], H, wqk[:, :], 2 * H)

                    def front(i, u):
                        pe.wait_ge(l_hot, base + i + 1)
                        if at_least(i, 2):
                            pe.wait_ge(l_flip, base + i - 1)
                        flip_one_hot(pe, u, l_flip_p)

                    def queries(i, u):
                        pe.wait_ge(rec_in[u], after_step(32, past + i, u))
                        pe.wait_ge(l_flip, base + i + 1)
                        if at_least(i, 1):
                            pe.wait_ge(l_prod, base + i)
                        gather_own(pe, u, p_own, QW, l_own)

                    def flip_masked(i, u):
                        if at_least(i, 2):
                            pe.wait_ge(l_gmax, base + i - 1)
                        for j in range(J):
                            pe.wait_ge(l_mask, J * (base + i) + j + 1)
                            mm = pe.transpose(p_mT[u % 2][:, j * P:(j + 1) * P], masked_t[u % 2][:, j * P:(j + 1) * P],
                                              ident[:, :])
                        mm.then_inc(l_mT, 1)

                    def gather_max(i, u):
                        pe.wait_ge(l_parts, base + i + 1)
                        if at_least(i, 1):
                            pe.wait_ge(l_msum, base + i)
                        for j in range(J):
                            mm = pe.matmul(p_mg[:, j * PARTS:(j + 1) * PARTS], ohT[u % S][0:NP, j * P:(j + 1) * P],
                                           parts[u % 2][:, :], start=True, stop=True)
                        mm.then_inc(l_mg, 1)

                    def sums(i, u):
                        pe.wait_ge(l_vals, base + i + 1)
                        pe.wait_ge(l_ohf, base + i + 1)
                        if at_least(i, 1):
                            pe.wait_ge(l_acc, base + i)
                        sum_group(pe, u, vals[u % 2], l_agg)

                    def body(i, u):
                        if at_least(i, 1):
                            gather_max(i - 1, (u - 1) % U)
                        flip_masked(i, u)
                        if before(i + 1, NG):
                            queries(i + 1, (u + 1) % U)
                        if before(i + 2, NG):
                            front(i + 2, (u + 2) % U)
                        if at_least(i, 2):
                            sums(i - 2, (u - 2) % U)
                    pe.wait_ge(n_std, 2 * l + 1)
                    front(0, 0)
                    front(1, 1)
                    queries(0, 0)
                    run_steps(pe, body, NG)
                    gather_max(NG - 1, (NG - 1) % U)
                    for i in (NG - 2, NG - 1):
                        sums(i, i % U)
                    pe.wait_ge(wmu_in, l * 16 + 16)
                    pe.wait_ge(a_agg, l + 1)
                    pe.sem_inc(held, 1)
                    dense_pe(pe, l * 2 * NC_ + NC_, lambda b: HA[:, b, :], 2 * H, wu[:, :], H)
                    pe.wait_ge(n_std, 2 * l + 2)

        c_h = sem("c_h")
        c_w = sem("c_w")
        c_var = sem("c_var")
        c_std = sem("c_std")
        c_tab = sem("c_tab")
        c_out = sem("c_out")
        DN = 2 * NC_ * LAYERS
        with nc.Block() as block:
            @block.vector
            def _(v):
                v.tensor_tensor(X[:, :, :], X[:, :, :], HA[:, :, 0:H], ALU.add)
                v.drain()
                layer_norm(v, big_a[:, :, 0:H], X[:, :, :], [NP, NB, H], c_var, c_std, 1, tmp=big_b[:, :, 0:H])
                v.tensor_scalar(HA[:, :, 0:H], big_a[:, :, 0:H], 0.0, None, ALU.max).then_inc(c_h, 1)
                v.wait_ge(y_s, DN + NC_)
                v.tensor_tensor(HA[:, :, H:2 * H], big_a[:, :, 0:H], bc(dinv[:, :].unsqueeze(2), [NP, NB, H]), ALU.mult)
                v.drain()
                split3(v, HA[:, :, H:2 * H], own3(H), big_a[:, :, 0:H])
                v.drain().then_inc(c_tab, 1)

            @block.scalar
            def _(act):
                deviation(act, NB, c_var, c_std, 1)
                dense_act(act, DN, H, H, lambda c: big_a[:, c * CH:(c + 1) * CH, 0:H])

            @block.tensor
            def _(pe):
                pe.wait_ge(c_w, 16)
                pe.wait_ge(c_h, 1)
                dense_pe(pe, DN, lambda b: HA[:, b, 0:H], H, wm[:, :], H)

            @block.sync
            def _(sp):
                sp.dma_start(wm[:, :], W1).then_inc(c_w, 16)
                sp.wait_ge(c_tab, 1)
                sp.dma_start(own_d[:, :, 0:PARTS * H].rearrange("b p c -> p b c"),
                             own3(H).rearrange("p b k c -> p b (k c)")).then_inc(c_out, 16)
                sp.wait_ge(c_out, 16)

        m_hot = sem("m_hot")
        m_flip_p = sem("m_flip_p")
        m_flip = sem("m_flip")
        m_own = sem("m_own")
        m_msg = sem("m_msg")
        mrow = [row[u][:, :, :].rearrange("p j c -> p (j c)").bitcast(BF16)[:, 0:J * MW]
                .rearrange("p (j c) -> p j c", j=J) for u in range(U)]
        msg_bank = [[p_own, p_x], [p_mT[0], p_mT[1]]]

        def msg_cols(u, j):
            return msg_bank[u % 2][j // 2][:, (j % 2) * PARTS * H:(j % 2 + 1) * PARTS * H]

        with nc.Block() as block:
            @block.sync
            def _(sp):
                def body(i, u):
                    if at_least(i, U):
                        sp.wait_ge(sent[u], before_step(64, STEPS + i, u))
                        sp.sem_inc(held, 1)
                    load_group(sp, i, u, 0, rec_t[u][:, 0:J * RW],
                               lean_d[ds(i, 1), :, :].rearrange("a p c -> p (a c)"), own_d, PARTS * H, rec_in, m_own)
                run_steps(sp, body, NG)

            @block.vector
            def _(v):
                def hots(i, u):
                    v.wait_ge(rec_in[u], after_step(32, PAST + i, u))
                    one_hot(v, u, rec[u], C_SRC, m_hot)

                def body(i, u):
                    if before(i + 1, NG):
                        hots(i + 1, (u + 1) % U)
                    if at_least(i, U):
                        v.wait_ge(sent[u], before_step(64, STEPS + i, u))
                    v.tensor_copy(mrow[u][:, :, PARTS * H:MW], bc(rec[u][:, :, C_DROW:C_DROW + 1], [P, J, 2]))
                    v.wait_ge(m_own, i + 1)
                    for q in range(2):
                        ins = v.tensor_copy(mrow[u][:, 2 * q:2 * q + 2, 0:PARTS * H],
                                            msg_bank[u % 2][q][:, 0:2 * PARTS * H].rearrange("p (j c) -> p j c", j=2))
                    ins.then_inc(m_msg, 1)
                hots(0, 0)
                run_steps(v, body, NG)

            @block.scalar
            def _(act):
                def body(i, u):
                    act.wait_ge(m_flip_p, i + 1)
                    if at_least(i, S):
                        act.wait_ge(m_own, i - S + 1)
                    act.activation(ohT[u % S][:, :], p_ohT[u % 2], ACT.Copy).then_inc(m_flip, 1)
                run_steps(act, body, NG)

            @block.tensor
            def _(pe):
                def front(i, u):
                    pe.wait_ge(m_hot, i + 1)
                    if at_least(i, 2):
                        pe.wait_ge(m_flip, i - 1)
                    flip_one_hot(pe, u, m_flip_p)

                def body(i, u):
                    if before(i + 1, NG):
                        front(i + 1, (u + 1) % U)
                    pe.wait_ge(m_flip, i + 1)
                    if at_least(i, 2):
                        pe.wait_ge(m_msg, i - 1)
                    for j in range(J):
                        mm = pe.matmul(msg_cols(u, j), ohT[u % S][0:NP, j * P:(j + 1) * P], own[u][:, 0:PARTS * H],
                                       start=True, stop=True)
                    mm.then_inc(m_own, 1)
                front(0, 0)
                run_steps(pe, body, NG)

            @block.gpsimd
            def _(pool):
                def body(i, u):
                    pool.wait_ge(m_msg, i + 1)
                    pool.sem_inc(held, 1)
                    for j in range(J):
                        pool.indirect_dma_start(
                            out=msg_d[:, :], out_offset=bass.IndirectOffsetOnAxis(
                                ap=rec[u][:, j, C_POS2:RW].bitcast(I32), axis=0),
                            in_=mrow[u][:, j, :], in_offset=None, bounds_check=NG * EG - 1,
                            oob_is_err=False).then_inc(sent[u], 16)
                run_steps(pool, body, NG)
                for u in range(U):
                    pool.wait_ge(sent[u], before_step(64, STEPS + NG, 0))

        d_hot = sem("d_hot")
        d_agg = sem("d_agg")
        d_acc = sem("d_acc")
        d_sums = sem("d_sums")
        d_res = sem("d_res")
        d_out = sem("d_out")
        part_sum = [neg_t[s][:, 0:H] for s in range(2)]
        with nc.Block() as block:
            @block.sync
            def _(sp):
                def body(i, u):
                    if at_least(i, U):
                        sp.wait_ge(d_agg, i - U + 1)
                    sp.dma_start(mrow[u].rearrange("p j c -> p (j c)"),
                                 msg_g[ds(i, 1), :, :].rearrange("a p c -> p (a c)")).then_inc(slot_in[u], 16)
                run_steps(sp, body, NG)
                sums_of_blocks(sp, 1, 0, NB // 2, PAST, d_sums, stored, NG)
                sp.wait_ge(d_res, 1)
                sp.dma_start(out.rearrange("(p b) c -> p b c", b=NB), X[:, :, :]).then_inc(d_out, 16)
                sp.wait_ge(d_out, 16)

            @block.vector
            def _(v):
                def hots(i, u):
                    v.wait_ge(slot_in[u], after_step(16, STEPS + i, u))
                    if at_least(i, S):
                        v.wait_ge(d_agg, i - S + 1)
                    v.tensor_copy(score[u][:, :].unsqueeze(2), mrow[u][:, :, PARTS * H:PARTS * H + 1])
                    v.drain()
                    one_hot(v, u, score[u][:, :].unsqueeze(2), 0, d_hot)

                def body(i, u):
                    if before(i + 1, NG):
                        hots(i + 1, (u + 1) % U)
                    if at_least(i, 1):
                        v.wait_ge(d_acc, i)
                    v.wait_ge(d_agg, i + 1)
                    if at_least(i, U):
                        v.wait_ge(stored[u], before_step(16, PAST + i, u))
                    v.tensor_reduce(part_sum[u % 2][0:NP, :], agg_bank[u % 2][0:NP, 0:PARTS * H]
                                    .rearrange("p (k c) -> p c k", k=PARTS), AX.X, ALU.add)
                    v.drain()
                    v.scalar_tensor_tensor(out=acc[u][:, 0:H], in0=acc[(u - 1) % U][:, 0:H],
                                           scalar=keep[1][0:NP, ds(i, 1)], in1=part_sum[u % 2][0:NP, :],
                                           op0=ALU.mult, op1=ALU.add).then_inc(d_acc, 1)
                hots(0, 0)
                run_steps(v, body, NG)
                v.wait_ge(d_sums, 16 * NB)
                v.tensor_tensor(big_a[:, :, 0:H], agg_in[:, :, 0:H], HA[:, :, H:2 * H], ALU.add)
                v.drain()
                v.tensor_tensor(big_a[:, :, 0:H], big_a[:, :, 0:H], bc(dinv[:, :].unsqueeze(2), [NP, NB, H]), ALU.mult)
                v.drain()
                v.tensor_tensor(X[:, :, :], X[:, :, :], big_a[:, :, 0:H], ALU.add)
                v.drain()
                v.tensor_tensor(X[:, :, :], X[:, :, :], bc(gains_n[:, 2 * H:3 * H].unsqueeze(1), [NP, NB, H]), ALU.add)
                v.drain().then_inc(d_res, 1)

            @block.scalar
            def _(act):
                def body(i, u):
                    act.wait_ge(d_acc, i + 1)
                    act.dma_start(acc_d[ds(i, 1), :, :].rearrange("a p c -> p (a c)"), acc[u][:, :]).then_inc(stored[u], 16)
                run_steps(act, body, NG)
                sums_of_blocks(act, 1, NB // 2, NB, PAST, d_sums, stored, NG)

            @block.tensor
            def _(pe):
                def body(i, u):
                    pe.wait_ge(d_hot, i + 1)
                    if at_least(i, 2):
                        pe.wait_ge(d_acc, i - 1)
                    for j in range(J):
                        mm = pe.matmul(agg_bank[u % 2][:, 0:PARTS * H], oh[u % S][:, j, :], mrow[u][:, j, 0:PARTS * H],
                                       start=(j == 0), stop=(j == J - 1))
                    mm.then_inc(d_agg, 1)
                run_steps(pe, body, NG)


_INS = ["x", "src", "dst", "edge_attr_40", "edge_weight", "node_type_119", "node_vec",
        "L0_gnn_Wq", "L0_gnn_gq", "L0_gnn_bq", "L0_gnn_Wk", "L0_gnn_gk", "L0_gnn_bk", "L0_gnn_Wm", "L0_gnn_Wu",
        "L0_gnn_go", "L0_gnn_bo", "L0_gnn_F1W", "L0_gnn_F1b", "L0_gnn_F2W", "L0_gnn_F2b", "L0_gnn_gn",
        "L0_gnn_bn", "L0_gnn_emb", "L0_gnn_adapt", "L1_gnn_W", "L1_gnn_b"]


def kernel(**inputs):
    import numpy as _np
    import concourse.bacc as _bacc
    from concourse import mybir as _mybir
    from concourse.bass_utils import run_bass_kernel_spmd as _run

    nc = _bacc.Bacc("TRN2", target_bir_lowering=False, num_devices=1)
    arrays, args = {}, []
    for name in _INS:
        a = _np.ascontiguousarray(inputs[name])
        arrays[f"in_{name}"] = a
        args.append(nc.dram_tensor(f"in_{name}", a.shape, _mybir.dt.from_np(a.dtype), kind="ExternalInput").ap())
    args.append(nc.dram_tensor("out_0", (N, H), F32, kind="ExternalOutput").ap())
    build(nc, *args)
    r = _run(nc, [arrays], core_ids=[0])
    return r.results[0]["out_0"]
```

```python
from contextlib import ExitStack

import concourse.bass as bass
from concourse import mybir

F32 = mybir.dt.float32
I32 = mybir.dt.int32
BF16 = mybir.dt.bfloat16
ALU = mybir.AluOpType
ACT = mybir.ActivationFunctionType
AX = mybir.AxisListType
ds = bass.ds

N, E, H, RBF, LAYERS, NELEM, EMB = 6250, 200000, 48, 40, 4, 119, 32
NB = 50
NP = N // NB
P = 128
J = 4
EG = P * J
NG = (E + NB * (EG - 1)) // EG
FREE_G = -(-E // EG)
EC = E // NP
U = 8
S = 4
RW = RBF + 5
RG = RW + H
C_SRC, C_CUT, C_DROW, C_DST, C_POS2 = RBF, RBF + 1, RBF + 2, RBF + 3, RBF + 4
PARTS = 3
MW = PARTS * H + 2
VW = H + 1
QW = H + 1
KW = 2 * H + 2
GW = H + EMB + 1
CH = 5
NC_ = NB // CH
BIG = 1.0e30
ROUND = 12582912.0
assert NG % U == 0 and NB * NP == N and EC * NP == E and EC % (U * J) == 0 and NC_ * CH == NB


def after_step(per_step, i, u):
    return per_step // U * (i - u) + per_step


def before_step(per_step, i, u):
    return per_step // U * (i - u)


def run_steps(eng, body, total):
    for i in range(U):
        body(i, i)
    with eng.Fori(U, total - U, U) as t:
        for u in range(U):
            body(t + u, u)
    for i in range(total - U, total):
        body(i, i % U)


def at_least(i, k):
    return not isinstance(i, int) or i >= k


def before(i, total):
    return not isinstance(i, int) or i < total


def build(nc, x, src, dst, ea, weight, z, mult, Wq, gq, bq, Wk, gk, bk, Wm, Wu, go, bo,
          F1W, F1b, F2W, F2b, gn, bn, emb, adapt, W1, b1, out):
    ctx = ExitStack()
    with ctx:
        def sb(name, shape, dt=F32):
            return ctx.enter_context(nc.sbuf_tensor(name, shape, dt))

        def ps(name, shape, dt=F32):
            return ctx.enter_context(nc.psum_tensor(name, shape, dt))

        def sem(name):
            return ctx.enter_context(nc.semaphore(name))

        def dram(name, shape, dt=F32):
            return nc.dram_tensor(name, shape, dt).ap()

        ctx.enter_context(nc.allow_non_contiguous_dma(reason="short rows of records and index columns"))

        rec_d = dram("rec_d", [NG * EG, RG])
        lean_d = dram("lean_d", [NG, P, J * RW])
        msg_d = dram("msg_d", [NG * EG, MW], BF16)
        emb2_d = dram("emb2_d", [NELEM, 2 * EMB])
        gate_d = dram("gate_d", [N, GW])
        kh_d = dram("kh_d", [N, KW])
        own_d = dram("own_d", [NB, NP, PARTS * QW], BF16)
        ei_d = dram("ei_d", [NB, NP, PARTS * EMB], BF16)
        acc_d = dram("acc_d", [NG, NP, VW])
        blk_d = [dram(f"blk_d{k}", [NG]) for k in range(2)]
        rec_g = rec_d.rearrange("(g p j) c -> g p (j c)", p=P, j=J)
        msg_g = msg_d.rearrange("(g p j) c -> g p (j c)", p=P, j=J)

        ident = sb("ident", [P, P])
        ones = sb("ones", [P, P])
        upper = sb("upper", [P, P])
        identb = sb("identb", [P, P], BF16)
        row_iota = sb("row_iota", [P, P], BF16)
        blk_iota = sb("blk_iota", [P, NB])
        grp_iota = sb("grp_iota", [NG // J, J])
        eps = sb("eps", [P, 1])
        half_pi = sb("half_pi", [P, 1])
        X = sb("X", [NP, NB, H])
        HA = sb("HA", [NP, NB, 2 * H])
        big_a = sb("big_a", [NP, NB, 2 * H])
        big_b = sb("big_b", [NP, NB, 2 * H])
        agg_in = sb("agg_in", [NP, NB, VW])
        row_out = sb("row_out", [NP, NB * KW])
        own_out = sb("own_out", [NP, NB, QW])
        stat = sb("stat", [NP, 3, 2 * NB])
        mult_sb = sb("mult_sb", [NP, NB])
        logm = sb("logm", [NP, NB])
        z_sb = sb("z_sb", [NP, NB], I32)
        dinv = sb("dinv", [NP, NB])
        emb_sb = sb("emb_sb", [NELEM, 2 * EMB])
        embT = sb("embT", [EMB, NELEM])
        adapt_sb = sb("adapt_sb", [EMB, EMB])
        F1W_sb = sb("F1W_sb", [RBF, H])
        F1b_sb = sb("F1b_sb", [H, 1])
        F2W_sb = sb("F2W_sb", [H + 1, H])
        wqk = sb("wqk", [H, 2 * H])
        wm = sb("wm", [H, H])
        wmT = sb("wmT", [H, H])
        wub = sb("wub", [H, H])
        wmu = sb("wmu", [H, H])
        wu = sb("wu", [2 * H, H])
        gains = sb("gains", [NP, 6 * H])
        gains_n = sb("gains_n", [NP, 3 * H])
        fill_r = sb("fill_r", [P, J, RG])
        fill_m = sb("fill_m", [P, J, MW], BF16)
        blk_src = sb("blk_src", [NP, EC])
        meta_t = sb("meta_t", [P, EC * 3])
        metaf = meta_t[0:NP, :].rearrange("p (t c) -> p t c", c=3)
        metai_t = sb("metai_t", [P, EC * 2], I32)
        metai = metai_t[0:NP, :].rearrange("p (t c) -> p t c", c=2)
        blks = [blk_src[:, :], metai_t[0:NP, :].bitcast(F32).rearrange("p (t c) -> p t c", c=2)[:, :, 1]]
        cnt = sb("cnt", [NP, NB])
        minus_b = sb("minus_b", [NP, NB])
        signs = sb("signs", [NP, NB + 1])
        first = sb("first", [NP, 2, NB])
        groups = sb("groups", [NP, NB])
        gend = sb("gend", [NP, NB])
        cmp_g = sb("cmp_g", [NG // J, J, NB])
        blk_g = sb("blk_g", [NG // J, J])
        blk_row = sb("blk_row", [P, NG + 1])
        keep = [sb(f"keep{k}", [P, NG]) for k in range(2)]
        fresh = sb("fresh", [P, NG])
        blk_i = [sb(f"blk_i{k}", [1, NG], I32) for k in range(2)]
        last_i = [sb(f"last_i{k}", [1, NB], I32) for k in range(2)]

        rec_t = [sb(f"rec{s}", [P, J * RG]) for s in range(U)]
        rec_w = [t[:, :].rearrange("p (j c) -> p j c", j=J) for t in rec_t]
        rec = [t[:, 0:J * RW].rearrange("p (j c) -> p j c", j=J) for t in rec_t]
        row = [metai_t[:, s * J * KW:(s + 1) * J * KW].bitcast(F32).rearrange("p (j c) -> p j c", j=J)
               for s in range(U)]
        own = [sb(f"own{s}", [NP, PARTS * QW], BF16) for s in range(U)]
        oh = [sb(f"oh{s}", [P, J, P], BF16) for s in range(S)]
        ohf = [meta_t[:, s * J * P:(s + 1) * J * P].rearrange("p (j n) -> p j n", j=J) for s in range(S)]
        xT = [meta_t[0:2 * H, S * J * P + s * CH * P:S * J * P + (s + 1) * CH * P] for s in range(2)]
        ohT = [sb(f"ohT{s}", [P, J * P], BF16) for s in range(S)]
        neg_t = [sb(f"neg{s}", [P, J * P]) for s in range(2)]
        masked_t = [sb(f"masked{s}", [P, J * P]) for s in range(2)]
        prod = [sb(f"prod{s}", [P, J, QW]) for s in range(2)]
        score = [sb(f"score{s}", [P, J]) for s in range(U)]
        smax = [sb(f"smax{s}", [NP, 1]) for s in range(U)]
        gmax = [sb(f"gmax{s}", [NP, 1]) for s in range(2)]
        parts = [sb(f"parts{s}", [NP, PARTS], BF16) for s in range(2)]
        msum = [sb(f"msum{s}", [P, J]) for s in range(2)]
        arg = [sb(f"arg{s}", [P, J + 1]) for s in range(U)]
        es = [sb(f"es{s}", [P, J + 1]) for s in range(U)]
        vals = [sb(f"vals{s}", [P, J, VW]) for s in range(2)]
        acc = [sb(f"acc{s}", [NP, VW]) for s in range(U)]
        idx = [sb(f"idx{s}", [NP, J], I32) for s in range(U)]

        flat_a = big_a[:, :, :].rearrange("p a b -> p (a b)")
        flat_b = big_b[:, :, :].rearrange("p a b -> p (a b)")
        key_i = [agg_in[:, :, :].rearrange("p a b -> p (a b)")[:, 0:EC].bitcast(I32),
                 row_out[:, 0:EC].bitcast(I32)]
        keyf, mask = flat_a[:, 0:EC], flat_a[:, EC:2 * EC]
        zero_b = flat_b[:, 0:NB]
        sign = flat_b[:, EC:2 * EC]
        wt = row_out[:, EC:2 * EC]
        cosw = row_out[:, 2 * EC:3 * EC]

        p_t = [ps(f"p_t{s}", [P, J * P]) for s in range(2)]
        p_ohT = [t[:, :].bitcast(BF16)[:, 0:J * P] for t in p_t]
        p_mT = [ps(f"p_mT{s}", [P, J * P]) for s in range(2)]
        p_own = ps("p_own", [P, 512])
        p_mg = ps("p_mg", [P, 512])
        p_agg = ps("p_agg", [P, 512])
        p_x = ps("p_x", [P, 512])
        own_bank = [p_own, p_x]
        agg_bank = [p_agg, p_mg]

        def bc(ap, shape):
            return ap.to_broadcast(shape)

        loaded = sem("loaded")
        consts = sem("consts")
        fills = sem("fills")
        filled = sem("filled")
        filled_last = sem("filled_last")
        held = sem("held")
        fill_of = [(rec_g, fill_r), (msg_g, fill_m)]
        ready_emb = sem("ready_emb")
        blocked = sem("blocked")
        signed = sem("signed")
        counted = sem("counted")
        summed = sem("summed")
        taken = sem("taken")
        blk_made = sem("blk_made")
        blk_out = sem("blk_out")
        blk_in = sem("blk_in")
        cos_in = sem("cos_in")
        cos_out = sem("cos_out")
        embT_p = sem("embT_p")
        embT_s = sem("embT_s")
        emb_p = sem("emb_p")
        emb_s = sem("emb_s")
        emb_out = sem("emb_out")
        var1 = sem("var1")
        std1 = sem("std1")

        def fill_last(eng, k, first_b, last_b):
            table, fill = fill_of[k]
            eng.wait_ge(filled, 32)
            eng.sem_inc(held, 1)
            with eng.Fori(first_b, last_b) as b:
                g = eng.value_load(last_i[k][0:1, ds(b, 1)], min_val=0, max_val=NG - 1)
                eng.dma_start(table[ds(g, 1), :, :].rearrange("a p c -> p (a c)"),
                              fill[:, :, :].rearrange("p j c -> p (j c)")).then_inc(filled_last, 16)

        def layer_norm(eng, dst_, src_, shape, var_sem, std_sem, v, tmp=None, at=0):
            n = shape[1]
            mean, var, rstd = stat[:, 0, at:at + n], stat[:, 1, at:at + n], stat[:, 2, at:at + n]
            eng.tensor_reduce(mean, src_, AX.X, ALU.add)
            eng.drain()
            eng.tensor_scalar(mean, mean, 1.0 / H, None, ALU.mult)
            eng.drain()
            eng.tensor_tensor(dst_, src_, bc(mean.unsqueeze(2), shape), ALU.subtract)
            eng.drain()
            eng.tensor_tensor(tmp, dst_, dst_, ALU.mult)
            eng.drain()
            eng.tensor_reduce(var, tmp, AX.X, ALU.add).then_inc(var_sem, 1)
            eng.wait_ge(std_sem, v)
            eng.reciprocal(rstd, rstd)
            eng.drain()
            eng.tensor_tensor(dst_, dst_, bc(rstd.unsqueeze(2), shape), ALU.mult)
            eng.drain()

        def layer_norm_in_place(eng, y, tmp, shape, var_sem, std_sem, v, at):
            layer_norm(eng, y, y, shape, var_sem, std_sem, v, tmp=tmp, at=at)

        def deviation(eng, n, var_sem, std_sem, v, at=0):
            eng.wait_ge(var_sem, v)
            eng.activation(stat[:, 2, at:at + n], stat[:, 1, at:at + n], ACT.Sqrt, bias=eps[0:NP, 0:1],
                           scale=1.0 / H).then_inc(std_sem, 1)

        def own3(w):
            return big_b[:, :, :].rearrange("p a b -> p (a b)").bitcast(BF16)[:, 0:NB * PARTS * w]\
                .rearrange("p (b k c) -> p b k c", b=NB, k=PARTS)

        def split3(v, src_, out3, rest):
            v.tensor_copy(out3[:, :, 0, :], src_)
            v.drain()
            v.tensor_tensor(rest, src_, out3[:, :, 0, :], ALU.subtract)
            v.drain()
            v.tensor_copy(out3[:, :, 1, :], rest)
            v.drain()
            v.tensor_tensor(out3[:, :, 2, :], rest, out3[:, :, 1, :], ALU.subtract)
            v.drain()

        with nc.Block() as block:
            @block.sync
            def _(sp):
                sp.dma_start(key_i[0], src.rearrange("(p t) -> p t", p=NP)).then_inc(loaded, 16)
                sp.dma_start(key_i[1], dst.rearrange("(p t) -> p t", p=NP)).then_inc(loaded, 16)
                sp.dma_start(wt, weight.rearrange("(p t) -> p t", p=NP)).then_inc(loaded, 16)
                sp.dma_start(X[:, :, :], x.rearrange("(p b) c -> p b c", b=NB)).then_inc(loaded, 16)
                sp.dma_start(mult_sb[:, :], mult.rearrange("(p b) -> p b", b=NB)).then_inc(loaded, 16)
                sp.dma_start(z_sb[:, :], z.rearrange("(p b) -> p b", b=NB)).then_inc(loaded, 16)
                sp.dma_start(emb_sb[:, 0:EMB], emb).then_inc(loaded, 16)
                sp.dma_start(adapt_sb[:, :], adapt).then_inc(loaded, 16)
                sp.dma_start(F1W_sb[:, :], F1W).then_inc(loaded, 16)
                sp.dma_start(F1b_sb[:, :], F1b.rearrange("(p a) -> p a", a=1)).then_inc(loaded, 16)
                sp.dma_start(F2W_sb[0:H, :], F2W).then_inc(loaded, 16)
                sp.dma_start(F2W_sb[H:H + 1, :], F2b.rearrange("(a p) -> a p", a=1)).then_inc(loaded, 16)
                for k, v in enumerate((gn, bn, b1)):
                    sp.dma_start(gains_n[:, k * H:(k + 1) * H],
                                 v.rearrange("(a p) -> a p", a=1).to_broadcast([NP, H])).then_inc(loaded, 16)
                sp.wait_ge(fills, 1)
                for table, fill in fill_of:
                    sp.dma_start(table[FREE_G:NG, :, :].rearrange("g p c -> p g c"),
                                 fill[:, :, :].rearrange("p j c -> p (j c)").unsqueeze(1)
                                 .to_broadcast([P, NG - FREE_G, J * fill.shape[2]])).then_inc(filled, 16)
                sp.wait_ge(emb_s, 1)
                sp.dma_start(emb2_d, emb_sb[:, :]).then_inc(emb_out, 16)
                sp.wait_ge(emb_out, 16)
                for k in range(2):
                    sp.wait_ge(blk_made, k + 1)
                    sp.dma_start(blk_d[k].rearrange("(p j) -> p j", j=J), blk_g[:, :]).then_inc(blk_out, 16)
                    sp.wait_ge(blk_out, 16 * (k + 1))
                    sp.dma_start(blk_row[:, 1:NG + 1], blk_d[k].rearrange("(a n) -> a n", a=1)
                                 .to_broadcast([P, NG])).then_inc(blk_in, 16)
                sp.wait_ge(blk_in, 32)
                fill_last(sp, 0, 0, NB // 2)
                sp.wait_ge(filled_last, NB * 16)

            @block.gpsimd
            def _(pool):
                pool.memset(ident[:, :], 0.0).then_inc(consts, 1)
                pool.memset(ones[:, :], 1.0).then_inc(consts, 1)
                pool.iota(row_iota[:, :], pattern=[[1, P]], base=0, channel_multiplier=0,
                          allow_small_or_imprecise_dtypes=True).then_inc(consts, 1)
                pool.iota(blk_iota[:, :], pattern=[[1, NB]], base=0, channel_multiplier=0,
                          allow_small_or_imprecise_dtypes=True).then_inc(consts, 1)
                pool.iota(grp_iota[:, :], pattern=[[1, J]], base=0, channel_multiplier=J,
                          allow_small_or_imprecise_dtypes=True).then_inc(consts, 1)
                pool.wait_ge(consts, 5)
                pool.affine_select(out=ident[:, :], in_=ident[:, :], compare_op=ALU.not_equal, fill=1.0,
                                   base=0, pattern=[[-1, P]], channel_multiplier=1).then_inc(consts, 1)
                pool.affine_select(out=upper[:, :], in_=ones[:, :], compare_op=ALU.is_gt, fill=0.0,
                                   base=0, pattern=[[1, P]], channel_multiplier=-1).then_inc(consts, 1)
                pool.wait_ge(loaded, 16 * 15)
                pool.wait_ge(emb_out, 16)
                for b in range(NB):
                    pool.indirect_dma_start(
                        out=HA[:, b, 0:2 * EMB], out_offset=None, in_=emb2_d[:, :],
                        in_offset=bass.IndirectOffsetOnAxis(ap=z_sb[:, b:b + 1], axis=0)
                    ).then_inc(ready_emb, 16)
                pool.wait_ge(ready_emb, 16 * NB)

            @block.tensor
            def _(pe):
                pe.wait_ge(consts, 7)
                pe.wait_ge(loaded, 16 * 15)
                pe.transpose(p_x[0:EMB, 0:NELEM], emb_sb[:, 0:EMB], ident[0:NELEM, 0:NELEM]).then_inc(embT_p, 1)
                pe.wait_ge(embT_s, 1)
                pe.matmul(p_x[0:NELEM, 256:256 + EMB], embT[:, :], adapt_sb[:, :],
                          start=True, stop=True).then_inc(emb_p, 1)
                for k in range(2):
                    pe.wait_ge(counted, k + 1)
                    if k:
                        pe.wait_ge(taken, k)
                    pe.matmul(p_own[0:NP, 0:NB], upper[0:NP, 0:NP], cnt[:, :], start=True, stop=True)
                    pe.matmul(p_own[0:NP, 256:256 + NB], ones[0:NP, 0:NP], cnt[:, :], start=True,
                              stop=True).then_inc(summed, 1)

            @block.scalar
            def _(act):
                act.wait_ge(embT_p, 1)
                act.activation(embT[:, :], p_x[0:EMB, 0:NELEM], ACT.Copy).then_inc(embT_s, 1)
                act.wait_ge(emb_p, 1)
                act.activation(emb_sb[:, EMB:2 * EMB], p_x[0:NELEM, 256:256 + EMB], ACT.Copy).then_inc(emb_s, 1)
                act.wait_ge(blocked, 1)
                for b in range(1, NB):
                    act.activation(sign, blks[1], ACT.Sign, bias=minus_b[:, b:b + 1], accum_out=signs[:, b:b + 1])
                    act.drain()
                act.drain().then_inc(signed, 1)
                act.wait_ge(cos_in, 1)
                act.activation(cosw, cosw, ACT.Sin, bias=half_pi[0:NP, 0:1],
                               scale=-3.141592653589793 / 6.0).then_inc(cos_out, 1)
                act.wait_ge(blk_made, 1)
                fill_last(act, 0, NB // 2, NB)
                deviation(act, NB, var1, std1, 1)

            @block.vector
            def _(v):
                v.memset(fill_r[:, :, 0:C_SRC], 0.0)
                v.memset(fill_r[:, :, C_SRC:C_SRC + 1], -1.0)
                v.memset(fill_r[:, :, C_CUT:C_DST + 1], 0.0)
                v.memset(fill_r[:, :, RW:RG], 0.0)
                v.memset(fill_r[:, :, C_POS2:RW].bitcast(I32), 2 * NG * EG)
                v.memset(fill_m[:, :, 0:PARTS * H], 0.0)
                v.memset(fill_m[:, :, PARTS * H:MW], -1.0).then_inc(fills, 1)
                v.memset(zero_b, 0.0)
                v.memset(eps[:, :], 1.0e-5)
                for s in range(2):
                    v.memset(neg_t[s][:, :], 1.0)
                v.memset(half_pi[:, :], 3.141592653589793 / 2.0)
                for s in range(U):
                    v.memset(arg[s][:, :], 0.0)
                    v.memset(smax[s][:, :], -BIG)
                    v.memset(acc[s][:, :], 0.0)
                v.memset(blk_row[:, 0:1], -1.0)
                v.wait_ge(consts, 7)
                v.wait_ge(loaded, 16 * 15)
                v.scalar_tensor_tensor(out=cosw, in0=wt, scalar=-1.0, in1=wt, op0=ALU.mult, op1=ALU.max)
                v.drain()
                v.tensor_scalar(cosw, cosw, 6.0, None, ALU.min).then_inc(cos_in, 1)
                v.tensor_scalar(minus_b[:, :], blk_iota[0:NP, :], -1.0, 0.5, ALU.mult, ALU.add)
                v.memset(signs[:, 0:1], float(EC))
                v.memset(signs[:, NB:NB + 1], -float(EC))
                for k in (1, 0):
                    v.tensor_copy(keyf, key_i[k])
                    v.drain()
                    v.tensor_scalar(mask, keyf, 1.0 / NB, 0.5 / NB - 0.5, ALU.mult, ALU.add)
                    v.drain()
                    where = metaf[:, :, 0] if k == 0 else metaf[:, :, 2]
                    v.tensor_scalar(where, mask, ROUND, ROUND, ALU.add, ALU.subtract)
                    v.drain()
                    v.scalar_tensor_tensor(out=blks[k], in0=where, scalar=-float(NB), in1=keyf,
                                           op0=ALU.mult, op1=ALU.add)
                    v.drain().then_inc(blocked, 1)
                for k in range(2):
                    if k == 0:
                        for b in range(NB):
                            v.tensor_scalar(mask, blks[0], float(b), 0.0, ALU.is_equal, ALU.add,
                                            accum_out=cnt[:, b:b + 1])
                            v.drain()
                    else:
                        v.wait_ge(signed, 1)
                        v.tensor_tensor(cnt[:, :], signs[:, 0:NB], signs[:, 1:NB + 1], ALU.subtract)
                        v.drain()
                        v.tensor_scalar(cnt[:, :], cnt[:, :], 0.5, None, ALU.mult)
                    v.drain().then_inc(counted, 1)
                    v.wait_ge(summed, k + 1)
                    v.tensor_scalar(groups[:, :], p_own[0:NP, 256:256 + NB], 1.0 / EG, 0.5 - 0.5 / EG,
                                    ALU.mult, ALU.add)
                    v.drain()
                    v.tensor_scalar(groups[:, :], groups[:, :], ROUND, ROUND, ALU.add, ALU.subtract)
                    v.drain()
                    v.tensor_scalar(groups[:, :], groups[:, :], 1.0, None, ALU.max)
                    v.drain()
                    v.tensor_tensor_scan(gend[:, :], groups[:, :], zero_b, 0.0, ALU.add, ALU.add)
                    v.drain()
                    v.tensor_tensor(first[:, k, :], gend[:, :], groups[:, :], ALU.subtract)
                    v.drain()
                    v.tensor_scalar(first[:, k, :], first[:, k, :], float(EG), None, ALU.mult)
                    v.drain()
                    v.tensor_tensor(first[:, k, :], first[:, k, :], p_own[0:NP, 0:NB], ALU.add).then_inc(taken, 1)
                    v.tensor_scalar(last_i[k][:, :], gend[0:1, :], -1.0, None, ALU.add)
                    v.tensor_tensor(cmp_g[:, :, :], bc(gend[0:NG // J, :].unsqueeze(1), [NG // J, J, NB]),
                                    bc(grp_iota[:, :].unsqueeze(2), [NG // J, J, NB]), ALU.is_le)
                    v.drain()
                    if k:
                        v.wait_ge(blk_out, 16)
                    v.tensor_reduce(blk_g[:, :], cmp_g[:, :, :], AX.X, ALU.add)
                    v.drain()
                    v.tensor_scalar(blk_g[:, :], blk_g[:, :], float(NB - 1), None, ALU.min).then_inc(blk_made, 1)
                    v.wait_ge(blk_in, 16 * (k + 1))
                    v.tensor_copy(blk_i[k][:, :], blk_row[0:1, 1:NG + 1])
                    v.tensor_tensor(keep[k][:, :], blk_row[:, 1:NG + 1], blk_row[:, 0:NG], ALU.is_equal)
                    v.drain()
                v.tensor_scalar(fresh[:, :], keep[0][:, :], -1.0, 2.0 * BIG, ALU.add, ALU.mult)
                v.tensor_copy(metai[:, :, 0], key_i[1])
                v.wait_ge(cos_out, 1)
                v.tensor_scalar(metaf[:, :, 1], cosw, 1.0, 0.5, ALU.add, ALU.mult)
                v.drain()
                layer_norm(v, big_a[:, :, 0:H], X[:, :, :], [NP, NB, H], var1, std1, 1, tmp=big_b[:, :, 0:H])
                g_rows = row_out[:, 0:NB * GW].rearrange("p (b c) -> p b c", b=NB)
                v.tensor_scalar(g_rows[:, :, 0:H], big_a[:, :, 0:H], 0.0, None, ALU.max)
                v.wait_ge(ready_emb, 16 * NB)
                v.tensor_copy(g_rows[:, :, H:H + EMB], HA[:, :, EMB:2 * EMB])
                v.tensor_copy(g_rows[:, :, H + EMB:GW], mult_sb[:, :].unsqueeze(2))
                v.tensor_copy(identb[:, :], ident[:, :])
                split3(v, HA[:, :, 0:EMB], own3(EMB), big_a[:, :, 0:EMB])
                v.tensor_copy(HA[:, :, 0:H], g_rows[:, :, 0:H])
                v.drain()

        tabs_out = sem("tabs_out")
        slot_in = [sem(f"slot_in{s}") for s in range(U)]
        meta_in = sem("meta_in")
        sent = [sem(f"sent{s}") for s in range(U)]
        hot = sem("hot")
        hist = sem("hist")
        hist_n = sem("hist_n")
        hot_r = [oh[s][:, :, :] for s in range(2)]
        hot_b = [ohT[s][0:NP, 0:J * NB].rearrange("p (j b) -> p j b", j=J) for s in range(4)]
        next_pos = flat_a[:, 0:16 * NB].rearrange("p (s k j b) -> p s k j b", s=2, k=2, j=J)
        picked = flat_a[:, 16 * NB:24 * NB].rearrange("p (k j b) -> p k j b", k=2, j=J)
        place = flat_a[:, 24 * NB:24 * NB + 4 * J].rearrange("p (s k j) -> p s k j", s=2, k=2)
        placed = sem("placed")
        s_eaT_p = sem("s_eaT_p")
        s_eaT = sem("s_eaT")
        s_f1 = sem("s_f1")
        s_silu = sem("s_silu")
        s_gate_p = sem("s_gate_p")
        s_gate = sem("s_gate")
        ea_p = ea.rearrange("(p t) c -> p t c", p=NP)
        eaT = [masked_t[s][0:RBF, 0:J * NP] for s in range(2)]
        silu = [neg_t[s][:, 0:J * NP] for s in range(2)]
        gate_bank = [p_own, p_mg]
        STEPS = EC // J

        with nc.Block() as block:
            @block.sync
            def _(sp):
                sp.dma_start(gate_d.rearrange("(p b) c -> p (b c)", b=NB), row_out[:, 0:NB * GW]).then_inc(tabs_out, 16)
                sp.dma_start(ei_d.rearrange("b p c -> p b c"),
                             own3(EMB).rearrange("p b k c -> p b (k c)")).then_inc(tabs_out, 16)

                def body(i, u):
                    if at_least(i, U):
                        sp.wait_ge(sent[u], before_step(64, i, u))
                    sp.dma_start(rec_w[u][0:NP, :, 0:RBF], ea_p[:, ds(i * J, J), :]).then_inc(slot_in[u], 16)
                run_steps(sp, body, STEPS)
                sp.wait_ge(tabs_out, 32)

            @block.vector
            def _(v):
                def rows_hot(i, u):
                    if at_least(i, 2):
                        v.wait_ge(hist, i - 1)
                    v.tensor_tensor(hot_r[u % 2][0:NP], bc(row_iota[0:NP, :].unsqueeze(1), [NP, J, P]),
                                    bc(metaf[:, ds(i * J, J), 2:3], [NP, J, P]), ALU.is_equal)

                def block_hot(i, u, k):
                    return v.tensor_tensor(hot_b[2 * k + u % 2], bc(blk_iota[0:NP, :].unsqueeze(1), [NP, J, NB]),
                                           bc(blks[k][:, ds(i * J, J)].unsqueeze(2), [NP, J, NB]), ALU.is_equal)

                def advance(i, u, j):
                    s = u % 2
                    if at_least(i, 1) or j:
                        v.wait_ge(placed, 6 * i + j - (2 if j == 0 else 0))
                    for k in range(2):
                        to = next_pos[:, s, k, j + 1, :] if j + 1 < J else next_pos[:, 1 - s, k, 0, :]
                        ins = v.tensor_tensor(to, next_pos[:, s, k, j, :], hot_b[2 * k + s][:, j, :], ALU.add)
                    ins.then_inc(placed, 1)

                def body(i, u):
                    s = u % 2
                    more = before(i + 1, STEPS)
                    advance(i, u, 0)
                    if more:
                        rows_hot(i + 1, (u + 1) % U)
                    advance(i, u, 1)
                    if more:
                        block_hot(i + 1, (u + 1) % U, 0)
                    advance(i, u, 2)
                    if more:
                        block_hot(i + 1, (u + 1) % U, 1).then_inc(hot, 1)
                    advance(i, u, 3)
                    if at_least(i, U):
                        v.wait_ge(sent[u], before_step(64, i, u))
                        v.sem_inc(held, 1)
                    v.tensor_copy(rec_w[u][0:NP, :, C_DST:C_DST + 1].bitcast(I32), metai[:, ds(i * J, J), 0:1])
                    v.wait_ge(placed, 6 * i + 3)
                    for k in range(2):
                        ins = v.tensor_tensor(picked[:, k], next_pos[:, s, k], hot_b[2 * k + s], ALU.mult)
                    ins.then_inc(placed, 1)
                    v.tensor_copy(rec_w[u][0:NP, :, C_SRC:C_DST], metaf[:, ds(i * J, J), :])
                    v.wait_ge(s_gate_p, i + 1)
                    v.tensor_copy(rec_w[u][0:NP, :, RW:RG], gate_bank[s][0:NP, 0:J * H]
                                  .rearrange("p (j c) -> p j c", j=J)).then_inc(s_gate, 1)
                    v.wait_ge(placed, 6 * i + 5)
                    v.tensor_reduce(place[:, s], picked, AX.X, ALU.add).then_inc(placed, 1)
                    v.wait_ge(placed, 6 * i + 6)
                    v.tensor_copy(rec_w[u][0:NP, :, C_POS2:RW].bitcast(I32), place[:, s, 1, :].unsqueeze(2))
                    v.tensor_copy(idx[u][:, :], place[:, s, 0, :]).then_inc(meta_in, 1)

                v.tensor_copy(next_pos[:, 0, :, 0, :], first[:, :, :])
                rows_hot(0, 0)
                block_hot(0, 0, 0)
                block_hot(0, 0, 1).then_inc(hot, 1)
                v.drain()
                run_steps(v, body, STEPS)
                v.wait_ge(hist, STEPS)
                v.tensor_scalar(dinv[:, :], p_x[0:NP, 0:NB], 1.0, None, ALU.add)
                v.drain().then_inc(hist_n, 1)
                v.wait_ge(hist_n, 2)
                v.reciprocal(dinv[:, :], dinv[:, :])
                v.drain()

            @block.scalar
            def _(act):
                def body(i, u):
                    s = u % 2
                    act.wait_ge(s_eaT_p, i + 1)
                    if at_least(i, 2):
                        act.wait_ge(s_f1, i - 1)
                    act.activation(eaT[s].rearrange("p (j e) -> p j e", j=J),
                                   p_mT[0][0:RBF, :].rearrange("p (j e) -> p j e", j=J)[:, :, 0:NP],
                                   ACT.Copy).then_inc(s_eaT, 1)
                    act.wait_ge(s_f1, i + 1)
                    if at_least(i, 2):
                        act.wait_ge(s_gate_p, i - 1)
                    act.activation(silu[s][0:H, :], p_mT[1][0:H, 0:J * NP], ACT.Silu,
                                   bias=F1b_sb[:, 0:1]).then_inc(s_silu, 1)
                run_steps(act, body, STEPS)
                act.wait_ge(hist_n, 1)
                act.activation(dinv[:, :], dinv[:, :], ACT.Sqrt)
                act.drain()
                act.activation(logm[:, :], mult_sb[:, :], ACT.Copy, bias=-1.0)
                act.drain()
                act.activation(logm[:, :], logm[:, :], ACT.Relu)
                act.drain()
                act.activation(logm[:, :], logm[:, :], ACT.Ln, bias=ones[0:NP, 0:1])
                act.drain().then_inc(hist_n, 1)

            @block.tensor
            def _(pe):
                def front(i, u):
                    s = u % 2
                    pe.wait_ge(slot_in[u], after_step(16, i, u))
                    if at_least(i, 1):
                        pe.wait_ge(s_eaT, i)
                    pe.sem_inc(held, 1)
                    for j in range(J):
                        mm = pe.transpose(p_mT[0][0:RBF, j * P:j * P + NP], rec_w[u][0:NP, j, 0:RBF],
                                          ident[0:NP, 0:NP])
                    mm.then_inc(s_eaT_p, 1)

                def hidden(i, u):
                    pe.wait_ge(s_eaT, i + 1)
                    if at_least(i, 1):
                        pe.wait_ge(s_silu, i)
                    pe.sem_inc(held, 1)
                    pe.matmul(p_mT[1][0:H, 0:J * NP], F1W_sb[:, :], eaT[u % 2], start=True,
                              stop=True).then_inc(s_f1, 1)

                def gates(i, u):
                    s = u % 2
                    pe.wait_ge(s_silu, i + 1)
                    if at_least(i, 2):
                        pe.wait_ge(s_gate, i - 1)
                    pe.sem_inc(held, 1)
                    for j in range(J):
                        mm = pe.matmul(gate_bank[s][0:NP, j * H:(j + 1) * H], silu[s][0:H + 1, j * NP:(j + 1) * NP],
                                       F2W_sb[:, :], start=True, stop=True)
                    mm.then_inc(s_gate_p, 1)

                def count(i, u):
                    pe.wait_ge(hot, i + 1)
                    for j in range(J):
                        mm = pe.matmul(p_x[:, 0:NB], hot_r[u % 2][0:NP, j, :], hot_b[2 + u % 2][:, j, :],
                                       start=isinstance(i, int) and i == 0 and j == 0,
                                       stop=isinstance(i, int) and i == STEPS - 1 and j == J - 1,
                                       skip_group_check=True)
                    mm.then_inc(hist, 1)

                def body(i, u):
                    if before(i + 1, STEPS):
                        front(i + 1, (u + 1) % U)
                    gates(i, u)
                    if before(i + 1, STEPS):
                        hidden(i + 1, (u + 1) % U)
                    count(i, u)
                front(0, 0)
                hidden(0, 0)
                run_steps(pe, body, STEPS)

            @block.gpsimd
            def _(pool):
                def body(i, u):
                    pool.wait_ge(slot_in[u], after_step(16, i, u))
                    pool.wait_ge(meta_in, i + 1)
                    pool.wait_ge(s_gate, i + 1)
                    pool.sem_inc(held, 1)
                    for j in range(J):
                        pool.indirect_dma_start(
                            out=rec_d[:, :], out_offset=bass.IndirectOffsetOnAxis(ap=idx[u][:, j:j + 1], axis=0),
                            in_=rec_w[u][0:NP, j, :], in_offset=None).then_inc(sent[u], 16)
                run_steps(pool, body, STEPS)
                for u in range(U):
                    pool.wait_ge(sent[u], before_step(64, STEPS, 0))

        def keep_sums(sp, i, u, past, made, base):
            sp.wait_ge(made, base + i + 1)
            sp.sem_inc(held, 1)
            b = sp.value_load(blk_i[0][0:1, ds(i, 1)], min_val=0, max_val=NB - 1)
            sp.wait_ge(stored[(u - 1) % U], after_step(16, past + U + i - 1, (u - 1) % U))
            sp.sem_inc(held, 1)
            sp.dma_start(agg_in[:, ds(b, 1), :].rearrange("p a c -> p (a c)"), acc[u][:, :]).then_inc(stored[u], 16)

        def sums_of_blocks(eng, k, first_b, last_b, base, sums_in, accs, total):
            for s in range(U):
                eng.wait_ge(accs[s], before_step(16, base + total, 0))
            eng.sem_inc(held, 1)
            with eng.Fori(first_b, last_b) as b:
                g = eng.value_load(last_i[k][0:1, ds(b, 1)], min_val=0, max_val=NG - 1)
                eng.dma_start(agg_in[:, ds(b, 1), :], acc_d[ds(g, 1), :, :]
                              .rearrange("a p c -> p a c")).then_inc(sums_in, 16)

        def one_hot(v, u, tile, col, ready, columns=range(J)):
            for j in columns:
                ins = v.tensor_scalar(oh[u % S][:, j, :], row_iota[:, :], tile[:, j, col:col + 1], None,
                                      ALU.is_equal)
            ins.then_inc(ready, 1)

        def gather_rows(pool, table, u, width, tile, arrived):
            for j in range(J):
                pool.indirect_dma_start(
                    out=row[u][:, j, 0:width], out_offset=None, in_=table,
                    in_offset=bass.IndirectOffsetOnAxis(ap=tile[:, j, C_DST:C_DST + 1].bitcast(I32), axis=0)
                ).then_inc(arrived[u], 16)

        def flip_one_hot(pe, u, flipped_p):
            for j in range(J):
                mm = pe.transpose(p_ohT[u % 2][:, j * P:(j + 1) * P], oh[u % S][:, j, :], identb[:, :])
            mm.then_inc(flipped_p, 1)

        def gather_own(pe, u, bank, width, done):
            for j in range(J):
                for k in range(PARTS):
                    mm = pe.matmul(bank[:, j * width:(j + 1) * width], ohT[u % S][0:NP, j * P:(j + 1) * P],
                                   own[u][:, k * width:(k + 1) * width], start=(k == 0), stop=(k == PARTS - 1))
            mm.then_inc(done, 1)

        def sum_group(pe, u, rhs, done):
            for j in range(J):
                mm = pe.matmul(p_agg[:, 0:VW], ohf[u % S][:, j, :], rhs[:, j, :], start=(j == 0), stop=(j == J - 1))
            mm.then_inc(done, 1)

        def load_group(sp, i, u, base, tile, group_rows, own_tab, width, arrived, used):
            if at_least(i, U):
                sp.wait_ge(used, base + i - U + 1)
                sp.sem_inc(held, 1)
            b = sp.value_load(blk_i[0][0:1, ds(i, 1)], min_val=0, max_val=NB - 1)
            sp.dma_start(tile, group_rows).then_inc(arrived[u], 16)
            sp.dma_start(own[u][:, 0:width], own_tab[ds(b, 1), :, 0:width]
                         .rearrange("a p c -> p (a c)")).then_inc(arrived[u], 16)

        rec_in = [sem(f"rec_in{s}") for s in range(U)]
        row_in = [sem(f"row_in{s}") for s in range(U)]
        stored = [sem(f"stored{s}") for s in range(U)]
        PAST = (1 + LAYERS) * NG

        g_hot = sem("g_hot")
        g_ohf = sem("g_ohf")
        g_flip_p = sem("g_flip_p")
        g_flip = sem("g_flip")
        g_own = sem("g_own")
        g_vals = sem("g_vals")
        g_agg = sem("g_agg")
        g_acc = sem("g_acc")
        g_lean = [sem(f"g_lean{s}") for s in range(U)]
        g_var = sem("g_var")
        g_std = sem("g_std")

        with nc.Block() as block:
            @block.sync
            def _(sp):
                def body(i, u):
                    if at_least(i, U):
                        sp.wait_ge(g_lean[u], before_step(16, i, u))
                        sp.sem_inc(held, 1)
                    load_group(sp, i, u, 0, rec_t[u][:, :], rec_g[ds(i, 1), :, :].rearrange("a p c -> p (a c)"),
                               ei_d, PARTS * EMB, rec_in, g_vals)
                    if at_least(i, U):
                        keep_sums(sp, i - U, u, 0, g_acc, 0)
                for s in range(U):
                    sp.sem_inc(stored[s], 16)
                run_steps(sp, body, NG)
                for i in range(NG - U, NG):
                    keep_sums(sp, i, i % U, 0, g_acc, 0)

            @block.gpsimd
            def _(pool):
                def body(i, u):
                    pool.wait_ge(rec_in[u], after_step(32, i, u))
                    if at_least(i, U):
                        pool.wait_ge(g_vals, i - U + 1)
                    pool.sem_inc(held, 1)
                    gather_rows(pool, gate_d[:, :], u, GW, rec_w[u], row_in)
                run_steps(pool, body, NG)

            @block.vector
            def _(v):
                def hots(i, u):
                    v.wait_ge(rec_in[u], after_step(32, i, u))
                    one_hot(v, u, rec_w[u], C_SRC, g_hot)

                def weights(i, u):
                    s = u % 2
                    v.wait_ge(row_in[u], after_step(64, i, u))
                    v.tensor_tensor(arg[u][:, 0:J].unsqueeze(2), rec_w[u][:, :, C_CUT:C_CUT + 1],
                                    row[u][:, :, H + EMB:GW], ALU.mult)
                    v.wait_ge(g_own, i + 1)
                    v.tensor_tensor(prod[s][:, :, 0:EMB], row[u][:, :, H:H + EMB],
                                    own_bank[s][:, 0:J * EMB].rearrange("p (j c) -> p j c", j=J), ALU.mult)
                    v.drain()
                    v.tensor_reduce(score[u][:, :], prod[s][:, :, 0:EMB], AX.X, ALU.add)
                    v.tensor_tensor(row[u][:, :, 0:H], row[u][:, :, 0:H],
                                    bc(arg[u][:, 0:J].unsqueeze(2), [P, J, H]), ALU.mult)
                    v.drain()
                    v.tensor_tensor(prod[s][:, :, 0:H], rec_w[u][:, :, RW:RG],
                                    bc(score[u][:, :].unsqueeze(2), [P, J, H]), ALU.add)
                    v.drain()
                    v.tensor_copy(vals[s][:, :, H:VW], row[u][:, :, H + EMB:GW])
                    v.tensor_tensor(vals[s][:, :, 0:H], prod[s][:, :, 0:H], row[u][:, :, 0:H],
                                    ALU.mult).then_inc(g_vals, 1)

                def sums(i, u):
                    v.wait_ge(g_agg, i + 1)
                    if at_least(i, U):
                        v.wait_ge(stored[u], before_step(16, U + i, u))
                    v.scalar_tensor_tensor(out=acc[u][:, :], in0=acc[(u - 1) % U][:, :],
                                           scalar=keep[0][0:NP, ds(i, 1)], in1=p_agg[0:NP, 0:VW],
                                           op0=ALU.mult, op1=ALU.add).then_inc(g_acc, 1)

                def body(i, u):
                    if before(i + 1, NG):
                        hots(i + 1, (u + 1) % U)
                    weights(i, u)
                    if at_least(i, 1):
                        sums(i - 1, (u - 1) % U)
                hots(0, 0)
                run_steps(v, body, NG)
                sums(NG - 1, (NG - 1) % U)
                v.wait_ge(stored[U - 1], before_step(16, U + NG, 0))
                v.tensor_scalar(stat[:, 0, 0:NB], agg_in[:, :, H], 1.0e-8, None, ALU.max)
                v.drain()
                v.reciprocal(stat[:, 0, 0:NB], stat[:, 0, 0:NB])
                v.drain()
                v.tensor_tensor(big_a[:, :, 0:H], agg_in[:, :, 0:H], bc(stat[:, 0, 0:NB].unsqueeze(2), [NP, NB, H]), ALU.mult)
                v.drain()
                v.tensor_tensor(big_a[:, :, 0:H], big_a[:, :, 0:H], HA[:, :, 0:H], ALU.add)
                v.drain()
                layer_norm(v, HA[:, :, 0:H], big_a[:, :, 0:H], [NP, NB, H], g_var, g_std, 1, tmp=big_b[:, :, 0:H])
                v.tensor_tensor(HA[:, :, 0:H], HA[:, :, 0:H], bc(gains_n[:, 0:H].unsqueeze(1), [NP, NB, H]), ALU.mult)
                v.drain()
                v.tensor_tensor(HA[:, :, 0:H], HA[:, :, 0:H], bc(gains_n[:, H:2 * H].unsqueeze(1), [NP, NB, H]), ALU.add)
                v.drain()

            @block.scalar
            def _(act):
                def turned(i, u):
                    s = u % 2
                    act.wait_ge(g_hot, i + 1)
                    if at_least(i, S):
                        act.wait_ge(g_agg, i - S + 1)
                    act.activation(ohf[u % S][:, :, :], oh[u % S][:, :, :], ACT.Copy).then_inc(g_ohf, 1)
                    act.wait_ge(g_flip_p, i + 1)
                    if at_least(i, S):
                        act.wait_ge(g_own, i - S + 1)
                    act.activation(ohT[u % S][:, :], p_ohT[u % 2], ACT.Copy).then_inc(g_flip, 1)

                def body(i, u):
                    act.wait_ge(rec_in[u], after_step(32, i, u))
                    act.dma_start(lean_d[ds(i, 1), :, :].rearrange("a p (j c) -> p (a j) c", j=J),
                                  rec_w[u][:, :, 0:RW]).then_inc(g_lean[u], 16)
                    if before(i + 1, NG):
                        turned(i + 1, (u + 1) % U)
                turned(0, 0)
                run_steps(act, body, NG)
                for s in range(U):
                    act.wait_ge(g_lean[s], before_step(16, NG, 0))
                deviation(act, NB, g_var, g_std, 1)

            @block.tensor
            def _(pe):
                def front(i, u):
                    pe.wait_ge(g_hot, i + 1)
                    if at_least(i, 2):
                        pe.wait_ge(g_flip, i - 1)
                    flip_one_hot(pe, u, g_flip_p)
                    if at_least(i, 2):
                        pe.wait_ge(g_vals, i - 1)
                    pe.wait_ge(g_flip, i + 1)
                    gather_own(pe, u, own_bank[u % 2], EMB, g_own)

                def sums(i, u):
                    pe.wait_ge(g_vals, i + 1)
                    pe.wait_ge(g_ohf, i + 1)
                    if at_least(i, 1):
                        pe.wait_ge(g_acc, i)
                    sum_group(pe, u, vals[u % 2], g_agg)

                def body(i, u):
                    if before(i + 1, NG):
                        front(i + 1, (u + 1) % U)
                    sums(i, u)
                front(0, 0)
                run_steps(pe, body, NG)

        w_in = sem("w_in")
        wmT_p = sem("wmT_p")
        wmT_s = sem("wmT_s")
        wmu_p = sem("wmu_p")
        wmu_s = sem("wmu_s")
        wmu_in = sem("wmu_in")
        n_h = sem("n_h")
        t_p = sem("t_p")
        t_s = sem("t_s")
        y_p = sem("y_p")
        y_s = sem("y_s")
        n_var = sem("n_var")
        n_std = sem("n_std")
        n_key = sem("n_key")
        n_tab = sem("n_tab")
        n_out = sem("n_out")
        a_agg = sem("a_agg")
        l_hot = sem("l_hot")
        l_flip_p = sem("l_flip_p")
        l_flip = sem("l_flip")
        l_neg = sem("l_neg")
        l_ohf = sem("l_ohf")
        l_own = sem("l_own")
        l_key = sem("l_key")
        l_prod = sem("l_prod")
        l_score = sem("l_score")
        l_mask = sem("l_mask")
        l_gmax = sem("l_gmax")
        l_smax = sem("l_smax")
        l_hi = sem("l_hi")
        l_mid = sem("l_mid")
        l_parts = sem("l_parts")
        l_msum = sem("l_msum")
        l_shift = sem("l_shift")
        l_mT = sem("l_mT")
        l_mg = sem("l_mg")
        l_arg = sem("l_arg")
        l_es = sem("l_es")
        l_vals = sem("l_vals")
        l_agg = sem("l_agg")
        l_acc = sem("l_acc")

        t_banks = [(p_t[0], p_t[1]), (p_own, p_mg)]

        def dense_pe(pe, n, chunks, src_, k, w, m):
            c0, c1 = chunks
            def flip(c):
                if c >= c0 + 2:
                    pe.wait_ge(t_s, n + c - 1)
                    pe.sem_inc(held, 1)
                for q in range(CH):
                    bank = t_banks[c % 2][q // 4]
                    mm = pe.transpose(bank[0:k, (q % 4) * P:(q % 4) * P + NP], src_(c * CH + q), ident[0:NP, 0:NP])
                mm.then_inc(t_p, 1)
            if c0:
                pe.wait_ge(y_s, n + c0)
                pe.sem_inc(held, 1)
            flip(c0)
            for c in range(c0, c1):
                if c + 1 < c1:
                    flip(c + 1)
                pe.wait_ge(t_s, n + c + 1)
                if c >= c0 + 2:
                    pe.wait_ge(y_s, n + c - 1)
                pe.sem_inc(held, 1)
                for q in range(CH):
                    mm = pe.matmul(p_mT[c % 2][0:NP, q * m:(q + 1) * m], xT[c % 2][0:k, q * P:q * P + NP], w,
                                   start=True, stop=True)
                mm.then_inc(y_p, 1)

        def dense_act(act, n, chunks, k, m, dst_, then=None):
            c0, c1 = chunks
            def turned(c):
                act.wait_ge(t_p, n + c + 1)
                if c >= c0 + 2:
                    act.wait_ge(y_p, n + c - 1)
                act.activation(xT[c % 2][0:k, 0:4 * P].rearrange("p (q e) -> p q e", q=4)[:, :, 0:NP],
                               t_banks[c % 2][0][0:k, :].rearrange("p (q e) -> p q e", q=4)[:, :, 0:NP], ACT.Copy)
                act.activation(xT[c % 2][0:k, 4 * P:4 * P + NP], t_banks[c % 2][1][0:k, 0:NP],
                               ACT.Copy).then_inc(t_s, 1)
            turned(c0)
            for c in range(c0, c1):
                if c + 1 < c1:
                    turned(c + 1)
                act.wait_ge(y_p, n + c + 1)
                act.activation(dst_(c), p_mT[c % 2][0:NP, 0:CH * m].rearrange("p (q m) -> p q m", m=m),
                               ACT.Copy).then_inc(y_s, 1)
                if then and c == then[0]:
                    then[1]()

        kh = row_out[:, :].rearrange("p (b c) -> p b c", b=NB)
        HB, HC = NB // 2, NC_ // 2
        HALVES = [(slice(q * HB, (q + 1) * HB), (q * HC, (q + 1) * HC)) for q in range(2)]
        norm_tmp = agg_in[:, :, :].rearrange("p a b -> p (a b)")[:, 0:HB * 2 * H].rearrange("p (b c) -> p b c", b=HB)
        w_end = sem("w_end")

        with nc.Block() as block:
            @block.sync
            def _(sp):
                with sp.Fori(0, LAYERS) as l:
                    base = l * NG
                    past = base + NG
                    for k, a in enumerate((gq, gk, bq, bk)):
                        sp.dma_start(gains[:, k * H:(k + 1) * H], a[ds(l, 1), :].to_broadcast([NP, H])).then_inc(w_in, 16)
                    sp.dma_start(wqk[:, 0:H], Wq[ds(l, 1), :, :].rearrange("a p c -> p (a c)")).then_inc(w_in, 16)
                    sp.dma_start(wqk[:, H:2 * H], Wk[ds(l, 1), :, :].rearrange("a p c -> p (a c)")).then_inc(w_in, 16)
                    sp.wait_ge(n_h, 2 * l + 2)
                    sp.sem_inc(held, 1)
                    for k, a in enumerate((go, bo)):
                        sp.dma_start(gains[:, (4 + k) * H:(5 + k) * H], a[ds(l, 1), :].to_broadcast([NP, H])).then_inc(w_end, 16)
                    sp.dma_start(wm[:, :], Wm[ds(l, 1), :, :].rearrange("a p c -> p (a c)")).then_inc(w_end, 16)
                    sp.dma_start(wub[:, :], Wu[ds(l, 1), H:2 * H, :].rearrange("a p c -> p (a c)")).then_inc(w_end, 16)
                    sp.dma_start(wu[0:H, :], Wu[ds(l, 1), 0:H, :].rearrange("a p c -> p (a c)")).then_inc(w_end, 16)
                    for q, (half, _) in enumerate(HALVES):
                        sp.wait_ge(n_key, 2 * l + q + 1)
                        sp.sem_inc(held, 1)
                        sp.dma_start(kh_d.rearrange("(p b) c -> p b c", b=NB)[:, half, :], kh[:, half, :]).then_inc(n_out, 16)
                        sp.wait_ge(n_tab, 2 * l + q + 1)
                        sp.sem_inc(held, 1)
                        sp.dma_start(own_d.rearrange("b p c -> p b c")[:, half, :],
                                     own3(QW)[:, half].rearrange("p b k c -> p b (k c)")).then_inc(n_out, 16)
                    sp.wait_ge(wmu_s, l + 1)
                    sp.dma_start(wu[H:2 * H, :], wmu[:, :]).then_inc(wmu_in, 16)
                    sp.wait_ge(n_out, l * 64 + 64)
                    sp.sem_inc(held, 1)

                    def body(i, u):
                        load_group(sp, i, u, base, rec_t[u][:, 0:J * RW],
                                   lean_d[ds(i, 1), :, :].rearrange("a p c -> p (a c)"),
                                   own_d, PARTS * QW, rec_in, l_prod)
                        if at_least(i, U):
                            keep_sums(sp, i - U, u, past, l_acc, base)
                    run_steps(sp, body, NG)
                    for i in range(NG - U, NG):
                        keep_sums(sp, i, i % U, past, l_acc, base)

            @block.gpsimd
            def _(pool):
                with pool.Fori(0, LAYERS) as l:
                    base = l * NG
                    past = base + NG
                    pool.wait_ge(n_out, l * 64 + 64)

                    def body(i, u):
                        pool.wait_ge(rec_in[u], after_step(32, past + i, u))
                        if at_least(i, U):
                            pool.wait_ge(l_vals, base + i - U + 1)
                        pool.sem_inc(held, 1)
                        gather_rows(pool, kh_d[:, :], u, KW, rec[u], row_in)
                    run_steps(pool, body, NG)

            @block.vector
            def _(v):
                v.memset(own_out[:, :, H:QW], 1.0)
                v.memset(kh[:, :, 2 * H + 1:KW], 1.0)
                v.tensor_copy(kh[:, :, H:H + 1], logm[:, :].unsqueeze(2))
                v.drain().then_inc(n_h, 2)
                v.drain().then_inc(n_var, 1)
                with v.Fori(0, LAYERS) as l:
                    base = l * NG
                    past = base + NG
                    v.wait_ge(w_in, l * 96 + 96)
                    for q, (half, (_, c1)) in enumerate(HALVES):
                        v.wait_ge(y_s, l * 2 * NC_ + c1)
                        v.tensor_copy(kh[:, half, H + 1:2 * H + 1], HA[:, half, 0:H])
                        layer_norm_in_place(v, big_a[:, half, :].rearrange("p b (a c) -> p (b a) c", a=2),
                                            norm_tmp.rearrange("p b (a c) -> p (b a) c", a=2),
                                            [NP, NB, H], n_var, n_std, 4 * l + 2 + q, q * NB)
                        wide, thin = [NP, HB, 2 * H], [NP, HB, H]
                        v.tensor_tensor(big_a[:, half, :], big_a[:, half, :], bc(gains[:, 0:2 * H].unsqueeze(1), wide), ALU.mult)
                        v.drain()
                        v.tensor_tensor(kh[:, half, 0:H], big_a[:, half, H:2 * H], bc(gains[:, 3 * H:4 * H].unsqueeze(1), thin), ALU.add).then_inc(n_key, 1)
                        v.tensor_tensor(own_out[:, half, 0:H], big_a[:, half, 0:H], bc(gains[:, 2 * H:3 * H].unsqueeze(1), thin), ALU.add)
                        v.drain()
                        split3(v, own_out[:, half, :], own3(QW)[:, half], big_a[:, half, 0:QW])
                        v.drain().then_inc(n_tab, 1)

                    def hots(i, u):
                        v.wait_ge(rec_in[u], after_step(32, past + i, u))
                        one_hot(v, u, rec[u], C_SRC, l_hot)

                    def keys(i, u):
                        v.wait_ge(row_in[u], after_step(64, past + i, u))
                        v.scalar_tensor_tensor(out=row[u][:, :, 0:RBF], in0=rec[u][:, :, 0:RBF], scalar=0.1,
                                               in1=row[u][:, :, 0:RBF], op0=ALU.mult, op1=ALU.add).then_inc(l_key, 1)

                    def products(i, u):
                        v.wait_ge(l_key, base + i + 1)
                        v.wait_ge(l_own, base + i + 1)
                        v.tensor_tensor(prod[u % 2][:, :, :], row[u][:, :, 0:QW],
                                        p_own[:, 0:J * QW].rearrange("p (j c) -> p j c", j=J),
                                        ALU.mult).then_inc(l_prod, 1)

                    def scores(i, u):
                        v.wait_ge(l_prod, base + i + 1)
                        v.tensor_reduce(score[u][:, :], prod[u % 2][:, :, :], AX.X, ALU.add).then_inc(l_score, 1)

                    def group_max(i, u):
                        v.wait_ge(l_mT, base + i + 1)
                        v.tensor_reduce(gmax[u % 2][:, :], p_mT[u % 2][0:NP, :], AX.X, ALU.max).then_inc(l_gmax, 1)

                    def run_max(i, u):
                        v.wait_ge(l_gmax, base + i + 1)
                        v.scalar_tensor_tensor(out=smax[u][:, :], in0=smax[(u - 1) % U][:, :],
                                               scalar=fresh[0:NP, ds(i, 1)], in1=gmax[u % 2][:, :],
                                               op0=ALU.add, op1=ALU.max).then_inc(l_smax, 1)

                    def high(i, u):
                        v.wait_ge(l_smax, base + i + 1)
                        v.tensor_copy(parts[u % 2][:, 0:1], smax[u][:, :]).then_inc(l_hi, 1)

                    def decay(i, u):
                        v.scalar_tensor_tensor(out=arg[u][0:NP, J:J + 1], in0=smax[(u - 1) % U][:, :],
                                               scalar=fresh[0:NP, ds(i, 1)], in1=smax[u][:, :],
                                               op0=ALU.add, op1=ALU.subtract)

                    def middle(i, u):
                        v.wait_ge(l_hi, base + i + 1)
                        v.tensor_tensor(parts[u % 2][:, 1:2], smax[u][:, :], parts[u % 2][:, 0:1],
                                        ALU.subtract).then_inc(l_mid, 1)

                    def low(i, u):
                        v.wait_ge(l_mid, base + i + 1)
                        v.scalar_tensor_tensor(out=parts[u % 2][:, 2:3], in0=smax[u][:, :],
                                               scalar=parts[u % 2][:, 0:1], in1=parts[u % 2][:, 1:2],
                                               op0=ALU.subtract, op1=ALU.subtract).then_inc(l_parts, 1)

                    def maximum_sum(i, u):
                        v.wait_ge(l_mg, base + i + 1)
                        v.tensor_reduce(msum[u % 2][:, :], p_mg[:, 0:J * PARTS].rearrange("p (j k) -> p j k", j=J),
                                        AX.X, ALU.add).then_inc(l_msum, 1)

                    def shifted(i, u):
                        v.wait_ge(l_msum, base + i + 1)
                        v.tensor_tensor(arg[u][:, 0:J], score[u][:, :], msum[u % 2][:, :],
                                        ALU.subtract).then_inc(l_shift, 1)

                    def clipped(i, u):
                        v.wait_ge(l_shift, base + i + 1)
                        v.tensor_scalar(arg[u][:, 0:J], arg[u][:, 0:J], 20.0, None, ALU.min).then_inc(l_arg, 1)

                    def weigh(i, u):
                        v.wait_ge(l_es, base + i + 1)
                        v.tensor_tensor(vals[u % 2][:, :, :], row[u][:, :, H + 1:KW],
                                        bc(es[u][:, 0:J].unsqueeze(2), [P, J, VW]), ALU.mult).then_inc(l_vals, 1)

                    def sums(i, u):
                        v.wait_ge(l_agg, base + i + 1)
                        if at_least(i, U):
                            v.wait_ge(stored[u], before_step(16, past + U + i, u))
                        v.scalar_tensor_tensor(out=acc[u][:, :], in0=acc[(u - 1) % U][:, :],
                                               scalar=es[u][0:NP, J:J + 1], in1=p_agg[0:NP, 0:VW],
                                               op0=ALU.mult, op1=ALU.add).then_inc(l_acc, 1)

                    def step(i, u, now, one, two, three):
                        a, b, c = (u - 1) % U, (u - 2) % U, (u - 3) % U
                        if one:
                            group_max(i - 1, a)
                        if now:
                            keys(i, u)
                        if one:
                            run_max(i - 1, a)
                        if now:
                            products(i, u)
                        if one:
                            high(i - 1, a)
                            decay(i - 1, a)
                        if now:
                            scores(i, u)
                        if one:
                            middle(i - 1, a)
                        if now and before(i + 2, NG):
                            hots(i + 2, (u + 2) % U)
                        if one:
                            low(i - 1, a)
                        if three:
                            sums(i - 3, c)
                        if one:
                            maximum_sum(i - 1, a)
                        if two:
                            weigh(i - 2, b)
                        if one:
                            shifted(i - 1, a)
                            clipped(i - 1, a)
                    hots(0, 0)
                    hots(1, 1)
                    run_steps(v, lambda i, u: step(i, u, True, at_least(i, 1), at_least(i, 2), at_least(i, 3)), NG)
                    step(NG, NG % U, False, True, True, True)
                    step(NG + 1, (NG + 1) % U, False, False, True, True)
                    step(NG + 2, (NG + 2) % U, False, False, False, True)
                    v.wait_ge(stored[U - 1], before_step(16, past + U + NG, 0))
                    v.tensor_scalar(stat[:, 0, 0:NB], agg_in[:, :, H], 1.0e-10, None, ALU.add)
                    v.drain()
                    v.reciprocal(stat[:, 0, 0:NB], stat[:, 0, 0:NB])
                    v.drain()
                    for half, _ in HALVES:
                        v.tensor_tensor(HA[:, half, H:2 * H], agg_in[:, half, 0:H],
                                        bc(stat[:, 0, half].unsqueeze(2), [NP, HB, H]), ALU.mult).then_inc(a_agg, 1)
                    v.drain()
                    for q, (half, (_, c1)) in enumerate(HALVES):
                        v.wait_ge(y_s, l * 2 * NC_ + NC_ + c1)
                        thin = [NP, HB, H]
                        zz, t1 = big_a[:, half, 0:H], norm_tmp[:, :, 0:H]
                        v.scalar_tensor_tensor(out=t1, in0=zz, scalar=0.01, in1=zz, op0=ALU.mult, op1=ALU.max)
                        v.drain()
                        v.tensor_tensor(zz, t1, HA[:, half, 0:H], ALU.add)
                        v.drain()
                        layer_norm_in_place(v, zz, t1, thin, n_var, n_std, 4 * l + 4 + q, q * HB)
                        if q == 0:
                            v.wait_ge(w_end, l * 80 + 80)
                        v.tensor_tensor(zz, zz, bc(gains[:, 4 * H:5 * H].unsqueeze(1), thin), ALU.mult)
                        v.drain()
                        v.tensor_tensor(HA[:, half, 0:H], zz, bc(gains[:, 5 * H:6 * H].unsqueeze(1), thin), ALU.add)
                        v.drain().then_inc(n_h, 1)

            @block.scalar
            def _(act):
                with act.Fori(0, LAYERS) as l:
                    base = l * NG
                    past = base + NG
                    dense_act(act, l * 2 * NC_, HALVES[0][1], H, 2 * H, lambda c: big_a[:, c * CH:(c + 1) * CH, :],
                              (2, lambda: deviation(act, HB, n_var, n_std, 4 * l + 1, HB)))
                    dense_act(act, l * 2 * NC_, HALVES[1][1], H, 2 * H, lambda c: big_a[:, c * CH:(c + 1) * CH, :],
                              (NC_ - 2, lambda: deviation(act, NB, n_var, n_std, 4 * l + 2, 0)))
                    deviation(act, NB, n_var, n_std, 4 * l + 3, NB)
                    act.wait_ge(wmT_p, l + 1)
                    act.activation(wmT[:, :], p_x[0:H, 0:H], ACT.Copy).then_inc(wmT_s, 1)
                    act.wait_ge(wmu_p, l + 1)
                    act.activation(wmu[:, :], p_x[0:H, 128:128 + H], ACT.Copy).then_inc(wmu_s, 1)

                    def turned(i, u):
                        act.wait_ge(l_hot, base + i + 1)
                        if at_least(i, 2):
                            act.wait_ge(l_mask, J * (base + i - 1))
                        act.activation(neg_t[u % 2][:, :], oh[u % S][:, :, :].rearrange("p j n -> p (j n)"), ACT.Copy,
                                       scale=BIG, bias=-BIG).then_inc(l_neg, 1)
                        act.wait_ge(l_flip_p, base + i + 1)
                        if at_least(i, S):
                            act.wait_ge(l_mg, base + i - S + 1)
                        act.activation(ohT[u % S][:, :], p_ohT[u % 2], ACT.Copy).then_inc(l_flip, 1)

                    def full(i, u):
                        if at_least(i, S):
                            act.wait_ge(l_agg, base + i - S + 1)
                        act.activation(ohf[u % S][:, :, :], oh[u % S][:, :, :], ACT.Copy).then_inc(l_ohf, 1)

                    def mask(i, u):
                        s = u % 2
                        act.wait_ge(l_score, base + i + 1)
                        act.wait_ge(l_neg, base + i + 1)
                        if at_least(i, 2):
                            act.wait_ge(l_mT, base + i - 1)
                        for j in range(J):
                            act.activation(masked_t[s][:, j * P:(j + 1) * P], neg_t[s][:, j * P:(j + 1) * P],
                                           ACT.Identity, bias=score[u][:, j:j + 1]).then_inc(l_mask, 1)

                    def exps(i, u):
                        act.wait_ge(l_arg, base + i + 1)
                        act.activation(es[u][:, :], arg[u][:, :], ACT.Exp).then_inc(l_es, 1)

                    def body(i, u):
                        mask(i, u)
                        if before(i + 2, NG):
                            turned(i + 2, (u + 2) % U)
                        full(i, u)
                        if at_least(i, 1):
                            exps(i - 1, (u - 1) % U)
                    turned(0, 0)
                    turned(1, 1)
                    run_steps(act, body, NG)
                    exps(NG - 1, (NG - 1) % U)
                    for _, chunks in HALVES:
                        dense_act(act, l * 2 * NC_ + NC_, chunks, 2 * H, H, lambda c: big_a[:, c * CH:(c + 1) * CH, 0:H])
                    deviation(act, HB, n_var, n_std, 4 * l + 4, 0)
                deviation(act, HB, n_var, n_std, 4 * LAYERS + 1, HB)

            @block.tensor
            def _(pe):
                with pe.Fori(0, LAYERS) as l:
                    base = l * NG
                    past = base + NG
                    pe.wait_ge(w_in, l * 96 + 96)
                    for q, (_, chunks) in enumerate(HALVES):
                        pe.wait_ge(n_h, 2 * l + q + 1)
                        pe.sem_inc(held, 1)
                        dense_pe(pe, l * 2 * NC_, chunks, lambda b: HA[:, b, 0:H], H, wqk[:, :], 2 * H)
                    pe.wait_ge(w_end, l * 80 + 80)
                    pe.sem_inc(held, 1)
                    pe.transpose(p_x[0:H, 0:H], wm[:, :], ident[0:H, 0:H]).then_inc(wmT_p, 1)
                    pe.wait_ge(wmT_s, l + 1)
                    pe.sem_inc(held, 1)
                    pe.matmul(p_x[0:H, 128:128 + H], wmT[:, :], wub[:, :], start=True, stop=True).then_inc(wmu_p, 1)

                    def front(i, u):
                        pe.wait_ge(l_hot, base + i + 1)
                        if at_least(i, 2):
                            pe.wait_ge(l_flip, base + i - 1)
                        flip_one_hot(pe, u, l_flip_p)

                    def queries(i, u):
                        pe.wait_ge(rec_in[u], after_step(32, past + i, u))
                        pe.wait_ge(l_flip, base + i + 1)
                        if at_least(i, 1):
                            pe.wait_ge(l_prod, base + i)
                        gather_own(pe, u, p_own, QW, l_own)

                    def flip_masked(i, u):
                        if at_least(i, 2):
                            pe.wait_ge(l_gmax, base + i - 1)
                        for j in range(J):
                            pe.wait_ge(l_mask, J * (base + i) + j + 1)
                            mm = pe.transpose(p_mT[u % 2][:, j * P:(j + 1) * P], masked_t[u % 2][:, j * P:(j + 1) * P],
                                              ident[:, :])
                        mm.then_inc(l_mT, 1)

                    def gather_max(i, u):
                        pe.wait_ge(l_parts, base + i + 1)
                        if at_least(i, 1):
                            pe.wait_ge(l_msum, base + i)
                        for j in range(J):
                            mm = pe.matmul(p_mg[:, j * PARTS:(j + 1) * PARTS], ohT[u % S][0:NP, j * P:(j + 1) * P],
                                           parts[u % 2][:, :], start=True, stop=True)
                        mm.then_inc(l_mg, 1)

                    def sums(i, u):
                        pe.wait_ge(l_vals, base + i + 1)
                        pe.wait_ge(l_ohf, base + i + 1)
                        if at_least(i, 1):
                            pe.wait_ge(l_acc, base + i)
                        sum_group(pe, u, vals[u % 2], l_agg)

                    def body(i, u):
                        if at_least(i, 1):
                            gather_max(i - 1, (u - 1) % U)
                        flip_masked(i, u)
                        if before(i + 1, NG):
                            queries(i + 1, (u + 1) % U)
                        if before(i + 2, NG):
                            front(i + 2, (u + 2) % U)
                        if at_least(i, 2):
                            sums(i - 2, (u - 2) % U)
                    pe.wait_ge(y_s, l * 2 * NC_ + NC_)
                    front(0, 0)
                    front(1, 1)
                    queries(0, 0)
                    run_steps(pe, body, NG)
                    gather_max(NG - 1, (NG - 1) % U)
                    for i in (NG - 2, NG - 1):
                        sums(i, i % U)
                    pe.wait_ge(wmu_in, l * 16 + 16)
                    for q, (_, chunks) in enumerate(HALVES):
                        pe.wait_ge(a_agg, 2 * l + q + 1)
                        pe.sem_inc(held, 1)
                        dense_pe(pe, l * 2 * NC_ + NC_, chunks, lambda b: HA[:, b, :], 2 * H, wu[:, :], H)
                    pe.wait_ge(y_s, l * 2 * NC_ + 2 * NC_)

        c_h = sem("c_h")
        c_w = sem("c_w")
        c_var = sem("c_var")
        c_std = sem("c_std")
        c_tab = sem("c_tab")
        c_out = sem("c_out")
        DN = 2 * NC_ * LAYERS
        with nc.Block() as block:
            @block.vector
            def _(v):
                v.tensor_tensor(X[:, :, :], X[:, :, :], HA[:, :, 0:H], ALU.add)
                v.drain()
                layer_norm(v, big_a[:, :, 0:H], X[:, :, :], [NP, NB, H], c_var, c_std, 1, tmp=big_b[:, :, 0:H])
                v.tensor_scalar(HA[:, :, 0:H], big_a[:, :, 0:H], 0.0, None, ALU.max).then_inc(c_h, 1)
                v.wait_ge(y_s, DN + NC_)
                v.tensor_tensor(HA[:, :, H:2 * H], big_a[:, :, 0:H], bc(dinv[:, :].unsqueeze(2), [NP, NB, H]), ALU.mult)
                v.drain()
                split3(v, HA[:, :, H:2 * H], own3(H), big_a[:, :, 0:H])
                v.drain().then_inc(c_tab, 1)

            @block.scalar
            def _(act):
                deviation(act, NB, c_var, c_std, 1)
                dense_act(act, DN, (0, NC_), H, H, lambda c: big_a[:, c * CH:(c + 1) * CH, 0:H])

            @block.tensor
            def _(pe):
                pe.wait_ge(c_w, 16)
                pe.wait_ge(c_h, 1)
                dense_pe(pe, DN, (0, NC_), lambda b: HA[:, b, 0:H], H, wm[:, :], H)

            @block.sync
            def _(sp):
                sp.dma_start(wm[:, :], W1).then_inc(c_w, 16)
                fill_last(sp, 1, 0, NB)
                sp.wait_ge(filled_last, 2 * NB * 16)
                sp.wait_ge(c_tab, 1)
                sp.dma_start(own_d[:, :, 0:PARTS * H].rearrange("b p c -> p b c"),
                             own3(H).rearrange("p b k c -> p b (k c)")).then_inc(c_out, 16)
                sp.wait_ge(c_out, 16)

        m_hot = sem("m_hot")
        m_flip_p = sem("m_flip_p")
        m_flip = sem("m_flip")
        m_own = sem("m_own")
        m_msg = sem("m_msg")
        mrow = [row[u][:, :, :].rearrange("p j c -> p (j c)").bitcast(BF16)[:, 0:J * MW]
                .rearrange("p (j c) -> p j c", j=J) for u in range(U)]
        msg_bank = [[p_own, p_x], [p_mT[0], p_mT[1]]]

        def msg_cols(u, j):
            return msg_bank[u % 2][j // 2][:, (j % 2) * PARTS * H:(j % 2 + 1) * PARTS * H]

        with nc.Block() as block:
            @block.sync
            def _(sp):
                def body(i, u):
                    if at_least(i, U):
                        sp.wait_ge(sent[u], before_step(64, STEPS + i, u))
                        sp.sem_inc(held, 1)
                    load_group(sp, i, u, 0, rec_t[u][:, 0:J * RW],
                               lean_d[ds(i, 1), :, :].rearrange("a p c -> p (a c)"), own_d, PARTS * H, rec_in, m_own)
                run_steps(sp, body, NG)

            @block.vector
            def _(v):
                def hots(i, u):
                    v.wait_ge(rec_in[u], after_step(32, PAST + i, u))
                    one_hot(v, u, rec[u], C_SRC, m_hot)

                def body(i, u):
                    if before(i + 1, NG):
                        hots(i + 1, (u + 1) % U)
                    if at_least(i, U):
                        v.wait_ge(sent[u], before_step(64, STEPS + i, u))
                    v.tensor_copy(mrow[u][:, :, PARTS * H:MW], bc(rec[u][:, :, C_DROW:C_DROW + 1], [P, J, 2]))
                    v.wait_ge(m_own, i + 1)
                    for q in range(2):
                        ins = v.tensor_copy(mrow[u][:, 2 * q:2 * q + 2, 0:PARTS * H],
                                            msg_bank[u % 2][q][:, 0:2 * PARTS * H].rearrange("p (j c) -> p j c", j=2))
                    ins.then_inc(m_msg, 1)
                hots(0, 0)
                run_steps(v, body, NG)

            @block.scalar
            def _(act):
                def body(i, u):
                    act.wait_ge(m_flip_p, i + 1)
                    if at_least(i, S):
                        act.wait_ge(m_own, i - S + 1)
                    act.activation(ohT[u % S][:, :], p_ohT[u % 2], ACT.Copy).then_inc(m_flip, 1)
                run_steps(act, body, NG)

            @block.tensor
            def _(pe):
                def front(i, u):
                    pe.wait_ge(m_hot, i + 1)
                    if at_least(i, 2):
                        pe.wait_ge(m_flip, i - 1)
                    flip_one_hot(pe, u, m_flip_p)

                def body(i, u):
                    if before(i + 1, NG):
                        front(i + 1, (u + 1) % U)
                    pe.wait_ge(m_flip, i + 1)
                    if at_least(i, 2):
                        pe.wait_ge(m_msg, i - 1)
                    for j in range(J):
                        mm = pe.matmul(msg_cols(u, j), ohT[u % S][0:NP, j * P:(j + 1) * P], own[u][:, 0:PARTS * H],
                                       start=True, stop=True)
                    mm.then_inc(m_own, 1)
                front(0, 0)
                run_steps(pe, body, NG)

            @block.gpsimd
            def _(pool):
                def body(i, u):
                    pool.wait_ge(m_msg, i + 1)
                    pool.sem_inc(held, 1)
                    for j in range(J):
                        pool.indirect_dma_start(
                            out=msg_d[:, :], out_offset=bass.IndirectOffsetOnAxis(
                                ap=rec[u][:, j, C_POS2:RW].bitcast(I32), axis=0),
                            in_=mrow[u][:, j, :], in_offset=None, bounds_check=NG * EG - 1,
                            oob_is_err=False).then_inc(sent[u], 16)
                run_steps(pool, body, NG)
                for u in range(U):
                    pool.wait_ge(sent[u], before_step(64, STEPS + NG, 0))

        d_idx = sem("d_idx")
        d_hot = sem("d_hot")
        d_hot_last = sem("d_hot_last")
        d_agg = sem("d_agg")
        d_acc = sem("d_acc")
        d_sums = sem("d_sums")
        d_res = sem("d_res")
        d_out = sem("d_out")
        with nc.Block() as block:
            @block.sync
            def _(sp):
                def body(i, u):
                    if at_least(i, U):
                        sp.wait_ge(d_agg, i - U + 1)
                    sp.dma_start(mrow[u].rearrange("p j c -> p (j c)"),
                                 msg_g[ds(i, 1), :, :].rearrange("a p c -> p (a c)")).then_inc(slot_in[u], 16)
                run_steps(sp, body, NG)
                sums_of_blocks(sp, 1, 0, NB // 2, PAST + U, d_sums, stored, NG)
                sp.wait_ge(d_res, 1)
                sp.dma_start(out.rearrange("(p b) c -> p b c", b=NB), X[:, :, :]).then_inc(d_out, 16)
                sp.wait_ge(d_out, 16)

            @block.vector
            def _(v):
                def hots(i, u):
                    v.wait_ge(d_idx, i + 1)
                    if at_least(i, S):
                        v.wait_ge(d_agg, i - S + 1)
                    one_hot(v, u, score[u][:, :].unsqueeze(2), 0, d_hot, range(J - 1))

                def body(i, u):
                    if before(i + 1, NG):
                        hots(i + 1, (u + 1) % U)
                    if at_least(i, 1):
                        v.wait_ge(d_acc, i)
                    v.wait_ge(d_agg, i + 1)
                    if at_least(i, U):
                        v.wait_ge(stored[u], before_step(16, PAST + U + i, u))
                    v.scalar_tensor_tensor(out=acc[u][:, 0:H], in0=acc[(u - 1) % U][:, 0:H],
                                           scalar=keep[1][0:NP, ds(i, 1)], in1=agg_bank[u % 2][0:NP, 0:H],
                                           op0=ALU.mult, op1=ALU.add).then_inc(d_acc, 1)
                hots(0, 0)
                run_steps(v, body, NG)
                v.wait_ge(d_sums, 16 * NB)
                v.tensor_tensor(big_a[:, :, 0:H], agg_in[:, :, 0:H], HA[:, :, H:2 * H], ALU.add)
                v.drain()
                v.tensor_tensor(big_a[:, :, 0:H], big_a[:, :, 0:H], bc(dinv[:, :].unsqueeze(2), [NP, NB, H]), ALU.mult)
                v.drain()
                v.tensor_tensor(X[:, :, :], X[:, :, :], big_a[:, :, 0:H], ALU.add)
                v.drain()
                v.tensor_tensor(X[:, :, :], X[:, :, :], bc(gains_n[:, 2 * H:3 * H].unsqueeze(1), [NP, NB, H]), ALU.add)
                v.drain().then_inc(d_res, 1)

            @block.gpsimd
            def _(pool):
                def body(i, u):
                    pool.wait_ge(d_idx, i + 1)
                    if at_least(i, S):
                        pool.wait_ge(d_agg, i - S + 1)
                    pool.sem_inc(held, 1)
                    one_hot(pool, u, score[u][:, :].unsqueeze(2), 0, d_hot_last, [J - 1])
                run_steps(pool, body, NG)

            @block.scalar
            def _(act):
                def local(i, u):
                    act.wait_ge(slot_in[u], after_step(16, STEPS + i, u))
                    if at_least(i, U):
                        act.wait_ge(d_hot, i - U + 1)
                        act.wait_ge(d_hot_last, i - U + 1)
                    act.activation(score[u][:, :].unsqueeze(2), mrow[u][:, :, PARTS * H:PARTS * H + 1],
                                   ACT.Copy).then_inc(d_idx, 1)

                def body(i, u):
                    if before(i + 2, NG):
                        local(i + 2, (u + 2) % U)
                    act.wait_ge(d_acc, i + 1)
                    act.dma_start(acc_d[ds(i, 1), :, :].rearrange("a p c -> p (a c)"), acc[u][:, :]).then_inc(stored[u], 16)
                local(0, 0)
                local(1, 1)
                run_steps(act, body, NG)
                sums_of_blocks(act, 1, NB // 2, NB, PAST + U, d_sums, stored, NG)

            @block.tensor
            def _(pe):
                def body(i, u):
                    pe.wait_ge(d_hot, i + 1)
                    pe.wait_ge(d_hot_last, i + 1)
                    if at_least(i, 2):
                        pe.wait_ge(d_acc, i - 1)
                    for j in range(J):
                        for k in range(PARTS):
                            mm = pe.matmul(agg_bank[u % 2][:, 0:H], oh[u % S][:, j, :],
                                           mrow[u][:, j, k * H:(k + 1) * H], start=(j == 0 and k == 0),
                                           stop=(j == J - 1 and k == PARTS - 1))
                    mm.then_inc(d_agg, 1)
                run_steps(pe, body, NG)


_INS = ["x", "src", "dst", "edge_attr_40", "edge_weight", "node_type_119", "node_vec",
        "L0_gnn_Wq", "L0_gnn_gq", "L0_gnn_bq", "L0_gnn_Wk", "L0_gnn_gk", "L0_gnn_bk", "L0_gnn_Wm", "L0_gnn_Wu",
        "L0_gnn_go", "L0_gnn_bo", "L0_gnn_F1W", "L0_gnn_F1b", "L0_gnn_F2W", "L0_gnn_F2b", "L0_gnn_gn",
        "L0_gnn_bn", "L0_gnn_emb", "L0_gnn_adapt", "L1_gnn_W", "L1_gnn_b"]


def kernel(**inputs):
    import numpy as _np
    import concourse.bacc as _bacc
    from concourse import mybir as _mybir
    from concourse.bass_utils import run_bass_kernel_spmd as _run

    nc = _bacc.Bacc("TRN2", target_bir_lowering=False, num_devices=1)
    arrays, args = {}, []
    for name in _INS:
        a = _np.ascontiguousarray(inputs[name])
        arrays[f"in_{name}"] = a
        args.append(nc.dram_tensor(f"in_{name}", a.shape, _mybir.dt.from_np(a.dtype), kind="ExternalInput").ap())
    args.append(nc.dram_tensor("out_0", (N, H), F32, kind="ExternalOutput").ap())
    build(nc, *args)
    r = _run(nc, [arrays], core_ids=[0])
    return r.results[0]["out_0"]
```
